# Optimizing a Trainium2 kernel written in Bass

```python
import numpy as np
import jax
import jax.numpy as jnp

def _softmax(x, axis=-1):
    return jax.nn.softmax(x, axis=axis)

def _gelu(x):
    return jax.nn.gelu(x, approximate=True)

def _silu(x):
    return jax.nn.silu(x)

def _sigmoid(x):
    return jax.nn.sigmoid(x)

def _layernorm(x, axis=-1, eps=1e-05):
    m = jnp.mean(x, axis=axis, keepdims=True)
    v = jnp.var(x, axis=axis, keepdims=True)
    return (x - m) / jnp.sqrt(v + eps)

def _scatter_add(tgt, idx, src, axis=0):
    return tgt.at[idx].add(src)

def _segment_sum(src, seg, n):
    return jax.ops.segment_sum(src, seg, n)
kernel_name = 'mk_gnn_resnorm_d4_gnn_r64_bd1290'

def setup_inputs(seed: int=0):
    np.random.seed(seed)
    _w = jnp.asarray

    def _rec_inputs():
        import jax
        import jax.numpy as jnp
        _gk = jax.random.key(seed)
        x = -0.000202 + 1 * jax.random.normal(jax.random.fold_in(_gk, 1), (100000, 128), jnp.float32)
        src = jax.random.randint(jax.random.fold_in(_gk, 2), (25000,), 0, 100000, jnp.int32)
        dst = jnp.minimum((100000 * jax.random.uniform(jax.random.fold_in(_gk, 3), (25000,)) ** 2.0).astype(jnp.int32), 99999)
        _o = jnp.argsort(dst, stable=True)
        src = src[_o]
        dst = dst[_o]
        edge_attr_64 = 0.000189758 + 1.00013 * jax.random.normal(jax.random.fold_in(_gk, 12), (25000, 64), jnp.float32)
        return (x, src, dst, edge_attr_64)
    x, src, dst, edge_attr_64 = _rec_inputs()

    def _L0_gnn_setup():
        import jax, jax.numpy as jnp
        import numpy as np
        N, E = (50000, 12500)
        D, DE = (128, 64)
        BN_EPS = 1e-05

        def _bn(h, gamma, beta):
            mu = jnp.mean(h, axis=0)
            var = jnp.var(h, axis=0)
            return (h - mu) * jax.lax.rsqrt(var + BN_EPS) * gamma + beta
        key = jax.random.key(seed)
        ks = jax.random.split(key, 12)
        s = lambda d: 1.0 / np.sqrt(d)
        return {'x': jax.random.normal(ks[0], (N, D), jnp.float32), 'edge_index': jax.random.randint(ks[1], (2, E), 0, N, jnp.int64), 'edge_attr_processed': jax.random.normal(ks[2], (E, DE), jnp.float32), 'We': jax.random.uniform(ks[3], (D, DE), jnp.float32, -s(DE), s(DE)), 'be': jnp.zeros((D,), jnp.float32), 'W1': jax.random.uniform(ks[4], (2 * D, D), jnp.float32, -s(D), s(D)), 'b1': jnp.zeros((2 * D,), jnp.float32), 'g1': jnp.ones((2 * D,), jnp.float32), 'beta1': jnp.zeros((2 * D,), jnp.float32), 'W2': jax.random.uniform(ks[5], (D, 2 * D), jnp.float32, -s(2 * D), s(2 * D)), 'b2': jnp.zeros((D,), jnp.float32), 'g2': jnp.ones((D,), jnp.float32), 'beta2': jnp.zeros((D,), jnp.float32), 'eps': jnp.zeros((), jnp.float32)}
    _L0_gnn_all = _L0_gnn_setup()
    _L0_gnn_in = {k: v for k, v in _L0_gnn_all.items() if k in ('We', 'be', 'W1', 'b1', 'g1', 'beta1', 'W2', 'b2', 'g2', 'beta2', 'eps')}
    del _L0_gnn_all

    def _L1_gnn_setup():
        import jax, jax.numpy as jnp
        import numpy as np
        N = 50000
        E = 12500
        C_IN = 128
        C_OUT = 128
        key = jax.random.key(seed)
        k1, k2, k3 = jax.random.split(key, 3)
        x = jax.random.normal(k1, (N, C_IN), dtype=jnp.float32)
        edge_index = jax.random.randint(k2, (2, E), 0, N, dtype=jnp.int32)
        W = jax.random.normal(k3, (C_OUT, C_IN), dtype=jnp.float32) / np.sqrt(C_IN).astype(np.float32)
        return {'x': x, 'edge_index': edge_index, 'W': W}
    _L1_gnn_all = _L1_gnn_setup()
    _L1_gnn_in = {k: v for k, v in _L1_gnn_all.items() if k in ('W',)}
    del _L1_gnn_all

    def _L2_gnn_setup():
        import jax, jax.numpy as jnp
        import numpy as np
        N_NODES = 100000
        N_EDGES = 9375
        EMB_DIM = 128
        HID_DIM = 128
        key = jax.random.key(seed)
        k1, k2, k3, k4 = jax.random.split(key, 4)
        x = jax.random.normal(k1, (N_NODES, EMB_DIM), dtype=jnp.float32)
        src = jax.random.randint(k2, (N_EDGES,), 0, N_NODES)
        dst = jax.random.randint(k3, (N_EDGES,), 0, N_NODES)
        W = jax.random.normal(k4, (HID_DIM, EMB_DIM), dtype=jnp.float32) / np.sqrt(EMB_DIM).astype(np.float32)
        b = jnp.zeros((HID_DIM,), dtype=jnp.float32)
        return {'x': x, 'W': W, 'b': b, 'src': src, 'dst': dst}
    _L2_gnn_all = _L2_gnn_setup()
    _L2_gnn_in = {k: v for k, v in _L2_gnn_all.items() if k in ('W', 'b')}
    del _L2_gnn_all

    def _L3_gnn_setup():
        import jax, jax.numpy as jnp
        import numpy as np
        N_NODES = 50000
        N_EDGES = 12500
        IN_FEATS = 128
        OUT_FEATS = 32
        NUM_HEADS = 4
        key = jax.random.key(seed)
        k1, k2, k3, k4 = jax.random.split(key, 4)
        feat = jax.random.normal(k1, (N_NODES, IN_FEATS), dtype=jnp.float32)
        W = jax.random.normal(k2, (NUM_HEADS * OUT_FEATS, IN_FEATS), dtype=jnp.float32) * 0.02
        src = jax.random.randint(k3, (N_EDGES,), 0, N_NODES)
        dst = jax.random.randint(k4, (N_EDGES,), 0, N_NODES)
        return {'feat': feat, 'W': W, 'src': src, 'dst': dst}
    _L3_gnn_all = _L3_gnn_setup()
    _L3_gnn_in = {k: v for k, v in _L3_gnn_all.items() if k in ('W',)}
    del _L3_gnn_all
    return {'x': x, 'src': src, 'dst': dst, 'edge_attr_64': edge_attr_64, 'L0_gnn_We': _L0_gnn_in['We'], 'L0_gnn_be': _L0_gnn_in['be'], 'L0_gnn_W1': _L0_gnn_in['W1'], 'L0_gnn_b1': _L0_gnn_in['b1'], 'L0_gnn_g1': _L0_gnn_in['g1'], 'L0_gnn_beta1': _L0_gnn_in['beta1'], 'L0_gnn_W2': _L0_gnn_in['W2'], 'L0_gnn_b2': _L0_gnn_in['b2'], 'L0_gnn_g2': _L0_gnn_in['g2'], 'L0_gnn_beta2': _L0_gnn_in['beta2'], 'L0_gnn_eps': _L0_gnn_in['eps'], 'L1_gnn_W': _L1_gnn_in['W'], 'L2_gnn_W': _L2_gnn_in['W'], 'L2_gnn_b': _L2_gnn_in['b'], 'L3_gnn_W': _L3_gnn_in['W']}

def reference(x, src, dst, edge_attr_64, L0_gnn_We, L0_gnn_be, L0_gnn_W1, L0_gnn_b1, L0_gnn_g1, L0_gnn_beta1, L0_gnn_W2, L0_gnn_b2, L0_gnn_g2, L0_gnn_beta2, L0_gnn_eps, L1_gnn_W, L2_gnn_W, L2_gnn_b, L3_gnn_W):
    import jax
    import jax.numpy as jnp

    def _L0_gnn_ref(x, edge_index, edge_attr_processed, We, be, W1, b1, g1, beta1, W2, b2, g2, beta2, eps):
        import jax, jax.numpy as jnp
        import numpy as np
        N, E = (50000, 12500)
        D, DE = (128, 64)
        BN_EPS = 1e-05

        def _bn(h, gamma, beta):
            mu = jnp.mean(h, axis=0)
            var = jnp.var(h, axis=0)
            return (h - mu) * jax.lax.rsqrt(var + BN_EPS) * gamma + beta
        src, dst = (edge_index[0], edge_index[1])
        msg = jax.nn.relu(x[src] + edge_attr_processed @ We.T + be)
        agg = jax.ops.segment_sum(msg, dst, num_segments=x.shape[0])
        h = (1.0 + eps) * x + agg
        h = jax.nn.relu(_bn(h @ W1.T + b1, g1, beta1)) @ W2.T + b2
        return jax.nn.relu(_bn(h, g2, beta2))

    def _L1_gnn_ref(x, edge_index, W):
        import jax, jax.numpy as jnp
        import numpy as np
        N = 50000
        E = 12500
        C_IN = 128
        C_OUT = 128
        n = x.shape[0]
        row, col = (edge_index[0], edge_index[1])
        deg = jax.ops.segment_sum(jnp.ones((row.shape[0],), x.dtype), row, num_segments=n)
        norm = jax.lax.rsqrt(deg + 1.0)
        x1 = x * norm[:, None]
        agg = jax.ops.segment_sum(x1[col], row, num_segments=n) + x1
        out = norm[:, None] * agg @ W.T
        return out

    def _L2_gnn_ref(x, W, b, src, dst):
        import jax, jax.numpy as jnp
        import numpy as np
        N_NODES = 100000
        N_EDGES = 9375
        EMB_DIM = 128
        HID_DIM = 128
        agg = jax.ops.segment_sum(x[src], dst, num_segments=x.shape[0])
        out = agg @ W.T + b
        return out

    def _L3_gnn_ref(feat, W, src, dst):
        import jax, jax.numpy as jnp
        import numpy as np
        N_NODES = 50000
        N_EDGES = 12500
        IN_FEATS = 128
        OUT_FEATS = 32
        NUM_HEADS = 4
        N = feat.shape[0]
        H, D = (NUM_HEADS, OUT_FEATS)
        ft = (feat @ W.T).reshape(N, H, D)
        ft_src = ft[src]
        ft_dst = ft[dst]
        a = jnp.einsum('ehd,ehd->eh', ft_src, ft_dst) / jnp.sqrt(jnp.float32(D))
        m = jax.ops.segment_max(a, dst, num_segments=N)
        e = jnp.exp(a - m[dst])
        denom = jax.ops.segment_sum(e, dst, num_segments=N)
        sa = e / denom[dst]
        rst = jax.ops.segment_sum(ft_src * sa[:, :, None], dst, num_segments=N)
        rst = rst + feat.reshape(N, -1, D)
        return rst.reshape(N, H * D)
    edge_index = jnp.stack([src, dst])
    x = _layernorm(x + _L0_gnn_ref(x, edge_index, edge_attr_64, L0_gnn_We, L0_gnn_be, L0_gnn_W1, L0_gnn_b1, L0_gnn_g1, L0_gnn_beta1, L0_gnn_W2, L0_gnn_b2, L0_gnn_g2, L0_gnn_beta2, L0_gnn_eps), axis=-1)
    x = _layernorm(x + _L1_gnn_ref(x, edge_index, L1_gnn_W), axis=-1)
    x = _layernorm(x + _L2_gnn_ref(x, L2_gnn_W, L2_gnn_b, src, dst), axis=-1)
    x = _layernorm(x + _L3_gnn_ref(x, L3_gnn_W, src, dst), axis=-1)
    return x

_drawn_inputs = setup_inputs


def setup_inputs(seed=0):
    import zlib

    import numpy as np

    out = dict(_drawn_inputs(seed))
    spreads = {'L0_gnn_be': (0.0, 0.375),
     'L0_gnn_b1': (0.0, 0.8),
     'L0_gnn_g1': (1.0, 0.2),
     'L0_gnn_beta1': (0.0, 0.1),
     'L0_gnn_b2': (0.0, 0.8),
     'L0_gnn_g2': (1.0, 0.2),
     'L0_gnn_beta2': (0.0, 0.1),
     'L2_gnn_b': (0.0, 0.1)}
    factors = {}
    for name, (base, spread) in spreads.items():
        noise = np.random.default_rng([zlib.crc32(name.encode()), seed]).standard_normal(out[name].shape)
        drawn = base * np.exp(spread * noise) if base else spread * noise
        out[name] = jnp.asarray(drawn.astype(out[name].dtype))
    for name, factor in factors.items():
        out[name] = (out[name] * factor).astype(out[name].dtype)
    return out
```

```python
import concourse.bass as bass
from concourse import mybir
from contextlib import ExitStack

FP32 = mybir.dt.float32
BF16 = mybir.dt.bfloat16
I32 = mybir.dt.int32
ALU = mybir.AluOpType
ACT = mybir.ActivationFunctionType
AXX = mybir.AxisListType.X

P = 128
D = 128
J = 8
CHUNK = P * J
W = J * D
HALF = W // 2
GROUP = 2 * P
HEADS = 4
HD = D // HEADS
STATE = D + 2 * HEADS
EPS = 1e-5
LOWEST = -3.0e38


def wait(eng, sem, value):
    if isinstance(value, int) and value <= 0:
        return
    eng.wait_ge(sem, value)


class Chain:

    def __init__(self, eng, sem):
        self.eng, self.sem, self.base, self.k = eng, sem, 0, 0

    def mark(self, ins):
        self.k += 1
        return ins.then_inc(self.sem, 1)

    def sync(self):
        self.eng.wait_ge(self.sem, self.base + self.k)

    def enter(self, i, start, per):
        self.fixed = self.base + self.k
        self.base, self.k, self.start, self.per = i * per + (self.fixed - start * per), 0, start, per

    def leave(self, count):
        assert self.k == self.per, f"this loop's body marks {self.k}"
        self.base, self.k = self.fixed + count * self.per, 0


def loop_pairs(eng, pairs, body, chain=None, per=0):
    body(0)
    with eng.Fori(1, pairs - 1) as i:
        if chain:
            chain.enter(i, 1, per)
        body(i)
    if chain:
        chain.leave(pairs - 2)
    body(pairs - 1)


def gnn_kernel(nc, x, src, dst, edge_attr, We, be, W1, b1, g1, beta1, W2, b2, g2, beta2, eps,
               WL1, WL2, bL2, WL3, out):
    N = x.shape[0]
    E = src.shape[0]
    DE = edge_attr.shape[1]
    CHUNKS = -(-N // CHUNK)
    TAIL_P = (N - (CHUNKS - 1) * CHUNK) // J
    PAIRS = CHUNKS // 2
    NPAD = CHUNKS * CHUNK
    EDGE_COLS = -(-E // (4 * P)) * 4
    FULL_P = E // EDGE_COLS
    REM = E - FULL_P * EDGE_COLS
    GROUPS = EDGE_COLS // 2
    EPAIRS = GROUPS // 2
    NCOLS = CHUNKS * J
    assert CHUNKS % 2 == 0 and (N - (CHUNKS - 1) * CHUNK) % J == 0 and N + GROUP < NPAD
    assert PAIRS > 2 and EPAIRS > 2

    ctx = ExitStack()

    def sb(name, shape, dt=FP32):
        return ctx.enter_context(nc.sbuf_tensor(name, shape, dt))

    def dram(name, cols):
        return nc.dram_tensor(name, (NPAD, cols), FP32, kind="Internal").ap()

    agg0, agg1, agg2 = dram("agg0", D), dram("agg1", D), dram("agg2", D)
    z2_t = nc.dram_tensor("z2_t", (CHUNKS, P, W), FP32, kind="Internal").ap()
    x1n_t, x2_t, x3_t = dram("x1n", D), dram("x2", D), dram("x3", D)
    state_t = dram("state", STATE)

    def chunked(table, rows=P):
        return table.rearrange("(m p j) f -> m p (j f)", p=P, j=J)

    def at(view, m, rows=P):
        if isinstance(m, int):
            return view[m, 0:rows, :]
        return view[bass.ds(m, 1), 0:rows, :].rearrange("a p f -> (a p) f")

    def node_rows(table, m, rows=P):
        if isinstance(m, int):
            v = table[m * CHUNK:m * CHUNK + rows * J, :]
            return v.rearrange("(p j) f -> p (j f)", j=J)
        body = table[0:(CHUNKS - 1) * CHUNK, :].rearrange("(m p j) f -> m p (j f)", p=P, j=J)
        return body[bass.ds(m, 1), :, :].rearrange("a p f -> (a p) f")

    def rows_of(m):
        return TAIL_P if isinstance(m, int) and m == CHUNKS - 1 else P

    with ctx:
        ident = sb("ident", [P, P])
        ones_col = sb("ones_col", [P, 1])
        eps_col = sb("eps_col", [P, 1])
        gin_scale = sb("gin_scale", [P, 1])
        WeT = sb("WeT", [DE + 1, D])
        W1T = sb("W1T", [P, 2 * D])
        W2T = sb("W2T", [P, 2, D])
        WLT = [sb(f"WLT{n}", [P, D]) for n in range(3)]
        b1c, g1c, beta1c = (sb(n, [P, 2]) for n in ("b1c", "g1c", "beta1c"))
        b2c, g2c, beta2c = (sb(n, [P, 1]) for n in ("b2c", "g2c", "beta2c"))
        bL2_all = sb("bL2_all", [P, D])
        keys = sb("keys", [P, 2 * EDGE_COLS])
        index = sb("index", [P, GROUPS, 4, 2], I32)
        lo_digit = sb("lo_digit", [P, EDGE_COLS])
        hi_digit = sb("hi_digit", [P, EDGE_COLS])
        deg1 = sb("deg1", [P, NCOLS])
        norm = sb("norm", [P, NCOLS])
        norm2 = sb("norm2", [P, NCOLS])
        a1, t1 = sb("a1", [P, 2]), sb("t1", [P, 2])
        a2, t2 = sb("a2", [P, 1]), sb("t2", [P, 1])
        moments = sb("moments", [P, D + 1])

        prepare(nc, locals())
        degrees_and_first_sum(nc, locals())
        first_norm(nc, locals())
        mlp(nc, locals())
        first_layer_out(nc, locals())
        aggregate(nc, locals(), "l1", x1n_t, agg1, EDGE_COLS, 1, 0)
        convolve(nc, locals(), "l1", x1n_t, agg1, x2_t, WLT[0])
        aggregate(nc, locals(), "l2", x2_t, agg2, 0, 2, 3)
        convolve(nc, locals(), "l2", x2_t, agg2, x3_t, WLT[1])
        attention(nc, locals())
        last_layer_out(nc, locals())


class Turns:

    def __init__(self, eng, name):
        self.eng = eng
        self.count = eng.alloc_register(name)
        eng.reg_mov(self.count, 1)

    def wait(self, sem, t):
        self.eng.wait_ge(sem, t + 1 if isinstance(t, int) else self.count)
        self.eng.reg_add(self.count, self.count, 1)


class Scope:

    def __init__(self, nc, tag):
        self.nc, self.tag, self.ctx, self.sems = nc, tag, ExitStack(), []

    def __enter__(self):
        self.ctx.__enter__()
        return self

    def __exit__(self, *e):
        self.ctx.__exit__(*e)
        self.nc.clear_and_free_semaphores(self.sems)
        self.nc.all_engine_barrier()

    def sb(self, name, shape, dt=FP32):
        return self.ctx.enter_context(self.nc.sbuf_tensor(f"{self.tag}_{name}", shape, dt))

    def ps(self, name, shape, dt=FP32):
        return self.ctx.enter_context(self.nc.psum_tensor(f"{self.tag}_{name}", shape, dt))

    def sem(self, name):
        self.sems.append(self.nc.alloc_semaphore(f"{self.tag}_{name}"))
        return self.sems[-1]

    def block(self):
        return self.ctx.enter_context(self.nc.Block())


def prepare(nc, g):
    N, E, DE = g["N"], g["E"], g["DE"]
    EC, GROUPS, FULL_P, REM, CHUNKS = g["EDGE_COLS"], g["GROUPS"], g["FULL_P"], g["REM"], g["CHUNKS"]
    keys, index, ident = g["keys"], g["index"], g["ident"]
    with Scope(nc, "prep") as sc:
        w1 = sc.sb("w1", [P, 2, D])
        w2 = sc.sb("w2", [P, 2, D])
        we = sc.sb("we", [P, DE])
        wl = [sc.sb(f"wl{n}", [P, D]) for n in range(3)]
        zero = sc.sb("zero", [P, W])
        raw = sc.sb("raw", [P, 2, EC], I32)
        no_edge = sc.sb("no_edge", [P, EC])
        later_mask = sc.sb("later_mask", [P, 2, GROUP])
        spare = sc.sb("spare", [P, 2 * GROUPS, 2])
        later = sc.sb("later", [P, 2 * EC])
        own = sc.sb("own", [P, 2 * EC])
        key_int = sc.sb("key_int", [P, 2, EC], I32)
        digit = sc.sb("digit", [P, 4, EC], I32)
        keyb = [sc.sb(f"keyb{s}", [P, 2, P]) for s in range(2)]
        mark = [sc.sb(f"mark{s}", [P, 2, GROUP]) for s in range(2)]
        wps = sc.ps("wps", [P, 8, 512])
        pwt = [wps[:, b, 0:P] for b in range(6)]
        key_rows = [wps[:, 6 + s, 0:GROUP] for s in range(2)]
        params_in, edges_in, zeroed = sc.sem("params_in"), sc.sem("edges_in"), sc.sem("zeroed")
        zero_ready, raw_ready, consts_ready, pool_step = (
            sc.sem(n) for n in ("zero_ready", "raw_ready", "consts_ready", "pool_step"))
        dve_step, wt_ready, keyb_ready, rows_ready, marked = (
            sc.sem(n) for n in ("dve_step", "wt_ready", "keyb_ready", "rows_ready", "marked"))
        block = sc.block()
        NPARAM = 16

        @block.sync
        def _(sp):
            with nc.allow_non_contiguous_dma(reason="parameter vectors as columns"):
                sp.dma_start(w1[:, :, :], g["W1"].rearrange("(b p) f -> p b f", p=P)).then_inc(params_in, 16)
                sp.dma_start(w2[:, :, :], g["W2"].rearrange("p (b f) -> p b f", b=2)).then_inc(params_in, 16)
                sp.dma_start(we[:, :], g["We"]).then_inc(params_in, 16)
                for n, name in enumerate(("WL1", "WL2", "WL3")):
                    sp.dma_start(wl[n][:, :], g[name]).then_inc(params_in, 16)
                sp.dma_start(g["WeT"][DE:DE + 1, :], g["be"][None, :]).then_inc(params_in, 16)
                for col, vec in (("b1c", "b1"), ("g1c", "g1"), ("beta1c", "beta1")):
                    sp.dma_start(g[col][:, :], g[vec].rearrange("(b p) -> p b", p=P)).then_inc(params_in, 16)
                for col, vec in (("b2c", "b2"), ("g2c", "g2"), ("beta2c", "beta2")):
                    sp.dma_start(g[col][:, :], g[vec].rearrange("(p b) -> p b", b=1)).then_inc(params_in, 16)
                sp.dma_start(g["bL2_all"][:, :], g["bL2"][None, :].to_broadcast([P, D])).then_inc(params_in, 16)
                sp.dma_start(g["gin_scale"][:, :], g["eps"][None, :].to_broadcast([P, 1])).then_inc(params_in, 16)
                sp.wait_ge(raw_ready, 1)
                for n, name in enumerate(("dst", "src")):
                    v = g[name]
                    sp.dma_start(raw[0:FULL_P, n, :],
                                 v[0:FULL_P * EC].rearrange("(p k) -> p k", k=EC)).then_inc(edges_in, 16)
                    sp.dma_start(raw[FULL_P:FULL_P + 1, n, 0:REM],
                                 v[FULL_P * EC:E][None, :]).then_inc(edges_in, 16)
            sp.wait_ge(zero_ready, 1)
            z = g["chunked"](g["agg0"])
            for m in range(CHUNKS):
                sp.dma_start(z[m, :, :], zero[:, :]).then_inc(zeroed, 16)
            sp.wait_ge(zeroed, 16 * CHUNKS)

        @block.gpsimd
        def _(pool):
            nc.gpsimd.memset(raw[:, :, :], 0).then_inc(raw_ready, 1)
            nc.gpsimd.memset(zero[:, :], 0.0).then_inc(zero_ready, 1)
            nc.gpsimd.memset(g["ones_col"][:, :], 1.0)
            nc.gpsimd.memset(g["eps_col"][:, :], EPS)
            nc.gpsimd.memset(ident[:, :], 1.0)
            nc.gpsimd.memset(later_mask[:, :, :], 1.0)
            nc.gpsimd.memset(no_edge[:, :], float(N)).then_inc(pool_step, 1)
            pool.wait_ge(pool_step, 1)
            nc.gpsimd.affine_select(out=ident[:, :], in_=ident[:, :], compare_op=ALU.is_equal, fill=0.0,
                                    base=0, pattern=[[-1, P]], channel_multiplier=1)
            nc.gpsimd.affine_select(out=later_mask[:, :, :], in_=later_mask[:, :, :], compare_op=ALU.is_gt,
                                    fill=0.0, base=0, pattern=[[-P, 2], [1, GROUP]], channel_multiplier=-1)
            nc.gpsimd.affine_select(out=no_edge[:, :], in_=no_edge[:, :], compare_op=ALU.is_ge, fill=0.0,
                                    base=-E, pattern=[[1, EC]], channel_multiplier=EC)
            nc.gpsimd.iota(spare[:, :, :], pattern=[[0, 2 * GROUPS], [P, 2]], base=N + 1, channel_multiplier=1,
                           allow_small_or_imprecise_dtypes=True).then_inc(consts_ready, 1)

        @block.tensor
        def _(pe):
            pe.wait_ge(consts_ready, 1)
            pe.wait_ge(params_in, 16 * (NPARAM - 1))
            wide = [w1[:, 0, :], w1[:, 1, :], w2[:, 0, :], w2[:, 1, :]]
            for b, w in enumerate(wide):
                last = nc.tensor.transpose(pwt[b], w, ident[:, :])
            for n in range(2):
                last = nc.tensor.transpose(pwt[4 + n], wl[n][:, :], ident[:, :])
            last = nc.tensor.transpose(wps[:, 4, P:2 * P], wl[2][:, :], ident[:, :])
            last = nc.tensor.transpose(wps[0:DE, 5, P:2 * P], we[:, :], ident[:, :])
            last.then_inc(wt_ready, 1)
            def rows(i):
                for s in range(2):
                    q = 2 * i + s
                    pe.wait_ge(keyb_ready, q + 1)
                    wait(pe, marked, q - 1)
                    for c in range(2):
                        last = nc.tensor.matmul(key_rows[s][:, c * P:(c + 1) * P], keyb[s][:, c, :],
                                                ident[:, :], start=True, stop=True)
                    last.then_inc(rows_ready, 1)
            loop_pairs(pe, GROUPS, rows)

        @block.vector
        def _(dve):
            ch = Chain(dve, dve_step)
            dve.wait_ge(wt_ready, 1)
            nc.vector.tensor_copy(g["W1T"][:, 0:D], pwt[0])
            nc.vector.tensor_copy(g["W1T"][:, D:2 * D], pwt[1])
            nc.vector.tensor_copy(g["W2T"][:, 0, :], pwt[2])
            nc.vector.tensor_copy(g["W2T"][:, 1, :], pwt[3])
            nc.vector.tensor_copy(g["WLT"][0][:, :], pwt[4])
            nc.vector.tensor_copy(g["WLT"][1][:, :], pwt[5])
            nc.vector.tensor_copy(g["WLT"][2][:, :], wps[:, 4, P:2 * P])
            nc.vector.tensor_copy(g["WeT"][0:DE, :], wps[0:DE, 5, P:2 * P])
            dve.wait_ge(params_in, 16 * (NPARAM - 1))
            nc.vector.tensor_scalar(g["gin_scale"][:, :], g["gin_scale"][:, :], 1.0, None, ALU.add)
            dve.wait_ge(edges_in, 64)
            dve.wait_ge(consts_ready, 1)
            for n in range(2):
                ch.mark(nc.vector.tensor_copy(keys[:, n * EC:(n + 1) * EC], raw[:, n, :]))
            ch.sync()
            for n in range(2):
                ch.mark(nc.vector.tensor_tensor(keys[:, n * EC:(n + 1) * EC], keys[:, n * EC:(n + 1) * EC],
                                                no_edge[:, :], ALU.add))
            ch.sync()
            ch.mark(nc.vector.tensor_copy(key_int[:, 1, :], keys[:, EC:2 * EC]))
            ch.sync()
            src_int = key_int[:, 1, :]
            ch.mark(nc.vector.tensor_scalar(digit[:, 0, :], src_int, 3, P - 1, ALU.logical_shift_right,
                                            ALU.bitwise_and))
            ch.mark(nc.vector.tensor_scalar(digit[:, 1, :], src_int, 10, 3, ALU.logical_shift_right,
                                            ALU.logical_shift_left))
            ch.mark(nc.vector.tensor_scalar(digit[:, 2, :], src_int, J - 1, None, ALU.bitwise_and))
            ch.sync()
            ch.mark(nc.vector.tensor_copy(g["lo_digit"][:, :], digit[:, 0, :]))
            ch.mark(nc.vector.tensor_tensor(g["hi_digit"][:, :], digit[:, 1, :], digit[:, 2, :], ALU.add))

            def spread(q, s):
                wait(dve, marked, q - 1)
                nc.vector.tensor_scalar(keyb[s][:, :, :],
                                        keys[:, bass.ds(2 * q, 2)].unsqueeze(2).to_broadcast([P, 2, P]), 1.0, None,
                                        ALU.mult).then_inc(keyb_ready, 1)

            def count(i):
                for s in range(2):
                    q = 2 * i + s
                    if s == 0 or not (isinstance(i, int) and i == GROUPS - 1):
                        spread(q + 1, 1 - s)
                    dve.wait_ge(rows_ready, q + 1)
                    for c in range(2):
                        last = nc.vector.scalar_tensor_tensor(
                            out=mark[s][:, c, :], in0=key_rows[s], scalar=keyb[s][:, c, 0:1],
                            in1=later_mask[:, c, :], op0=ALU.is_equal, op1=ALU.mult,
                            accum_out=later[:, bass.ds(2 * q + c, 1)])
                    last.then_inc(marked, 1)
            spread(0, 0)
            loop_pairs(dve, GROUPS, count)
            dve.wait_ge(marked, 2 * GROUPS)
            spare_flat = spare[:, :, :].rearrange("p q c -> p (q c)")
            ch.mark(nc.vector.tensor_scalar(later[:, :], later[:, :], 1.0, None, ALU.min))
            ch.mark(nc.vector.tensor_tensor(own[:, :], spare_flat, keys[:, :], ALU.subtract))
            ch.sync()
            ch.mark(nc.vector.tensor_tensor(own[:, :], own[:, :], later[:, :], ALU.mult))
            ch.sync()
            ch.mark(nc.vector.tensor_tensor(own[:, :], own[:, :], keys[:, :], ALU.add))
            ch.sync()
            own_v = own[:, :].rearrange("p (n q c) -> p n q c", n=2, c=2)
            raw_v = raw[:, :, :].rearrange("p n (q c) -> p n q c", c=2)
            nc.vector.tensor_copy(index[:, :, 0, :], own_v[:, 1, :, :])
            nc.vector.tensor_copy(index[:, :, 1, :], raw_v[:, 0, :, :])
            nc.vector.tensor_copy(index[:, :, 2, :], raw_v[:, 1, :, :])
            nc.vector.tensor_copy(index[:, :, 3, :], own_v[:, 0, :, :])


def gathered(i, s, lag=0):
    return 32 * (i + 1 - lag)


def slot_step(i, s, ahead):
    return i + (s + ahead) // 2, (s + ahead) % 2


def degrees_and_first_sum(nc, g):
    DE, EC, GROUPS, EPAIRS = g["DE"], g["EDGE_COLS"], g["GROUPS"], g["EPAIRS"]
    FULL_P, REM, E, NCOLS = g["FULL_P"], g["REM"], g["E"], g["NCOLS"]
    keys, index, ident, x, agg0 = g["keys"], g["index"], g["ident"], g["x"], g["agg0"]
    with Scope(nc, "l0") as sc:
        two = range(2)
        attr = sc.sb("attr", [P, EC, DE])
        columns = sc.sb("columns", [P, max(NCOLS, P)])
        gi = [sc.sb(f"gi{s}", [P, 2], I32) for s in two]
        oi = [sc.sb(f"oi{s}", [P, 2], I32) for s in two]
        keyb = [sc.sb(f"keyb{s}", [P, 2, P]) for s in two]
        eq = [sc.sb(f"eq{s}", [P, 2, GROUP]) for s in two]
        rows = [sc.sb(f"rows{s}", [P, 2, D]) for s in two]
        sums = [sc.sb(f"sums{s}", [P, 2, D]) for s in two]
        attr_now = [sc.sb(f"attr_now{s}", [P, 2 * DE + P - DE]) for s in two]
        attrT = [sc.sb(f"attrT{s}", [DE + 1, 2, P]) for s in two]
        msg = [sc.sb(f"msg{s}", [P, 2, D]) for s in two]
        hot_lo = [sc.sb(f"hot_lo{s}", [P, 2, P], BF16) for s in two]
        hot_hi = [sc.sb(f"hot_hi{s}", [P, 2, NCOLS], BF16) for s in two]
        p_keys = sc.ps("p_keys", [P, 512])
        p_attr = sc.ps("p_attr", [P, 512])
        p_sums = [sc.ps(f"p_sums{s}", [P, 512]) for s in two]
        p_msg = [sc.ps(f"p_msg{s}", [P, 512]) for s in two]
        p_deg = sc.ps("p_deg", [P, 2, 512])
        arrived = [sc.sem(f"arrived{s}") for s in two]
        attr_in, cols_ready, attr_zero, added = (sc.sem(n) for n in ("attr_in", "cols_ready", "attr_zero", "added"))
        gi_ready, oi_ready, keyb_ready, rows_ready, eq_ready = (
            sc.sem(n) for n in ("gi_ready", "oi_ready", "keyb_ready", "rows_ready", "eq_ready"))
        attr_now_ready, attrT_psum, attrT_ready, msg_psum, msg_added, msg_ready = (
            sc.sem(n) for n in ("attr_now_ready", "attrT_psum", "attrT_ready", "msg_psum", "msg_added", "msg_ready"))
        summed, sums_ready, hot_ready, hot_used, ones_ready, deg_ready, sq_ready = (
            sc.sem(n) for n in ("summed", "sums_ready", "hot_ready", "hot_used", "ones_ready", "deg_ready", "sq_ready"))
        block = sc.block()
        HI2 = NCOLS - 512 if NCOLS > 512 else 0

        def last_pair(i):
            return isinstance(i, int) and i == EPAIRS - 1

        @block.sync
        def _(sp):
            sp.wait_ge(attr_zero, 1)
            ea = g["edge_attr"]
            sp.dma_start(attr[0:FULL_P, :, :],
                         ea[0:FULL_P * EC, :].rearrange("(p k) f -> p k f", k=EC)).then_inc(attr_in, 16)
            sp.dma_start(attr[FULL_P:FULL_P + 1, 0:REM, :], ea[FULL_P * EC:E, :][None, :, :]).then_inc(attr_in, 16)

        @block.gpsimd
        def _(pool):
            nc.gpsimd.memset(attr[96:P, :, :], 0.0).then_inc(attr_zero, 1)
            pool.wait_ge(attr_zero, 1)
            nc.gpsimd.iota(columns[:, :], pattern=[[1, max(NCOLS, P)]], base=0, channel_multiplier=0,
                           allow_small_or_imprecise_dtypes=True).then_inc(cols_ready, 1)
            gathers, scatters = Turns(pool, sc.tag + "_gathers"), Turns(pool, sc.tag + "_scatters")

            def gather(i, s):
                t = 2 * i + s
                wait(pool, msg_added, t - 1)
                gathers.wait(gi_ready, t)
                for c in two:
                    pool.indirect_dma_start(rows[s][:, c, :], None, x,
                                            bass.IndirectOffsetOnAxis(ap=gi[s][:, c:c + 1], axis=0)
                                            ).then_inc(arrived[s], 16)

            def step(i):
                for s in two:
                    t = 2 * i + s
                    if not (last_pair(i) and s == 1):
                        gather(*slot_step(i, s, 1))
                    pool.wait_ge(oi_ready, t + 1)
                    wait(pool, added, 32 * t)
                    scatters.wait(sums_ready, t)
                    for c in two:
                        pool.indirect_dma_start(agg0, bass.IndirectOffsetOnAxis(ap=oi[s][:, c:c + 1], axis=0),
                                                sums[s][:, c, :], None, compute_op=ALU.add).then_inc(added, 16)
            gather(0, 0)
            loop_pairs(pool, EPAIRS, step)
            pool.wait_ge(added, 32 * GROUPS)

        @block.tensor
        def _(pe):
            def front(i, s):
                t = 2 * i + s
                pe.wait_ge(keyb_ready, t + 1)
                wait(pe, eq_ready, t)
                for c in two:
                    last = nc.tensor.matmul(p_keys[:, c * P:(c + 1) * P], keyb[s][:, c, :], ident[:, :],
                                            start=True, stop=True)
                last.then_inc(rows_ready, 1)
                pe.wait_ge(attr_now_ready, t + 1)
                wait(pe, attrT_ready, t)
                for c in two:
                    last = nc.tensor.transpose(p_attr[:, c * P:(c + 1) * P], attr_now[s][:, c * DE:c * DE + P],
                                               ident[:, :])
                last.then_inc(attrT_psum, 1)
                pe.wait_ge(attrT_ready, t + 1)
                wait(pe, msg_added, t - 1)
                for c in two:
                    last = nc.tensor.matmul(p_msg[s][:, c * D:(c + 1) * D], attrT[s][:, c, :], g["WeT"][:, :],
                                            start=True, stop=True)
                last.then_inc(msg_psum, 1)

            def step(i):
                for s in two:
                    t = 2 * i + s
                    if not (last_pair(i) and s == 1):
                        front(*slot_step(i, s, 1))
                    pe.wait_ge(hot_ready, t + 1)
                    for c in two:
                        first, final = isinstance(i, int) and t == 0 and c == 0, last_pair(i) and s == 1 and c == 1
                        last = nc.tensor.matmul(p_deg[:, 0, 0:min(NCOLS, 512)], hot_lo[s][:, c, :],
                                                hot_hi[s][:, c, 0:min(NCOLS, 512)], start=first, stop=final)
                        if HI2:
                            last = nc.tensor.matmul(p_deg[:, 1, 0:HI2], hot_lo[s][:, c, :],
                                                    hot_hi[s][:, c, 512:NCOLS], start=first, stop=final)
                    last.then_inc(hot_used, 1)
                    pe.wait_ge(eq_ready, t + 1)
                    pe.wait_ge(msg_ready, t + 1)
                    wait(pe, sums_ready, t - 1)
                    for c in two:
                        for k in two:
                            last = nc.tensor.matmul(p_sums[s][:, c * D:(c + 1) * D], eq[s][:, k, c * P:(c + 1) * P],
                                                    msg[s][:, k, :], start=(k == 0), stop=(k == 1))
                    last.then_inc(summed, 1)
            pe.wait_ge(ones_ready, 1)
            front(0, 0)
            loop_pairs(pe, EPAIRS, step)

        @block.scalar
        def _(act):
            def front(i, s):
                t = 2 * i + s
                wait(act, attrT_psum, t - 1)
                nc.scalar.copy(attr_now[s][:, 0:2 * DE].rearrange("p (c f) -> p c f", c=2), attr[:, bass.ds(2 * t, 2), :]).then_inc(attr_now_ready, 1)
                act.wait_ge(attrT_psum, t + 1)
                wait(act, msg_psum, t - 1)
                nc.scalar.copy(attrT[s][0:DE, :, :].rearrange("p c e -> p (c e)"), p_attr[0:DE, 0:GROUP]
                               ).then_inc(attrT_ready, 1)

            def step(i):
                for s in two:
                    t = 2 * i + s
                    if not (last_pair(i) and s == 1):
                        front(*slot_step(i, s, 1))
                    act.wait_ge(msg_added, t + 1)
                    nc.scalar.activation(msg[s][:, :, :], msg[s][:, :, :], ACT.Relu).then_inc(msg_ready, 1)
                    act.wait_ge(summed, t + 1)
                    wait(act, added, 32 * (t - 1))
                    nc.scalar.copy(sums[s][:, :, :].rearrange("p c f -> p (c f)"), p_sums[s][:, 0:2 * D]
                                   ).then_inc(sums_ready, 1)
            act.wait_ge(attr_in, 32)
            front(0, 0)
            loop_pairs(act, EPAIRS, step)
            act.wait_ge(deg_ready, 1)
            nc.scalar.activation(g["norm"][:, :], g["deg1"][:, :], ACT.Sqrt).then_inc(sq_ready, 1)

        @block.vector
        def _(dve):
            for s in two:
                nc.vector.memset(attr_now[s][:, 2 * DE:DE + P], 0.0)
                last = nc.vector.memset(attrT[s][DE:DE + 1, :, :], 1.0)
            last.then_inc(ones_ready, 1)
            dve.wait_ge(cols_ready, 1)

            def front(i, s):
                t = 2 * i + s
                wait(dve, arrived[s], gathered(i, s, 1))
                nc.vector.tensor_scalar(gi[s][:, :], index[:, bass.ds(t, 1), 2, :].rearrange("p a c -> p (a c)"), 1.0, None, ALU.mult
                                      ).then_inc(gi_ready, 1)
                wait(dve, eq_ready, t - 1)
                nc.vector.tensor_copy(keyb[s][:, :, :],
                                      keys[:, bass.ds(2 * t, 2)].unsqueeze(2).to_broadcast([P, 2, P])
                                      ).then_inc(keyb_ready, 1)

            def step(i):
                for s in two:
                    t = 2 * i + s
                    if not (last_pair(i) and s == 1):
                        front(*slot_step(i, s, 1))
                    wait(dve, hot_used, t - 1)
                    for c in two:
                        nc.vector.tensor_scalar(hot_lo[s][:, c, :], columns[:, 0:P],
                                                g["lo_digit"][:, bass.ds(2 * t + c, 1)], None, ALU.is_equal)
                        last = nc.vector.tensor_scalar(hot_hi[s][:, c, :], columns[:, 0:NCOLS],
                                                       g["hi_digit"][:, bass.ds(2 * t + c, 1)], None, ALU.is_equal)
                    last.then_inc(hot_ready, 1)
                    dve.wait_ge(rows_ready, t + 1)
                    wait(dve, summed, t - 1)
                    for c in two:
                        last = nc.vector.tensor_scalar(eq[s][:, c, :], p_keys[:, 0:GROUP], keyb[s][:, c, 0:1], None,
                                                       ALU.is_equal)
                    last.then_inc(eq_ready, 1)
                    wait(dve, added, 32 * (t - 1))
                    nc.vector.tensor_scalar(oi[s][:, :], index[:, bass.ds(t, 1), 3, :].rearrange("p a c -> p (a c)"), 1.0, None, ALU.mult
                                          ).then_inc(oi_ready, 1)
                    dve.wait_ge(msg_psum, t + 1)
                    dve.wait_ge(arrived[s], gathered(i, s))
                    nc.vector.tensor_tensor(msg[s][:, :, :].rearrange("p c f -> p (c f)"), p_msg[s][:, 0:2 * D],
                                            rows[s][:, :, :].rearrange("p c f -> p (c f)"), ALU.add
                                            ).then_inc(msg_added, 1)
            front(0, 0)
            loop_pairs(dve, EPAIRS, step)
            dve.wait_ge(hot_used, GROUPS)
            last = nc.vector.tensor_scalar(g["deg1"][:, 0:min(NCOLS, 512)], p_deg[:, 0, 0:min(NCOLS, 512)], 1.0, None,
                                           ALU.add)
            if HI2:
                last = nc.vector.tensor_scalar(g["deg1"][:, 512:NCOLS], p_deg[:, 1, 0:HI2], 1.0, None, ALU.add)
            last.then_inc(deg_ready, 1)
            dve.wait_ge(sq_ready, 1)
            nc.vector.reciprocal(g["norm"][:, :], g["norm"][:, :])
            nc.vector.reciprocal(g["norm2"][:, :], g["deg1"][:, :])


def first_norm(nc, g):
    N, CHUNKS, PAIRS = g["N"], g["CHUNKS"], g["PAIRS"]
    moments, W1T = g["moments"], g["W1T"]
    with Scope(nc, "bn1") as sc:
        two = range(2)
        xb = [sc.sb(f"xb{s}", [P, W]) for s in two]
        ab = [sc.sb(f"ab{s}", [P, W]) for s in two]
        hb = [sc.sb(f"hb{s}", [P, J, D + 1]) for s in two]
        mrow = sc.sb("mrow", [1, D])
        cov = sc.sb("cov", [P, D])
        prod = sc.sb("prod", [P, 2 * D])
        mean_z, var_z, std_z = (sc.sb(n, [P, 2]) for n in ("mean_z", "var_z", "std_z"))
        p_mom = sc.ps("p_mom", [P, 512])
        p_small = sc.ps("p_small", [P, 512])
        p_prod = sc.ps("p_prod", [P, 512])
        p_row = sc.ps("p_row", [1, 512])
        p_out = sc.ps("p_out", [P, 512])
        p_var = sc.ps("p_var", [P, 512])
        x_in = [sc.sem(f"x_in{s}") for s in two]
        a_in = [sc.sem(f"a_in{s}") for s in two]
        h_ready, h_used, dve_step, pe_step, std_ready = (
            sc.sem(n) for n in ("h_ready", "h_used", "dve_step", "pe_step", "std_ready"))
        block = sc.block()
        aggv = g["chunked"](g["agg0"])

        @block.sync
        def _(sp):
            def load(i):
                for s in two:
                    m = 2 * i + s
                    r = g["rows_of"](m)
                    wait(sp, h_ready, m - 1)
                    sp.dma_start(xb[s][0:r, :], g["node_rows"](g["x"], m, r)).then_inc(x_in[s], 16)
                    sp.dma_start(ab[s][:, :], g["at"](aggv, m)).then_inc(a_in[s], 16)
            loop_pairs(sp, PAIRS, load)

        @block.vector
        def _(dve):
            for s in two:
                nc.vector.memset(hb[s][:, :, D:D + 1], 1.0)

            def add(i):
                for s in two:
                    m = 2 * i + s
                    dve.wait_ge(x_in[s], 16 * (i + 1))
                    dve.wait_ge(a_in[s], 16 * (i + 1))
                    wait(dve, h_used, m - 1)
                    nc.vector.scalar_tensor_tensor(
                        out=hb[s][:, :, 0:D], in0=xb[s][:, :].rearrange("p (j f) -> p j f", j=J),
                        scalar=g["gin_scale"][:, 0:1], in1=ab[s][:, :].rearrange("p (j f) -> p j f", j=J),
                        op0=ALU.mult, op1=ALU.add).then_inc(h_ready, 1)
            loop_pairs(dve, PAIRS, add)
            ch = Chain(dve, dve_step)
            dve.wait_ge(h_used, CHUNKS)
            ch.mark(nc.vector.tensor_scalar(moments[:, :], p_mom[:, 0:D + 1], 1.0 / N, None, ALU.mult))
            dve.wait_ge(pe_step, 1)
            ch.mark(nc.vector.tensor_copy(mrow[:, :], p_row[0:1, 0:D]))
            dve.wait_ge(pe_step, 2)
            ch.sync()
            ch.mark(nc.vector.tensor_tensor(cov[:, :], moments[:, 0:D], p_out[:, 0:D], ALU.subtract))
            dve.wait_ge(pe_step, 3)
            ch.mark(nc.vector.tensor_tensor(prod[:, :], W1T[:, :], p_prod[:, 0:2 * D], ALU.mult))
            ch.mark(nc.vector.tensor_tensor(mean_z[:, :], p_small[:, 0:2], g["b1c"][:, :], ALU.add))
            dve.wait_ge(pe_step, 4)
            ch.mark(nc.vector.tensor_copy(var_z[:, :], p_var[:, 0:2]))
            dve.wait_ge(std_ready, 1)
            ch.mark(nc.vector.reciprocal(std_z[:, :], std_z[:, :]))
            ch.mark(nc.vector.tensor_tensor(mean_z[:, :], g["b1c"][:, :], mean_z[:, :], ALU.subtract))
            ch.sync()
            ch.mark(nc.vector.tensor_tensor(g["a1"][:, :], std_z[:, :], g["g1c"][:, :], ALU.mult))
            ch.sync()
            ch.mark(nc.vector.tensor_tensor(mean_z[:, :], mean_z[:, :], g["a1"][:, :], ALU.mult))
            ch.sync()
            ch.mark(nc.vector.tensor_tensor(g["t1"][:, :], mean_z[:, :], g["beta1c"][:, :], ALU.add))

        @block.tensor
        def _(pe):
            def products(i):
                for s in two:
                    m = 2 * i + s
                    r = g["rows_of"](m)
                    pe.wait_ge(h_ready, m + 1)
                    for j in range(J):
                        last = nc.tensor.matmul(
                            p_mom[:, 0:D + 1], hb[s][0:r, j, 0:D], hb[s][0:r, j, :],
                            start=(isinstance(i, int) and m == 0 and j == 0),
                            stop=(isinstance(i, int) and m == CHUNKS - 1 and j == J - 1))
                    last.then_inc(h_used, 1)
            loop_pairs(pe, PAIRS, products)
            pe.wait_ge(dve_step, 1)
            nc.tensor.transpose(p_row[0:1, 0:P], moments[:, D:D + 1], g["ident"][:, :]).then_inc(pe_step, 1)
            pe.wait_ge(dve_step, 2)
            nc.tensor.matmul(p_out[:, 0:D], mrow[:, :], mrow[:, :], start=True, stop=True).then_inc(pe_step, 1)
            for b in two:
                nc.tensor.matmul(p_small[:, b:b + 1], W1T[:, b * D:(b + 1) * D], moments[:, D:D + 1],
                                 start=True, stop=True)
            pe.wait_ge(dve_step, 3)
            nc.tensor.matmul(p_prod[:, 0:2 * D], cov[:, :], W1T[:, :], start=True, stop=True).then_inc(pe_step, 1)
            pe.wait_ge(dve_step, 4)
            for b in two:
                last = nc.tensor.matmul(p_var[:, b:b + 1], prod[:, b * D:(b + 1) * D], g["ones_col"][:, :],
                                        start=True, stop=True)
            last.then_inc(pe_step, 1)

        @block.scalar
        def _(act):
            act.wait_ge(dve_step, 6)
            nc.scalar.activation(std_z[:, :], var_z[:, :], ACT.Sqrt, bias=g["eps_col"][:, 0:1]).then_inc(std_ready, 1)


def mlp(nc, g):
    CHUNKS, PAIRS, NPAD = g["CHUNKS"], g["PAIRS"], g["NPAD"]
    W1T, W2T, ident = g["W1T"], g["W2T"], g["ident"]
    with Scope(nc, "mlp") as sc:
        two = range(2)
        xb = [sc.sb(f"xb{s}", [P, W]) for s in two]
        ab = [sc.sb(f"ab{s}", [P, W]) for s in two]
        hb = [sc.sb(f"hb{s}", [P, W]) for s in two]
        hT = [sc.sb(f"hT{q}", [P, HALF]) for q in two]
        act1 = [sc.sb(f"act1{q}", [P, 2, HALF]) for q in two]
        z2 = [sc.sb(f"z2{s}", [P, W]) for s in two]
        stats = sc.sb("stats", [P, 2 * CHUNKS, 6])
        mv = sc.sb("mv", [P, 2])
        std = sc.sb("std", [P, 1])
        zero = sc.sb("zero", [P, W])
        fresh = sc.sb("fresh", [P, J, STATE])
        p_hT = [sc.ps(f"p_hT{q}", [P, HALF]) for q in two]
        p_z1 = [sc.ps(f"p_z1{q}", [P, 2, HALF]) for q in two]
        p_z2 = [sc.ps(f"p_z2{q}", [P, HALF]) for q in two]
        x_in = [sc.sem(f"x_in{s}") for s in two]
        a_in = [sc.sem(f"a_in{s}") for s in two]
        stored = [sc.sem(f"stored{s}") for s in two]
        cleared, zero_ready, pool_step = (sc.sem(n) for n in ("cleared", "zero_ready", "pool_step"))
        h_ready, h_used, hT_ready, z1_ready, act1_ready, z2_psum, z2_ready, z2_counted = (
            sc.sem(n) for n in ("h_ready", "h_used", "hT_ready", "z1_ready", "act1_ready", "z2_psum", "z2_ready",
                                "z2_counted"))
        dve_step, std_ready = sc.sem("dve_step"), sc.sem("std_ready")
        block = sc.block()
        aggv = g["chunked"](g["agg0"])
        cleared_tables = [(g["chunked"](g["agg1"]), zero[:, :]), (g["chunked"](g["agg2"]), zero[:, :]),
                          (g["chunked"](g["state_t"]), fresh[:, :, :].rearrange("p j f -> p (j f)"))]

        @block.sync
        def _(sp):
            sp.wait_ge(zero_ready, 1)

            def load(i):
                for s in two:
                    m = 2 * i + s
                    r = g["rows_of"](m)
                    wait(sp, h_ready, m - 1)
                    sp.dma_start(xb[s][0:r, :], g["node_rows"](g["x"], m, r)).then_inc(x_in[s], 16)
                    sp.dma_start(ab[s][:, :], g["at"](aggv, m)).then_inc(a_in[s], 16)
                    for table, value in cleared_tables:
                        sp.dma_start(g["at"](table, m), value).then_inc(cleared, 16)
            loop_pairs(sp, PAIRS, load)
            sp.wait_ge(cleared, 16 * 3 * CHUNKS)

        @block.gpsimd
        def _(pool):
            nc.gpsimd.memset(zero[:, :], 0.0)
            nc.gpsimd.memset(fresh[:, :, 0:D + HEADS], 0.0)
            nc.gpsimd.memset(fresh[:, :, D + HEADS:STATE], LOWEST).then_inc(zero_ready, 1)

            def store(i):
                for s in two:
                    m = 2 * i + s
                    pool.wait_ge(z2_ready, 2 * (m + 1))
                    pool.dma_start(g["at"](g["z2_t"], m), z2[s][:, :]).then_inc(stored[s], 16)
            loop_pairs(pool, PAIRS, store)
            for s in two:
                pool.wait_ge(stored[s], 16 * PAIRS)

        @block.vector
        def _(dve):
            def add(i, s):
                m = 2 * i + s
                dve.wait_ge(x_in[s], 16 * (i + 1))
                dve.wait_ge(a_in[s], 16 * (i + 1))
                wait(dve, h_used, 2 * (m - 1))
                nc.vector.scalar_tensor_tensor(out=hb[s][:, :], in0=xb[s][:, :], scalar=g["gin_scale"][:, 0:1],
                                               in1=ab[s][:, :], op0=ALU.mult, op1=ALU.add).then_inc(h_ready, 1)

            def evacuate(i, s, q):
                u = 4 * i + 2 * s + q
                dve.wait_ge(h_used, u + 1)
                wait(dve, z1_ready, u - 1)
                nc.vector.tensor_copy(hT[q][:, :], p_hT[q][:, :]).then_inc(hT_ready, 1)

            def count(i, s, q):
                u = 4 * i + 2 * s + q
                r = g["rows_of"](2 * i + s)
                dve.wait_ge(z2_ready, u + 1)
                z = z2[s][:, q * HALF:(q + 1) * HALF]
                z = z if r == P else z.rearrange("p (j n) -> p j n", n=P)[:, :, 0:r]
                if isinstance(u, int):
                    o = stats[:, u, :]
                else:
                    o = stats[:, bass.ds(u, 1), :].rearrange("p a k -> p (a k)")
                nc.vector.bn_stats(o, z).then_inc(z2_counted, 1)

            def step(i):
                last_pair = isinstance(i, int) and i == PAIRS - 1
                first_pair = isinstance(i, int) and i == 0
                for s in two:
                    for q in two:
                        u4 = 2 * s + q
                        if u4 == 0 and not first_pair:
                            count(i - 1, 1, 1)
                        if u4 == 3 and last_pair:
                            count(i, 1, 0)
                            continue
                        if q == 1 and not (last_pair and s == 1):
                            add(*slot_step(i, s, 1))
                            evacuate(*slot_step(i, s, 1), 0)
                        elif q == 0:
                            evacuate(i, s, 1)
                        if u4:
                            count(i, (u4 - 1) // 2, (u4 - 1) % 2)
            dve.wait_ge(zero_ready, 1)
            add(0, 0)
            evacuate(0, 0, 0)
            loop_pairs(dve, PAIRS, step)
            count(PAIRS - 1, 1, 1)
            dve.wait_ge(z2_counted, 2 * CHUNKS)
            ch = Chain(dve, dve_step)
            ch.mark(nc.vector.bn_aggr(mv[:, :], stats[:, :, :].rearrange("p u k -> p (u k)")))
            dve.wait_ge(std_ready, 1)
            ch.sync()
            ch.mark(nc.vector.reciprocal(std[:, :], std[:, :]))
            ch.mark(nc.vector.tensor_tensor(mv[:, 0:1], mv[:, 0:1], g["b2c"][:, :], ALU.add))
            ch.sync()
            ch.mark(nc.vector.tensor_tensor(g["a2"][:, :], std[:, :], g["g2c"][:, :], ALU.mult))
            ch.mark(nc.vector.tensor_tensor(mv[:, 0:1], g["b2c"][:, :], mv[:, 0:1], ALU.subtract))
            ch.sync()
            ch.mark(nc.vector.tensor_tensor(mv[:, 0:1], mv[:, 0:1], g["a2"][:, :], ALU.mult))
            ch.sync()
            ch.mark(nc.vector.tensor_tensor(g["t2"][:, :], mv[:, 0:1], g["beta2c"][:, :], ALU.add))

        @block.scalar
        def _(act):
            def relu(i, s, q):
                u = 4 * i + 2 * s + q
                act.wait_ge(z1_ready, u + 1)
                wait(act, z2_psum, u - 1)
                for b in two:
                    last = nc.scalar.activation(act1[q][:, b, :], p_z1[q][:, b, :], ACT.Relu,
                                                bias=g["t1"][:, b:b + 1], scale=g["a1"][:, b:b + 1])
                last.then_inc(act1_ready, 1)

            def evacuate(i, s, q):
                u = 4 * i + 2 * s + q
                act.wait_ge(z2_psum, u + 1)
                if q == 0:
                    wait(act, stored[s], 16 * i)
                    wait(act, z2_counted, 4 * i + 2 * s - 2)
                nc.scalar.copy(z2[s][:, q * HALF:(q + 1) * HALF], p_z2[q][:, :]).then_inc(z2_ready, 1)

            def step(i):
                first_pair = isinstance(i, int) and i == 0
                for s in two:
                    for q in two:
                        relu(i, s, q)
                        u4 = 2 * s + q
                        if u4:
                            evacuate(i, (u4 - 1) // 2, (u4 - 1) % 2)
                        elif not first_pair:
                            evacuate(i - 1, 1, 1)
            loop_pairs(act, PAIRS, step)
            evacuate(PAIRS - 1, 1, 1)
            act.wait_ge(dve_step, 1)
            nc.scalar.activation(std[:, :], mv[:, 1:2], ACT.Sqrt, bias=g["eps_col"][:, 0:1]).then_inc(std_ready, 1)

        @block.tensor
        def _(pe):
            def turn(i, s, q):
                u = 4 * i + 2 * s + q
                pe.wait_ge(h_ready, 2 * i + s + 1)
                wait(pe, hT_ready, u - 1)
                for k in range(J // 2):
                    j = q * (J // 2) + k
                    last = nc.tensor.transpose(p_hT[q][:, k * P:(k + 1) * P], hb[s][:, j * D:(j + 1) * D], ident[:, :])
                last.then_inc(h_used, 1)

            def first(i, s, q):
                u = 4 * i + 2 * s + q
                pe.wait_ge(hT_ready, u + 1)
                wait(pe, act1_ready, u - 1)
                for b in two:
                    last = nc.tensor.matmul(p_z1[q][:, b, :], W1T[:, b * D:(b + 1) * D], hT[q][:, :],
                                            start=True, stop=True)
                last.then_inc(z1_ready, 1)

            def second(i, s, q):
                u = 4 * i + 2 * s + q
                pe.wait_ge(act1_ready, u + 1)
                wait(pe, z2_ready, u - 1)
                for b in two:
                    last = nc.tensor.matmul(p_z2[q][:, :], W2T[:, b, :], act1[q][:, b, :],
                                            start=(b == 0), stop=(b == 1))
                last.then_inc(z2_psum, 1)

            def step(i):
                first_pair = isinstance(i, int) and i == 0
                last_pair = isinstance(i, int) and i == PAIRS - 1
                for s in two:
                    for q in two:
                        first(i, s, q)
                        if q == 0:
                            turn(i, s, 1)
                        elif not (last_pair and s == 1):
                            turn(*slot_step(i, s, 1), 0)
                        u4 = 2 * s + q
                        if u4:
                            second(i, (u4 - 1) // 2, (u4 - 1) % 2)
                        elif not first_pair:
                            second(i - 1, 1, 1)
            turn(0, 0, 0)
            loop_pairs(pe, PAIRS, step)
            second(PAIRS - 1, 1, 1)


class NodeNorm:

    def __init__(self, nc, sc, g):
        self.nc, self.g = nc, g
        self.u = [sc.sb(f"u{s}", [P, J, D]) for s in range(2)]
        self.y = [sc.sb(f"y{s}", [P, J, D]) for s in range(2)]
        self.stats = sc.sb("stats", [P, J, 6])
        self.tmp = sc.sb("tmp", [P, 3, J])
        self.mean = [sc.sb(f"mean{s}", [P, J]) for s in range(2)]
        self.var = [sc.sb(f"var{s}", [P, J]) for s in range(2)]
        self.std = [sc.sb(f"std{s}", [P, J]) for s in range(2)]
        self.rstd = [sc.sb(f"rstd{s}", [P, J]) for s in range(2)]
        self.step = sc.sem("dve_step")
        self.u_ready, self.var_ready, self.std_ready, self.y_ready = (
            sc.sem(n) for n in ("u_ready", "var_ready", "std_ready", "y_ready"))
        self.stored = [sc.sem(f"stored{s}") for s in range(2)]

    def statistics(self, dve, ch, i, s, scale2=None):
        nc, st = self.nc, self.stats
        m = 2 * i + s
        dve.wait_ge(self.u_ready, m + 1)
        for j in range(J):
            last = nc.vector.bn_stats(st[:, j, :], self.u[s][:, j, :])
        ch.mark(last)
        ch.sync()
        tot, dif, m2 = (self.tmp[:, k, :] for k in range(3))
        wait(dve, self.y_ready, m - 1)
        ch.mark(nc.vector.tensor_tensor(tot, st[:, :, 1], st[:, :, 4], ALU.add))
        ch.mark(nc.vector.tensor_tensor(dif, st[:, :, 1], st[:, :, 4], ALU.subtract))
        ch.mark(nc.vector.tensor_tensor(m2, st[:, :, 2], st[:, :, 5], ALU.add))
        ch.sync()
        ch.mark(nc.vector.tensor_scalar(self.mean[s][:, :], tot, 0.5, None, ALU.mult))
        ch.mark(nc.vector.scalar_tensor_tensor(out=dif, in0=dif, scalar=0.25, in1=dif, op0=ALU.mult, op1=ALU.mult))
        ch.sync()
        wait(dve, self.std_ready, m - 1)
        var = nc.vector.scalar_tensor_tensor(out=self.var[s][:, :], in0=m2, scalar=1.0 / D, in1=dif,
                                             op0=ALU.mult, op1=ALU.add)
        if scale2 is not None:
            ch.mark(var)
            ch.sync()
            var = nc.vector.tensor_tensor(self.var[s][:, :], self.var[s][:, :], scale2, ALU.mult)
        var.then_inc(self.var_ready, 1)

    def root(self, act, i, s):
        m = 2 * i + s
        act.wait_ge(self.var_ready, m + 1)
        wait(act, self.y_ready, m - 1)
        self.nc.scalar.activation(self.std[s][:, :], self.var[s][:, :], ACT.Sqrt,
                                  bias=self.g["eps_col"][:, 0:1]).then_inc(self.std_ready, 1)

    def apply(self, dve, ch, i, s, scale=None):
        nc = self.nc
        dve.wait_ge(self.std_ready, 2 * i + s + 1)
        ch.mark(nc.vector.reciprocal(self.rstd[s][:, :], self.std[s][:, :]))
        ch.sync()
        if scale is not None:
            ch.mark(nc.vector.tensor_tensor(self.rstd[s][:, :], self.rstd[s][:, :], scale, ALU.mult))
            ch.sync()
        wait(dve, self.stored[s], 16 * i)
        for j in range(J):
            last = nc.vector.tensor_scalar(self.y[s][:, j, :], self.u[s][:, j, :], self.mean[s][:, j:j + 1],
                                           self.rstd[s][:, j:j + 1], ALU.subtract, ALU.mult)
        last.then_inc(self.y_ready, 1)

    def store(self, sp, i, s, where):
        sp.wait_ge(self.y_ready, 2 * i + s + 1)
        rows = where.shape[0]
        sp.dma_start(where, self.y[s][0:rows, :, :].rearrange("p j f -> p (j f)")).then_inc(self.stored[s], 16)

    def finish(self, sp, pairs):
        for s in range(2):
            sp.wait_ge(self.stored[s], 16 * pairs)


def flat(b):
    return b[:, :, :].rearrange("p j f -> p (j f)")


def ahead(pairs, i, s):
    return None if isinstance(i, int) and i == pairs - 1 and s == 1 else slot_step(i, s, 1)


def behind(i, s):
    if s == 1:
        return i, 0
    return None if isinstance(i, int) and i == 0 else (i - 1, 1)


def per_node(table, i, s):
    return table[:, bass.ds((2 * i + s) * J, J)]


def first_layer_out(nc, g):
    PAIRS = g["PAIRS"]
    with Scope(nc, "out1") as sc:
        two = range(2)
        xb = [sc.sb(f"xb{s}", [P, W]) for s in two]
        zb = [sc.sb(f"zb{s}", [P, W]) for s in two]
        rb = [sc.sb(f"rb{s}", [P, W]) for s in two]
        p_r = [sc.ps(f"p_r{s}", [P, W]) for s in two]
        nn = NodeNorm(nc, sc, g)
        x_in = [sc.sem(f"x_in{s}") for s in two]
        z_in = [sc.sem(f"z_in{s}") for s in two]
        r_ready, turned = sc.sem("r_ready"), sc.sem("turned")
        block = sc.block()
        outv = g["chunked"](g["x1n_t"])

        @block.sync
        def _(sp):
            def load(i, s):
                m = 2 * i + s
                r = g["rows_of"](m)
                wait(sp, r_ready, m - 1)
                sp.dma_start(zb[s][:, :], g["at"](g["z2_t"], m)).then_inc(z_in[s], 16)
                wait(sp, nn.u_ready, m - 1)
                sp.dma_start(xb[s][0:r, :], g["node_rows"](g["x"], m, r)).then_inc(x_in[s], 16)

            def step(i):
                for s in two:
                    if ahead(PAIRS, i, s):
                        load(*ahead(PAIRS, i, s))
                    if behind(i, s):
                        b = behind(i, s)
                        nn.store(sp, *b, g["at"](outv, 2 * b[0] + b[1]))
            load(0, 0)
            loop_pairs(sp, PAIRS, step)
            nn.store(sp, PAIRS - 1, 1, g["at"](outv, 2 * PAIRS - 1))
            nn.finish(sp, PAIRS)

        @block.scalar
        def _(act):
            def relu(i, s):
                m = 2 * i + s
                act.wait_ge(z_in[s], 16 * (i + 1))
                wait(act, turned, m - 1)
                nc.scalar.activation(rb[s][:, :], zb[s][:, :], ACT.Relu, bias=g["t2"][:, 0:1],
                                     scale=g["a2"][:, 0:1]).then_inc(r_ready, 1)

            def step(i):
                for s in two:
                    if ahead(PAIRS, i, s):
                        relu(*ahead(PAIRS, i, s))
                    nn.root(act, i, s)
            relu(0, 0)
            loop_pairs(act, PAIRS, step)

        @block.tensor
        def _(pe):
            def step(i):
                for s in two:
                    m = 2 * i + s
                    pe.wait_ge(r_ready, m + 1)
                    wait(pe, nn.u_ready, m - 1)
                    for j in range(J):
                        last = nc.tensor.transpose(p_r[s][:, j * D:(j + 1) * D], rb[s][:, j * P:(j + 1) * P],
                                                   g["ident"][:, :])
                    last.then_inc(turned, 1)
            loop_pairs(pe, PAIRS, step)

        @block.vector
        def _(dve):
            ch = Chain(dve, nn.step)

            def step(i):
                for s in two:
                    m = 2 * i + s
                    dve.wait_ge(x_in[s], 16 * (i + 1))
                    dve.wait_ge(turned, m + 1)
                    wait(dve, nn.y_ready, m - 1)
                    nc.vector.tensor_tensor(flat(nn.u[s]), p_r[s][:, :], xb[s][:, :], ALU.add
                                            ).then_inc(nn.u_ready, 1)
                    nn.statistics(dve, ch, i, s)
                    if behind(i, s):
                        b = behind(i, s)
                        nn.apply(dve, ch, *b, scale=per_node(g["norm"], *b))
            loop_pairs(dve, PAIRS, step, ch, 16)
            nn.apply(dve, ch, PAIRS - 1, 1, scale=per_node(g["norm"], PAIRS - 1, 1))


def aggregate(nc, g, tag, table, acc, key_at, gather_kind, owner_kind):
    EC, GROUPS, EPAIRS = g["EDGE_COLS"], g["GROUPS"], g["EPAIRS"]
    keys, index, ident = g["keys"], g["index"], g["ident"]
    with Scope(nc, "sum_" + tag) as sc:
        two = range(2)
        gi = [sc.sb(f"gi{s}", [P, 2], I32) for s in two]
        oi = [sc.sb(f"oi{s}", [P, 2], I32) for s in two]
        keyb = [sc.sb(f"keyb{s}", [P, 2, P]) for s in two]
        eq = [sc.sb(f"eq{s}", [P, 2, GROUP]) for s in two]
        rows = [sc.sb(f"rows{s}", [P, 2, D]) for s in two]
        sums = [sc.sb(f"sums{s}", [P, 2, D]) for s in two]
        p_keys = [sc.ps(f"p_keys{s}", [P, 512]) for s in two]
        p_sums = [sc.ps(f"p_sums{s}", [P, 512]) for s in two]
        arrived = [sc.sem(f"arrived{s}") for s in two]
        added, gi_ready, oi_ready, keyb_ready, rows_ready, eq_ready, summed, sums_ready = (
            sc.sem(n) for n in ("added", "gi_ready", "oi_ready", "keyb_ready", "rows_ready", "eq_ready", "summed",
                                "sums_ready"))
        block = sc.block()

        @block.gpsimd
        def _(pool):
            gathers, scatters = Turns(pool, sc.tag + "_gathers"), Turns(pool, sc.tag + "_scatters")

            def gather(i, s):
                t = 2 * i + s
                wait(pool, summed, t - 1)
                gathers.wait(gi_ready, t)
                for c in two:
                    pool.indirect_dma_start(rows[s][:, c, :], None, table,
                                            bass.IndirectOffsetOnAxis(ap=gi[s][:, c:c + 1], axis=0)
                                            ).then_inc(arrived[s], 16)

            def step(i):
                for s in two:
                    t = 2 * i + s
                    if ahead(EPAIRS, i, s):
                        gather(*ahead(EPAIRS, i, s))
                    pool.wait_ge(oi_ready, t + 1)
                    wait(pool, added, 32 * t)
                    scatters.wait(sums_ready, t)
                    for c in two:
                        pool.indirect_dma_start(acc, bass.IndirectOffsetOnAxis(ap=oi[s][:, c:c + 1], axis=0),
                                                sums[s][:, c, :], None, compute_op=ALU.add).then_inc(added, 16)
            gather(0, 0)
            loop_pairs(pool, EPAIRS, step)
            pool.wait_ge(added, 32 * GROUPS)

        @block.tensor
        def _(pe):
            def spread(i, s):
                t = 2 * i + s
                pe.wait_ge(keyb_ready, t + 1)
                wait(pe, eq_ready, t - 1)
                for c in two:
                    last = nc.tensor.matmul(p_keys[s][:, c * P:(c + 1) * P], keyb[s][:, c, :], ident[:, :],
                                            start=True, stop=True)
                last.then_inc(rows_ready, 1)

            def step(i):
                for s in two:
                    t = 2 * i + s
                    if ahead(EPAIRS, i, s):
                        spread(*ahead(EPAIRS, i, s))
                    pe.wait_ge(eq_ready, t + 1)
                    pe.wait_ge(arrived[s], gathered(i, s))
                    wait(pe, sums_ready, t - 1)
                    for c in two:
                        for k in two:
                            last = nc.tensor.matmul(p_sums[s][:, c * D:(c + 1) * D], eq[s][:, k, c * P:(c + 1) * P],
                                                    rows[s][:, k, :], start=(k == 0), stop=(k == 1))
                    last.then_inc(summed, 1)
            spread(0, 0)
            loop_pairs(pe, EPAIRS, step)

        @block.scalar
        def _(act):
            def step(i):
                for s in two:
                    t = 2 * i + s
                    act.wait_ge(summed, t + 1)
                    wait(act, added, 32 * (t - 1))
                    nc.scalar.copy(sums[s][:, :, :].rearrange("p c f -> p (c f)"), p_sums[s][:, 0:2 * D]
                                   ).then_inc(sums_ready, 1)
            loop_pairs(act, EPAIRS, step)

        @block.vector
        def _(dve):
            def front(i, s):
                t = 2 * i + s
                wait(dve, arrived[s], gathered(i, s, 1))
                nc.vector.tensor_scalar(gi[s][:, :],
                                      index[:, bass.ds(t, 1), gather_kind, :].rearrange("p a c -> p (a c)"), 1.0, None, ALU.mult
                                      ).then_inc(gi_ready, 1)
                wait(dve, eq_ready, t - 1)
                nc.vector.tensor_copy(keyb[s][:, :, :],
                                      keys[:, bass.ds(2 * t + key_at, 2)].unsqueeze(2).to_broadcast([P, 2, P])
                                      ).then_inc(keyb_ready, 1)

            def step(i):
                for s in two:
                    t = 2 * i + s
                    if ahead(EPAIRS, i, s):
                        front(*ahead(EPAIRS, i, s))
                    dve.wait_ge(rows_ready, t + 1)
                    wait(dve, summed, t - 1)
                    for c in two:
                        last = nc.vector.tensor_scalar(eq[s][:, c, :], p_keys[s][:, 0:GROUP], keyb[s][:, c, 0:1], None,
                                                       ALU.is_equal)
                    last.then_inc(eq_ready, 1)
                    wait(dve, added, 32 * (t - 1))
                    nc.vector.tensor_scalar(oi[s][:, :],
                                          index[:, bass.ds(t, 1), owner_kind, :].rearrange("p a c -> p (a c)"), 1.0, None, ALU.mult
                                          ).then_inc(oi_ready, 1)
            front(0, 0)
            loop_pairs(dve, EPAIRS, step)


def convolve(nc, g, tag, table, acc, result, WT):
    PAIRS = g["PAIRS"]
    first = tag == "l1"
    with Scope(nc, "conv_" + tag) as sc:
        two = range(2)
        xb = [sc.sb(f"xb{s}", [P, J, D]) for s in two]
        ab = [sc.sb(f"ab{s}", [P, J, D]) for s in two]
        gb = [sc.sb(f"gb{s}", [P, J, D]) for s in two] if first else ab
        vb = [sc.sb(f"vb{s}", [P, J, D]) for s in two]
        gT = [sc.sb(f"gT{s}", [P, W]) for s in two]
        p_g = [sc.ps(f"p_g{s}", [P, W]) for s in two]
        p_o = [sc.ps(f"p_o{s}", [P, W]) for s in two]
        nn = NodeNorm(nc, sc, g)
        x_in = [sc.sem(f"x_in{s}") for s in two]
        a_in = [sc.sem(f"a_in{s}") for s in two]
        g_ready, v_ready, turned, gT_ready, o_ready = (
            sc.sem(n) for n in ("g_ready", "v_ready", "turned", "gT_ready", "o_ready"))
        block = sc.block()
        xv, av, outv = (g["chunked"](t) for t in (table, acc, result))

        @block.sync
        def _(sp):
            def load(i, s):
                m = 2 * i + s
                wait(sp, v_ready, m - 1)
                sp.dma_start(flat(xb[s]), g["at"](xv, m)).then_inc(x_in[s], 16)
                if not first:
                    wait(sp, turned, m - 1)
                sp.dma_start(flat(ab[s]), g["at"](av, m)).then_inc(a_in[s], 16)

            def step(i):
                for s in two:
                    if ahead(PAIRS, i, s):
                        load(*ahead(PAIRS, i, s))
                    if behind(i, s):
                        b = behind(i, s)
                        nn.store(sp, *b, g["at"](outv, 2 * b[0] + b[1]))
            load(0, 0)
            loop_pairs(sp, PAIRS, step)
            nn.store(sp, PAIRS - 1, 1, g["at"](outv, 2 * PAIRS - 1))
            nn.finish(sp, PAIRS)

        @block.gpsimd
        def _(pool):
            def step(i):
                for s in two:
                    m = 2 * i + s
                    pool.wait_ge(x_in[s], 16 * (i + 1))
                    if first:
                        pool.wait_ge(a_in[s], 16 * (i + 1))
                        wait(pool, turned, m - 1)
                        nc.gpsimd.tensor_tensor(flat(gb[s]), flat(xb[s]), flat(ab[s]), ALU.add
                                                ).then_inc(g_ready, 1)
                        wait(pool, nn.u_ready, m - 1)
                        nc.gpsimd.tensor_tensor(
                            vb[s][:, :, :], xb[s][:, :, :],
                            per_node(g["deg1"], i, s).unsqueeze(2).to_broadcast([P, J, D]), ALU.mult
                            ).then_inc(v_ready, 1)
                    else:
                        wait(pool, nn.u_ready, m - 1)
                        nc.gpsimd.tensor_tensor(vb[s][:, :, :], xb[s][:, :, :],
                                                g["bL2_all"][:, :].unsqueeze(1).to_broadcast([P, J, D]), ALU.add
                                                ).then_inc(v_ready, 1)
            loop_pairs(pool, PAIRS, step)

        @block.tensor
        def _(pe):
            def turn(i, s):
                m = 2 * i + s
                if first:
                    pe.wait_ge(g_ready, m + 1)
                else:
                    pe.wait_ge(a_in[s], 16 * (i + 1))
                wait(pe, gT_ready, m - 1)
                for j in range(J):
                    last = nc.tensor.transpose(p_g[s][:, j * P:(j + 1) * P], gb[s][:, j, :], g["ident"][:, :])
                last.then_inc(turned, 1)

            def step(i):
                for s in two:
                    m = 2 * i + s
                    if ahead(PAIRS, i, s):
                        turn(*ahead(PAIRS, i, s))
                    pe.wait_ge(gT_ready, m + 1)
                    wait(pe, nn.u_ready, m - 1)
                    for j in range(J):
                        last = nc.tensor.matmul(p_o[s][:, j * D:(j + 1) * D], gT[s][:, j * P:(j + 1) * P], WT[:, :],
                                                start=True, stop=True)
                    last.then_inc(o_ready, 1)
            turn(0, 0)
            loop_pairs(pe, PAIRS, step)

        @block.scalar
        def _(act):
            def evacuate(i, s):
                m = 2 * i + s
                act.wait_ge(turned, m + 1)
                wait(act, o_ready, m - 1)
                nc.scalar.copy(gT[s][:, :], p_g[s][:, :]).then_inc(gT_ready, 1)

            def step(i):
                for s in two:
                    if ahead(PAIRS, i, s):
                        evacuate(*ahead(PAIRS, i, s))
                    nn.root(act, i, s)
            evacuate(0, 0)
            loop_pairs(act, PAIRS, step)

        @block.vector
        def _(dve):
            ch = Chain(dve, nn.step)

            def step(i):
                for s in two:
                    m = 2 * i + s
                    dve.wait_ge(v_ready, m + 1)
                    dve.wait_ge(o_ready, m + 1)
                    wait(dve, nn.y_ready, m - 1)
                    nc.vector.tensor_tensor(flat(nn.u[s]), p_o[s][:, :], flat(vb[s]), ALU.add
                                            ).then_inc(nn.u_ready, 1)
                    nn.statistics(dve, ch, i, s, scale2=per_node(g["norm2"], i, s) if first else None)
                    if behind(i, s):
                        b = behind(i, s)
                        nn.apply(dve, ch, *b, scale=per_node(g["norm"], *b) if first else None)
            loop_pairs(dve, PAIRS, step, ch, 18 if first else 14)
            nn.apply(dve, ch, PAIRS - 1, 1, scale=per_node(g["norm"], PAIRS - 1, 1) if first else None)


def attention(nc, g):
    GROUPS, EPAIRS = g["GROUPS"], g["EPAIRS"]
    keys, index, ident, x3_t, state_t, WT = (g[n] for n in ("keys", "index", "ident", "x3_t", "state_t", "WLT"))
    WT = WT[2]
    SUMS = D + HEADS
    SCALE = HD ** -0.5
    with Scope(nc, "attn") as sc:
        two = range(2)
        gi = [sc.sb(f"gi{s}", [P, 4], I32) for s in two]
        oi = [sc.sb(f"oi{s}", [P, 4], I32) for s in two]
        keyb = [sc.sb(f"keyb{s}", [P, 2, P]) for s in two]
        eq = [sc.sb(f"eq{s}", [P, 2, GROUP]) for s in two]
        below = sc.sb("below", [P, 2, GROUP])
        ends = [sc.sb(f"ends{s}", [P, 4, D]) for s in two]
        endsT = [sc.sb(f"endsT{s}", [P, 4 * P]) for s in two]
        ft = [sc.sb(f"ft{s}", [P, 4, D]) for s in two]
        prod = sc.sb("prod", [P, 2, D])
        logit = [sc.sb(f"logit{s}", [P, 2, HEADS]) for s in two]
        shifted = sc.sb("shifted", [P, HEADS, GROUP])
        peak = [sc.sb(f"peak{s}", [P, 2, HEADS]) for s in two]
        gap = [sc.sb(f"gap{s}", [P, 2, HEADS]) for s in two]
        weight = [sc.sb(f"weight{s}", [P, 2, HEADS]) for s in two]
        terms = [sc.sb(f"terms{s}", [P, 2, SUMS]) for s in two]
        old = [sc.sb(f"old{s}", [P, 2, STATE]) for s in two]
        new = [sc.sb(f"new{s}", [P, 2, STATE]) for s in two]
        drop = [sc.sb(f"drop{s}", [P, 2, 2, HEADS]) for s in two]
        keep = [sc.sb(f"keep{s}", [P, 2, 2, HEADS]) for s in two]
        part = sc.sb("part", [P, 2, SUMS])
        p_keys = sc.ps("p_keys", [P, 512])
        p_endsT = sc.ps("p_endsT", [P, 512])
        p_ft = sc.ps("p_ft", [P, 512])
        p_logit = sc.ps("p_logit", [P, HEADS, GROUP])
        p_sums = [sc.ps(f"p_sums{s}", [P, 512]) for s in two]
        arrived = [sc.sem(f"arrived{s}") for s in two]
        state_in = [sc.sem(f"state_in{s}") for s in two]
        state_out = sc.sem("state_out")
        names = ("gi_ready", "oi_ready", "keyb_ready", "rows_ready", "eq_ready", "turned", "endsT_ready", "ft_psum",
                 "ft_ready", "logit_ready", "logit_rows", "peak_ready", "weight_ready", "terms_ready", "summed",
                 "drop_ready", "keep_ready", "new_ready", "shift_used", "dve_step", "gap_ready")
        S = {n: sc.sem(n) for n in names}
        block = sc.block()

        def heads(ap):
            return ap.rearrange("p c (h f) -> p c h f", h=HEADS)

        @block.gpsimd
        def _(pool):
            gathers, scatters = Turns(pool, sc.tag + "_gathers"), Turns(pool, sc.tag + "_scatters")
            states = Turns(pool, sc.tag + "_states")

            def gather(i, s):
                t = 2 * i + s
                wait(pool, S["turned"], t - 1)
                gathers.wait(S["gi_ready"], t)
                for c in range(4):
                    pool.indirect_dma_start(ends[s][:, c, :], None, x3_t,
                                            bass.IndirectOffsetOnAxis(ap=gi[s][:, c:c + 1], axis=0)
                                            ).then_inc(arrived[s], 16)

            def step(i):
                for s in two:
                    t = 2 * i + s
                    wait(pool, state_out, 32 * t)
                    wait(pool, S["new_ready"], t - 1)
                    states.wait(S["oi_ready"], t)
                    for c in two:
                        pool.indirect_dma_start(old[s][:, c, :], None, state_t,
                                                bass.IndirectOffsetOnAxis(ap=oi[s][:, c:c + 1], axis=0)
                                                ).then_inc(state_in[s], 16)
                    if ahead(EPAIRS, i, s):
                        gather(*ahead(EPAIRS, i, s))
                    scatters.wait(S["new_ready"], t)
                    for c in two:
                        pool.indirect_dma_start(state_t, bass.IndirectOffsetOnAxis(ap=oi[s][:, 2 + c:3 + c], axis=0),
                                                new[s][:, c, :], None).then_inc(state_out, 16)
            gather(0, 0)
            loop_pairs(pool, EPAIRS, step)
            pool.wait_ge(state_out, 32 * GROUPS)

        @block.tensor
        def _(pe):
            def front(i, s):
                t = 2 * i + s
                pe.wait_ge(S["keyb_ready"], t + 1)
                wait(pe, S["eq_ready"], t)
                for c in two:
                    last = nc.tensor.matmul(p_keys[:, c * P:(c + 1) * P], keyb[s][:, c, :], ident[:, :],
                                            start=True, stop=True)
                last.then_inc(S["rows_ready"], 1)
                pe.wait_ge(arrived[s], 64 * (i + 1))
                wait(pe, S["endsT_ready"], t)
                for c in range(4):
                    last = nc.tensor.transpose(p_endsT[:, c * P:(c + 1) * P], ends[s][:, c, :], ident[:, :])
                last.then_inc(S["turned"], 1)
                pe.wait_ge(S["endsT_ready"], t + 1)
                wait(pe, S["ft_ready"], t)
                for c in range(4):
                    last = nc.tensor.matmul(p_ft[:, c * D:(c + 1) * D], endsT[s][:, c * P:(c + 1) * P], WT[:, :],
                                            start=True, stop=True)
                last.then_inc(S["ft_psum"], 1)

            def middle(i, s):
                t = 2 * i + s
                pe.wait_ge(S["logit_ready"], t + 1)
                wait(pe, S["peak_ready"], t)
                for h in range(HEADS):
                    for c in two:
                        last = nc.tensor.matmul(p_logit[:, h, c * P:(c + 1) * P],
                                                logit[s][:, c, h:h + 1].to_broadcast([P, P]), ident[:, :],
                                                start=True, stop=True)
                last.then_inc(S["logit_rows"], 1)

            def back(i, s):
                t = 2 * i + s
                pe.wait_ge(S["terms_ready"], t + 1)
                wait(pe, S["new_ready"], t - 1)
                for c in two:
                    for k in two:
                        last = nc.tensor.matmul(p_sums[s][:, c * SUMS:(c + 1) * SUMS],
                                                eq[s][:, k, c * P:(c + 1) * P], terms[s][:, k, :],
                                                start=(k == 0), stop=(k == 1))
                last.then_inc(S["summed"], 1)

            def step(i):
                for s in two:
                    middle(i, s)
                    back(i, s)
                    if ahead(EPAIRS, i, s):
                        front(*ahead(EPAIRS, i, s))
            front(0, 0)
            loop_pairs(pe, EPAIRS, step)

        @block.scalar
        def _(act):
            def front(i, s):
                t = 2 * i + s
                act.wait_ge(S["turned"], t + 1)
                wait(act, S["ft_psum"], t - 1)
                nc.scalar.copy(endsT[s][:, :], p_endsT[:, :]).then_inc(S["endsT_ready"], 1)
                act.wait_ge(S["ft_psum"], t + 1)
                wait(act, S["terms_ready"], t - 1)
                nc.scalar.copy(flat(ft[s]), p_ft[:, :]).then_inc(S["ft_ready"], 1)

            def step(i):
                for s in two:
                    t = 2 * i + s
                    act.wait_ge(S["gap_ready"], t + 1)
                    wait(act, S["terms_ready"], t - 1)
                    nc.scalar.activation(weight[s][:, :, :], gap[s][:, :, :], ACT.Exp).then_inc(S["weight_ready"], 1)
                    act.wait_ge(S["drop_ready"], t + 1)
                    wait(act, S["new_ready"], t - 1)
                    nc.scalar.activation(keep[s][:, :, :, :], drop[s][:, :, :, :], ACT.Exp
                                         ).then_inc(S["keep_ready"], 1)
                    if ahead(EPAIRS, i, s):
                        front(*ahead(EPAIRS, i, s))
            front(0, 0)
            loop_pairs(act, EPAIRS, step)

        @block.vector
        def _(dve):
            ch = Chain(dve, S["dve_step"])

            def indices(i, s):
                t = 2 * i + s
                wait(dve, arrived[s], 64 * i)
                nc.vector.tensor_scalar(gi[s][:, :].rearrange("p (k c) -> p k c", c=2),
                                      index[:, bass.ds(t, 1), 1:3, :].rearrange("p a k c -> p (a k) c"), 1.0, None, ALU.mult
                                      ).then_inc(S["gi_ready"], 1)
                wait(dve, S["eq_ready"], t - 1)
                nc.vector.tensor_copy(keyb[s][:, :, :],
                                      keys[:, bass.ds(2 * t, 2)].unsqueeze(2).to_broadcast([P, 2, P])
                                      ).then_inc(S["keyb_ready"], 1)

            def state_indices(i, s):
                t = 2 * i + s
                wait(dve, state_out, 32 * (t - 1))
                nc.vector.tensor_scalar(oi[s][:, :].rearrange("p (k c) -> p k c", c=2),
                                      index[:, bass.ds(t, 1), 1:4:2, :].rearrange("p a k c -> p (a k) c"), 1.0, None, ALU.mult
                                      ).then_inc(S["oi_ready"], 1)

            def front(i, s):
                t = 2 * i + s
                dve.wait_ge(S["rows_ready"], t + 1)
                wait(dve, S["summed"], t - 1)
                for c in two:
                    last = nc.vector.tensor_scalar(eq[s][:, c, :], p_keys[:, 0:GROUP], keyb[s][:, c, 0:1], None,
                                                   ALU.is_equal)
                last.then_inc(S["eq_ready"], 1)
                dve.wait_ge(S["ft_ready"], t + 1)
                ch.mark(nc.vector.tensor_tensor(prod[:, :, :], ft[s][:, 0:2, :], ft[s][:, 2:4, :], ALU.mult))
                ch.sync()
                dve.wait_ge(S["eq_ready"], t + 1)
                ch.mark(nc.vector.tensor_reduce(logit[s][:, :, :], heads(prod[:, :, :]), AXX, ALU.add))
                ch.mark(nc.vector.tensor_scalar(below[:, :, :], eq[s][:, :, :], 1.0, -LOWEST, ALU.subtract, ALU.mult))
                ch.sync()
                nc.vector.tensor_scalar(logit[s][:, :, :], logit[s][:, :, :], SCALE, None, ALU.mult
                                        ).then_inc(S["logit_ready"], 1)
                dve.wait_ge(S["logit_ready"], t + 1)
                dve.wait_ge(S["logit_rows"], t + 1)
                for c in two:
                    ch.mark(nc.vector.tensor_tensor(shifted[:, :, :], p_logit[:, :, :],
                                                    below[:, c, :].unsqueeze(1).to_broadcast([P, HEADS, GROUP]),
                                                    ALU.add))
                    ch.sync()
                    if c == 0:
                        ch.mark(nc.vector.tensor_reduce(peak[s][:, c, :], shifted[:, :, :], AXX, ALU.max))
                        ch.sync()
                    else:
                        nc.vector.tensor_reduce(peak[s][:, c, :], shifted[:, :, :], AXX, ALU.max
                                                ).then_inc(S["peak_ready"], 1)
                dve.wait_ge(S["peak_ready"], t + 1)
                nc.vector.tensor_tensor(gap[s][:, :, :], logit[s][:, :, :], peak[s][:, :, :], ALU.subtract
                                        ).then_inc(S["gap_ready"], 1)
                dve.wait_ge(S["weight_ready"], t + 1)
                nc.vector.tensor_copy(terms[s][:, :, D:SUMS], weight[s][:, :, :])
                nc.vector.tensor_tensor(heads(terms[s][:, :, 0:D]), heads(ft[s][:, 2:4, :]),
                                        weight[s][:, :, :].unsqueeze(3).to_broadcast([P, 2, HEADS, HD]), ALU.mult
                                        ).then_inc(S["terms_ready"], 1)

            def join(i, s):
                t = 2 * i + s
                dve.wait_ge(state_in[s], 32 * (i + 1))
                new_max = new[s][:, :, SUMS:STATE]
                ch.mark(nc.vector.tensor_tensor(new_max, old[s][:, :, SUMS:STATE], peak[s][:, :, :], ALU.max))
                ch.sync()
                ch.mark(nc.vector.tensor_tensor(drop[s][:, 0, :, :], old[s][:, :, SUMS:STATE], new_max, ALU.subtract))
                nc.vector.tensor_tensor(drop[s][:, 1, :, :], peak[s][:, :, :], new_max, ALU.subtract
                                        ).then_inc(S["drop_ready"], 1)
                dve.wait_ge(S["keep_ready"], t + 1)
                dve.wait_ge(S["summed"], t + 1)
                p_s = p_sums[s][:, 0:2 * SUMS].rearrange("p (c f) -> p c f", c=2)

                def kept(k):
                    return keep[s][:, k, :, :]
                ch.mark(nc.vector.tensor_tensor(heads(new[s][:, :, 0:D]), heads(old[s][:, :, 0:D]),
                                                kept(0).unsqueeze(3).to_broadcast([P, 2, HEADS, HD]), ALU.mult))
                ch.mark(nc.vector.tensor_tensor(new[s][:, :, D:SUMS], old[s][:, :, D:SUMS], kept(0), ALU.mult))
                ch.mark(nc.vector.tensor_tensor(heads(part[:, :, 0:D]), heads(p_s[:, :, 0:D]),
                                                kept(1).unsqueeze(3).to_broadcast([P, 2, HEADS, HD]), ALU.mult))
                ch.mark(nc.vector.tensor_tensor(part[:, :, D:SUMS], p_s[:, :, D:SUMS], kept(1), ALU.mult))
                ch.sync()
                nc.vector.tensor_tensor(new[s][:, :, 0:SUMS], new[s][:, :, 0:SUMS], part[:, :, :], ALU.add
                                        ).then_inc(S["new_ready"], 1)
                dve.wait_ge(S["new_ready"], t + 1)

            def step(i):
                for s in two:
                    if ahead(EPAIRS, i, s):
                        indices(*ahead(EPAIRS, i, s))
                        state_indices(*ahead(EPAIRS, i, s))
                    front(i, s)
                    join(i, s)
            indices(0, 0)
            state_indices(0, 0)
            loop_pairs(dve, EPAIRS, step, ch, 24)


def last_layer_out(nc, g):
    PAIRS = g["PAIRS"]
    with Scope(nc, "out4") as sc:
        two = range(2)
        xb = [sc.sb(f"xb{s}", [P, J, D]) for s in two]
        sb_ = [sc.sb(f"state{s}", [P, J, STATE]) for s in two]
        mean_ft = [sc.sb(f"mean_ft{s}", [P, J, D]) for s in two]
        den = sc.sb("den", [P, J, HEADS])
        inv = [sc.sb(f"inv{s}", [P, J, HEADS]) for s in two]
        nn = NodeNorm(nc, sc, g)
        x_in = [sc.sem(f"x_in{s}") for s in two]
        s_in = [sc.sem(f"s_in{s}") for s in two]
        inv_ready, mean_ready = sc.sem("inv_ready"), sc.sem("mean_ready")
        block = sc.block()
        xv, sv = g["chunked"](g["x3_t"]), g["chunked"](g["state_t"])

        @block.sync
        def _(sp):
            def load(i, s):
                m = 2 * i + s
                wait(sp, mean_ready, m - 1)
                sp.dma_start(flat(sb_[s]), g["at"](sv, m)).then_inc(s_in[s], 16)
                wait(sp, nn.u_ready, m - 1)
                sp.dma_start(flat(xb[s]), g["at"](xv, m)).then_inc(x_in[s], 16)

            def step(i):
                for s in two:
                    if ahead(PAIRS, i, s):
                        load(*ahead(PAIRS, i, s))
                    if behind(i, s):
                        b = behind(i, s)
                        nn.store(sp, *b, g["node_rows"](g["out"], 2 * b[0] + b[1], P))
            load(0, 0)
            loop_pairs(sp, PAIRS, step)
            nn.store(sp, PAIRS - 1, 1, g["node_rows"](g["out"], 2 * PAIRS - 1, g["TAIL_P"]))
            nn.finish(sp, PAIRS)

        @block.gpsimd
        def _(pool):
            def step(i):
                for s in two:
                    m = 2 * i + s
                    pool.wait_ge(inv_ready, m + 1)
                    wait(pool, nn.u_ready, m - 1)
                    nc.gpsimd.tensor_tensor(
                        mean_ft[s][:, :, :].rearrange("p j (h f) -> p j h f", h=HEADS),
                        sb_[s][:, :, 0:D].rearrange("p j (h f) -> p j h f", h=HEADS),
                        inv[s][:, :, :].unsqueeze(3).to_broadcast([P, J, HEADS, HD]), ALU.mult
                        ).then_inc(mean_ready, 1)
            loop_pairs(pool, PAIRS, step)

        @block.scalar
        def _(act):
            def step(i):
                for s in two:
                    nn.root(act, i, s)
            loop_pairs(act, PAIRS, step)

        @block.vector
        def _(dve):
            ch = Chain(dve, nn.step)

            def invert(i, s):
                m = 2 * i + s
                dve.wait_ge(s_in[s], 16 * (i + 1))
                d = sb_[s][:, :, D:D + HEADS]
                ch.mark(nc.vector.scalar_tensor_tensor(out=den[:, :, :], in0=d, scalar=0.0, in1=d,
                                                       op0=ALU.is_equal, op1=ALU.add))
                ch.sync()
                wait(dve, mean_ready, m - 1)
                nc.vector.reciprocal(inv[s][:, :, :], den[:, :, :]).then_inc(inv_ready, 1)
                dve.wait_ge(inv_ready, m + 1)

            def step(i):
                for s in two:
                    m = 2 * i + s
                    if ahead(PAIRS, i, s):
                        invert(*ahead(PAIRS, i, s))
                    else:
                        pass
                    dve.wait_ge(mean_ready, m + 1)
                    dve.wait_ge(x_in[s], 16 * (i + 1))
                    wait(dve, nn.y_ready, m - 1)
                    nc.vector.scalar_tensor_tensor(out=flat(nn.u[s]), in0=flat(xb[s]), scalar=2.0,
                                                   in1=flat(mean_ft[s]), op0=ALU.mult, op1=ALU.add
                                                   ).then_inc(nn.u_ready, 1)
                    nn.statistics(dve, ch, i, s)
                    if behind(i, s):
                        nn.apply(dve, ch, *behind(i, s))
            invert(0, 0)
            loop_pairs(dve, PAIRS, step, ch, 16)
            nn.apply(dve, ch, PAIRS - 1, 1)


_INS = ['x', 'src', 'dst', 'edge_attr_64', 'L0_gnn_We', 'L0_gnn_be', 'L0_gnn_W1', 'L0_gnn_b1', 'L0_gnn_g1',
        'L0_gnn_beta1', 'L0_gnn_W2', 'L0_gnn_b2', 'L0_gnn_g2', 'L0_gnn_beta2', 'L0_gnn_eps', 'L1_gnn_W',
        'L2_gnn_W', 'L2_gnn_b', 'L3_gnn_W']


def kernel(**inputs):
    import numpy as _np
    import concourse.bacc as _bacc
    from concourse import mybir as _mybir
    from concourse.bass_utils import run_bass_kernel_spmd as _run

    nc = _bacc.Bacc("TRN2", target_bir_lowering=False, num_devices=1)
    arrays, args = {}, []
    for name in _INS:
        a = _np.ascontiguousarray(inputs[name])
        if name == 'L0_gnn_eps':
            a = a.reshape(1)
        arrays[f"in_{name}_dram"] = a
        args.append(nc.dram_tensor(f"in_{name}_dram", a.shape, _mybir.dt.from_np(a.dtype), kind="ExternalInput").ap())
    args.append(nc.dram_tensor("out_0_dram", tuple(inputs['x'].shape), _mybir.dt.float32, kind="ExternalOutput").ap())
    gnn_kernel(nc, *args)
    r = _run(nc, [arrays], core_ids=[0])
    return r.results[0]["out_0_dram"]
```

```python
import concourse.bass as bass
from concourse import mybir
from contextlib import ExitStack

FP32 = mybir.dt.float32
BF16 = mybir.dt.bfloat16
I32 = mybir.dt.int32
ALU = mybir.AluOpType
ACT = mybir.ActivationFunctionType
AXX = mybir.AxisListType.X

P = 128
D = 128
J = 8
CHUNK = P * J
W = J * D
HALF = W // 2
GROUP = 2 * P
HEADS = 4
HD = D // HEADS
HS = HD + 1
SUMS = HEADS * HS
STATE = SUMS + HEADS
EPS = 1e-5
LOWEST = -3.0e38
ACT_ROWS = 4


def wait(eng, sem, value):
    if isinstance(value, int) and value <= 0:
        return
    eng.wait_ge(sem, value)


class Chain:

    def __init__(self, eng, sem):
        self.eng, self.sem, self.base, self.k = eng, sem, 0, 0

    def mark(self, ins):
        self.k += 1
        ins.then_inc(self.sem, 1)
        return self.base + self.k

    def after(self, ticket):
        self.eng.wait_ge(self.sem, ticket)

    def sync(self):
        self.eng.wait_ge(self.sem, self.base + self.k)

    def enter(self, i, start, per):
        self.fixed = self.base + self.k
        self.base, self.k, self.start, self.per = i * per + (self.fixed - start * per), 0, start, per

    def leave(self, count):
        assert self.k == self.per, f"this loop's body marks {self.k}"
        self.base, self.k = self.fixed + count * self.per, 0


def loop_pairs(eng, pairs, body, chain=None, per=0):
    body(0)
    with eng.Fori(1, pairs - 1) as i:
        if chain:
            chain.enter(i, 1, per)
        body(i)
    if chain:
        chain.leave(pairs - 2)
    body(pairs - 1)


def gnn_kernel(nc, x, src, dst, edge_attr, We, be, W1, b1, g1, beta1, W2, b2, g2, beta2, eps,
               WL1, WL2, bL2, WL3, out):
    N = x.shape[0]
    E = src.shape[0]
    DE = edge_attr.shape[1]
    CHUNKS = -(-N // CHUNK)
    TAIL_P = (N - (CHUNKS - 1) * CHUNK) // J
    PAIRS = CHUNKS // 2
    NPAD = CHUNKS * CHUNK
    EDGE_COLS = -(-E // (4 * P)) * 4
    FULL_P = E // EDGE_COLS
    REM = E - FULL_P * EDGE_COLS
    GROUPS = EDGE_COLS // 2
    EPAIRS = GROUPS // 2
    NCOLS = CHUNKS * J
    assert CHUNKS % 2 == 0 and (N - (CHUNKS - 1) * CHUNK) % J == 0 and N + GROUP < NPAD
    assert PAIRS > 2 and EPAIRS > 2

    ctx = ExitStack()

    def sb(name, shape, dt=FP32):
        return ctx.enter_context(nc.sbuf_tensor(name, shape, dt))

    def dram(name, cols):
        return nc.dram_tensor(name, (NPAD, cols), FP32, kind="Internal").ap()

    h_t, agg1, agg2 = dram("h", D), dram("agg1", D), dram("agg2", D)
    z2_t = nc.dram_tensor("z2_t", (CHUNKS, P, W), FP32, kind="Internal").ap()
    x1n_t, x2_t, x3_t = dram("x1n", D), dram("x2", D), dram("x3", D)
    state_t = dram("state", STATE)

    def chunked(table, rows=P):
        return table.rearrange("(m p j) f -> m p (j f)", p=P, j=J)

    def at(view, m, rows=P):
        if isinstance(m, int):
            return view[m, 0:rows, :]
        return view[bass.ds(m, 1), 0:rows, :].rearrange("a p f -> (a p) f")

    def node_rows(table, m, rows=P):
        if isinstance(m, int):
            v = table[m * CHUNK:m * CHUNK + rows * J, :]
            return v.rearrange("(p j) f -> p (j f)", j=J)
        body = table[0:(CHUNKS - 1) * CHUNK, :].rearrange("(m p j) f -> m p (j f)", p=P, j=J)
        return body[bass.ds(m, 1), :, :].rearrange("a p f -> (a p) f")

    def rows_of(m):
        return TAIL_P if isinstance(m, int) and m == CHUNKS - 1 else P

    with ctx:
        ident = sb("ident", [P, P])
        ones_col = sb("ones_col", [P, 1])
        eps_col = sb("eps_col", [P, 1])
        gin_scale = sb("gin_scale", [P, 1])
        WeT = sb("WeT", [DE + 1, D])
        W1T = sb("W1T", [P, 2 * D])
        W2T = sb("W2T", [P, 2, D])
        WLT = [sb(f"WLT{n}", [P, D]) for n in range(3)]
        b1c, g1c, beta1c = (sb(n, [P, 2]) for n in ("b1c", "g1c", "beta1c"))
        b2c, g2c, beta2c = (sb(n, [P, 1]) for n in ("b2c", "g2c", "beta2c"))
        bL2_all = sb("bL2_all", [P, D])
        keys = sb("keys", [P, 2 * EDGE_COLS])
        index = sb("index", [P, GROUPS, 4, 2], I32)
        lo_digit = sb("lo_digit", [P, EDGE_COLS])
        hi_digit = sb("hi_digit", [P, EDGE_COLS])
        deg1 = sb("deg1", [P, NCOLS])
        norm = sb("norm", [P, NCOLS])
        norm2 = sb("norm2", [P, NCOLS])
        a1, t1 = sb("a1", [P, 2]), sb("t1", [P, 2])
        a2, t2 = sb("a2", [P, 1]), sb("t2", [P, 1])
        moments = sb("moments", [P, D + 1])

        prepare(nc, locals())
        degrees_and_first_sum(nc, locals())
        first_norm(nc, locals())
        mlp(nc, locals())
        first_layer_out(nc, locals())
        aggregate(nc, locals(), "l1", x1n_t, agg1, EDGE_COLS, 1, 0)
        convolve(nc, locals(), "l1", x1n_t, agg1, x2_t, WLT[0])
        aggregate(nc, locals(), "l2", x2_t, agg2, 0, 2, 3)
        convolve(nc, locals(), "l2", x2_t, agg2, x3_t, WLT[1])
        attention(nc, locals())
        last_layer_out(nc, locals())


class Turns:

    def __init__(self, eng, name):
        self.eng = eng
        self.count = eng.alloc_register(name)
        eng.reg_mov(self.count, 1)

    def wait(self, sem, t):
        self.eng.wait_ge(sem, t + 1 if isinstance(t, int) else self.count)
        self.eng.reg_add(self.count, self.count, 1)


class Scope:

    def __init__(self, nc, tag):
        self.nc, self.tag, self.ctx, self.sems = nc, tag, ExitStack(), []

    def __enter__(self):
        self.ctx.__enter__()
        return self

    def __exit__(self, *e):
        self.ctx.__exit__(*e)
        self.nc.clear_and_free_semaphores(self.sems)
        self.nc.all_engine_barrier()

    def sb(self, name, shape, dt=FP32):
        return self.ctx.enter_context(self.nc.sbuf_tensor(f"{self.tag}_{name}", shape, dt))

    def ps(self, name, shape, dt=FP32):
        return self.ctx.enter_context(self.nc.psum_tensor(f"{self.tag}_{name}", shape, dt))

    def sem(self, name):
        self.sems.append(self.nc.alloc_semaphore(f"{self.tag}_{name}"))
        return self.sems[-1]

    def block(self):
        return self.ctx.enter_context(self.nc.Block())


def prepare(nc, g):
    N, E, DE = g["N"], g["E"], g["DE"]
    EC, GROUPS, FULL_P, REM, CHUNKS = g["EDGE_COLS"], g["GROUPS"], g["FULL_P"], g["REM"], g["CHUNKS"]
    keys, index, ident = g["keys"], g["index"], g["ident"]
    with Scope(nc, "prep") as sc:
        w1 = sc.sb("w1", [P, 2, D])
        w2 = sc.sb("w2", [P, 2, D])
        we = sc.sb("we", [P, DE])
        wl = [sc.sb(f"wl{n}", [P, D]) for n in range(3)]
        xb = [sc.sb(f"xb{s}", [P, W]) for s in range(2)]
        hb = [sc.sb(f"hb{s}", [P, W]) for s in range(2)]
        raw = sc.sb("raw", [P, 2, EC], I32)
        no_edge = sc.sb("no_edge", [P, EC])
        later_mask = sc.sb("later_mask", [P, 2, GROUP])
        spare = sc.sb("spare", [P, 2 * GROUPS, 2])
        later = sc.sb("later", [P, 2 * EC])
        own = sc.sb("own", [P, 2 * EC])
        key_int = sc.sb("key_int", [P, 2, EC], I32)
        digit = sc.sb("digit", [P, 4, EC], I32)
        keyb = [sc.sb(f"keyb{s}", [P, 2, P]) for s in range(2)]
        mark = [sc.sb(f"mark{s}", [P, 2, GROUP]) for s in range(2)]
        wps = sc.ps("wps", [P, 8, 512])
        pwt = [wps[:, b, 0:P] for b in range(6)]
        key_rows = [wps[:, 6 + s, 0:GROUP] for s in range(2)]
        params_in, edges_in, h_ready, scale_ready = (
            sc.sem(n) for n in ("params_in", "edges_in", "h_ready", "scale_ready"))
        x_in = [sc.sem(f"x_in{s}") for s in range(2)]
        stored = [sc.sem(f"stored{s}") for s in range(2)]
        raw_ready, consts_ready, pool_step = (sc.sem(n) for n in ("raw_ready", "consts_ready", "pool_step"))
        dve_step, wt_ready, keyb_ready, rows_ready, marked = (
            sc.sem(n) for n in ("dve_step", "wt_ready", "keyb_ready", "rows_ready", "marked"))
        block = sc.block()
        NPARAM = 16

        @block.sync
        def _(sp):
            with nc.allow_non_contiguous_dma(reason="parameter vectors as columns"):
                sp.dma_start(w1[:, :, :], g["W1"].rearrange("(b p) f -> p b f", p=P)).then_inc(params_in, 16)
                sp.dma_start(w2[:, :, :], g["W2"].rearrange("p (b f) -> p b f", b=2)).then_inc(params_in, 16)
                sp.dma_start(we[:, :], g["We"]).then_inc(params_in, 16)
                for n, name in enumerate(("WL1", "WL2", "WL3")):
                    sp.dma_start(wl[n][:, :], g[name]).then_inc(params_in, 16)
                sp.dma_start(g["WeT"][DE:DE + 1, :], g["be"][None, :]).then_inc(params_in, 16)
                for col, vec in (("b1c", "b1"), ("g1c", "g1"), ("beta1c", "beta1")):
                    sp.dma_start(g[col][:, :], g[vec].rearrange("(b p) -> p b", p=P)).then_inc(params_in, 16)
                for col, vec in (("b2c", "b2"), ("g2c", "g2"), ("beta2c", "beta2")):
                    sp.dma_start(g[col][:, :], g[vec].rearrange("(p b) -> p b", b=1)).then_inc(params_in, 16)
                sp.dma_start(g["bL2_all"][:, :], g["bL2"][None, :].to_broadcast([P, D])).then_inc(params_in, 16)
                sp.dma_start(g["gin_scale"][:, :], g["eps"][None, :].to_broadcast([P, 1])).then_inc(params_in, 16)
                sp.wait_ge(raw_ready, 1)
                for n, name in enumerate(("dst", "src")):
                    v = g[name]
                    sp.dma_start(raw[0:FULL_P, n, :],
                                 v[0:FULL_P * EC].rearrange("(p k) -> p k", k=EC)).then_inc(edges_in, 16)
                    sp.dma_start(raw[FULL_P:FULL_P + 1, n, 0:REM],
                                 v[FULL_P * EC:E][None, :]).then_inc(edges_in, 16)
            def load(i):
                for s in range(2):
                    m = 2 * i + s
                    r = g["rows_of"](m)
                    wait(sp, h_ready, m - 1)
                    sp.dma_start(xb[s][0:r, :], g["node_rows"](g["x"], m, r)).then_inc(x_in[s], 16)
            loop_pairs(sp, g["PAIRS"], load)

        @block.scalar
        def _(act):
            h_v = g["chunked"](g["h_t"])
            act.wait_ge(scale_ready, 1)

            def scale(i):
                for s in range(2):
                    m = 2 * i + s
                    act.wait_ge(x_in[s], 16 * (i + 1))
                    wait(act, stored[s], 16 * i)
                    nc.scalar.mul(hb[s][:, :], xb[s][:, :], g["gin_scale"][:, 0:1]).then_inc(h_ready, 1)
                    act.wait_ge(h_ready, m + 1)
                    act.dma_start(g["at"](h_v, m), hb[s][:, :]).then_inc(stored[s], 16)
            loop_pairs(act, g["PAIRS"], scale)
            for s in range(2):
                act.wait_ge(stored[s], 16 * g["PAIRS"])

        @block.gpsimd
        def _(pool):
            nc.gpsimd.memset(raw[:, :, :], 0).then_inc(raw_ready, 1)
            nc.gpsimd.memset(g["ones_col"][:, :], 1.0)
            nc.gpsimd.memset(g["eps_col"][:, :], EPS)
            nc.gpsimd.memset(ident[:, :], 1.0)
            nc.gpsimd.memset(later_mask[:, :, :], 1.0)
            nc.gpsimd.memset(no_edge[:, :], float(N)).then_inc(pool_step, 1)
            pool.wait_ge(pool_step, 1)
            nc.gpsimd.affine_select(out=ident[:, :], in_=ident[:, :], compare_op=ALU.is_equal, fill=0.0,
                                    base=0, pattern=[[-1, P]], channel_multiplier=1)
            nc.gpsimd.affine_select(out=later_mask[:, :, :], in_=later_mask[:, :, :], compare_op=ALU.is_gt,
                                    fill=0.0, base=0, pattern=[[-P, 2], [1, GROUP]], channel_multiplier=-1)
            nc.gpsimd.affine_select(out=no_edge[:, :], in_=no_edge[:, :], compare_op=ALU.is_ge, fill=0.0,
                                    base=-E, pattern=[[1, EC]], channel_multiplier=EC)
            nc.gpsimd.iota(spare[:, :, :], pattern=[[0, 2 * GROUPS], [P, 2]], base=N + 1, channel_multiplier=1,
                           allow_small_or_imprecise_dtypes=True).then_inc(consts_ready, 1)

        @block.tensor
        def _(pe):
            pe.wait_ge(consts_ready, 1)
            pe.wait_ge(params_in, 16 * (NPARAM - 1))
            wide = [w1[:, 0, :], w1[:, 1, :], w2[:, 0, :], w2[:, 1, :]]
            for b, w in enumerate(wide):
                last = nc.tensor.transpose(pwt[b], w, ident[:, :])
            for n in range(2):
                last = nc.tensor.transpose(pwt[4 + n], wl[n][:, :], ident[:, :])
            last = nc.tensor.transpose(wps[:, 4, P:2 * P], wl[2][:, :], ident[:, :])
            last = nc.tensor.transpose(wps[0:DE, 5, P:2 * P], we[:, :], ident[:, :])
            last.then_inc(wt_ready, 1)
            def rows(i):
                for s in range(2):
                    q = 2 * i + s
                    pe.wait_ge(keyb_ready, q + 1)
                    wait(pe, marked, q - 1)
                    for c in range(2):
                        last = nc.tensor.matmul(key_rows[s][:, c * P:(c + 1) * P], keyb[s][:, c, :],
                                                ident[:, :], start=True, stop=True)
                    last.then_inc(rows_ready, 1)
            loop_pairs(pe, GROUPS, rows)

        @block.vector
        def _(dve):
            ch = Chain(dve, dve_step)
            dve.wait_ge(params_in, 16 * (NPARAM - 1))
            nc.vector.tensor_scalar(g["gin_scale"][:, :], g["gin_scale"][:, :], 1.0, None, ALU.add).then_inc(scale_ready, 1)
            dve.wait_ge(wt_ready, 1)
            nc.vector.tensor_copy(g["W1T"][:, 0:D], pwt[0])
            nc.vector.tensor_copy(g["W1T"][:, D:2 * D], pwt[1])
            nc.vector.tensor_copy(g["W2T"][:, 0, :], pwt[2])
            nc.vector.tensor_copy(g["W2T"][:, 1, :], pwt[3])
            nc.vector.tensor_copy(g["WLT"][0][:, :], pwt[4])
            nc.vector.tensor_copy(g["WLT"][1][:, :], pwt[5])
            nc.vector.tensor_copy(g["WLT"][2][:, :], wps[:, 4, P:2 * P])
            nc.vector.tensor_copy(g["WeT"][0:DE, :], wps[0:DE, 5, P:2 * P])
            dve.wait_ge(edges_in, 64)
            dve.wait_ge(consts_ready, 1)
            for n in range(2):
                ch.mark(nc.vector.tensor_copy(keys[:, n * EC:(n + 1) * EC], raw[:, n, :]))
            ch.sync()
            for n in range(2):
                ch.mark(nc.vector.tensor_tensor(keys[:, n * EC:(n + 1) * EC], keys[:, n * EC:(n + 1) * EC],
                                                no_edge[:, :], ALU.add))
            ch.sync()
            ch.mark(nc.vector.tensor_copy(key_int[:, 1, :], keys[:, EC:2 * EC]))
            ch.sync()
            src_int = key_int[:, 1, :]
            ch.mark(nc.vector.tensor_scalar(digit[:, 0, :], src_int, 3, P - 1, ALU.logical_shift_right,
                                            ALU.bitwise_and))
            ch.mark(nc.vector.tensor_scalar(digit[:, 1, :], src_int, 10, 3, ALU.logical_shift_right,
                                            ALU.logical_shift_left))
            ch.mark(nc.vector.tensor_scalar(digit[:, 2, :], src_int, J - 1, None, ALU.bitwise_and))
            ch.sync()
            ch.mark(nc.vector.tensor_copy(g["lo_digit"][:, :], digit[:, 0, :]))
            ch.mark(nc.vector.tensor_tensor(g["hi_digit"][:, :], digit[:, 1, :], digit[:, 2, :], ALU.add))

            def spread(q, s):
                wait(dve, marked, q - 1)
                nc.vector.tensor_scalar(keyb[s][:, :, :],
                                        keys[:, bass.ds(2 * q, 2)].unsqueeze(2).to_broadcast([P, 2, P]), 1.0, None,
                                        ALU.mult).then_inc(keyb_ready, 1)

            def count(i):
                for s in range(2):
                    q = 2 * i + s
                    if s == 0 or not (isinstance(i, int) and i == GROUPS - 1):
                        spread(q + 1, 1 - s)
                    dve.wait_ge(rows_ready, q + 1)
                    for c in range(2):
                        last = nc.vector.scalar_tensor_tensor(
                            out=mark[s][:, c, :], in0=key_rows[s], scalar=keyb[s][:, c, 0:1],
                            in1=later_mask[:, c, :], op0=ALU.is_equal, op1=ALU.mult,
                            accum_out=later[:, bass.ds(2 * q + c, 1)])
                    last.then_inc(marked, 1)
            spread(0, 0)
            loop_pairs(dve, GROUPS, count)
            dve.wait_ge(marked, 2 * GROUPS)
            spare_flat = spare[:, :, :].rearrange("p q c -> p (q c)")
            ch.mark(nc.vector.tensor_scalar(later[:, :], later[:, :], 1.0, None, ALU.min))
            ch.mark(nc.vector.tensor_tensor(own[:, :], spare_flat, keys[:, :], ALU.subtract))
            ch.sync()
            ch.mark(nc.vector.tensor_tensor(own[:, :], own[:, :], later[:, :], ALU.mult))
            ch.sync()
            ch.mark(nc.vector.tensor_tensor(own[:, :], own[:, :], keys[:, :], ALU.add))
            ch.sync()
            own_v = own[:, :].rearrange("p (n q c) -> p n q c", n=2, c=2)
            raw_v = raw[:, :, :].rearrange("p n (q c) -> p n q c", c=2)
            nc.vector.tensor_copy(index[:, :, 0, :], own_v[:, 1, :, :])
            nc.vector.tensor_copy(index[:, :, 1, :], raw_v[:, 0, :, :])
            nc.vector.tensor_copy(index[:, :, 2, :], raw_v[:, 1, :, :])
            nc.vector.tensor_copy(index[:, :, 3, :], own_v[:, 0, :, :])


def gathered(i, s, lag=0):
    return 32 * (i + 1 - lag)


def slot_step(i, s, ahead):
    return i + (s + ahead) // 2, (s + ahead) % 2


def degrees_and_first_sum(nc, g):
    DE, EC, GROUPS, EPAIRS = g["DE"], g["EDGE_COLS"], g["GROUPS"], g["EPAIRS"]
    FULL_P, REM, E, NCOLS = g["FULL_P"], g["REM"], g["E"], g["NCOLS"]
    keys, index, ident, x, h_t = g["keys"], g["index"], g["ident"], g["x"], g["h_t"]
    with Scope(nc, "l0") as sc:
        two = range(2)
        attr = sc.sb("attr", [P, EC, DE])
        columns = sc.sb("columns", [P, max(NCOLS, P)])
        gi = [sc.sb(f"gi{s}", [P, 2], I32) for s in two]
        oi = [sc.sb(f"oi{s}", [P, 2], I32) for s in two]
        keyb = [sc.sb(f"keyb{s}", [P, 2, P]) for s in two]
        eq = [sc.sb(f"eq{s}", [P, 2, GROUP]) for s in two]
        rows = [sc.sb(f"rows{s}", [P, 2, D]) for s in two]
        sums = [sc.sb(f"sums{s}", [P, 2, D]) for s in two]
        attr_now = [sc.sb(f"attr_now{s}", [P, 2 * DE + P - DE]) for s in two]
        attrT = [sc.sb(f"attrT{s}", [DE + 1, 2, P]) for s in two]
        msg = [sc.sb(f"msg{s}", [P, 2, D]) for s in two]
        hot_lo = [sc.sb(f"hot_lo{s}", [P, 2, P], BF16) for s in two]
        hot_hi = [sc.sb(f"hot_hi{s}", [P, 2, NCOLS], BF16) for s in two]
        p_keys = sc.ps("p_keys", [P, 512])
        p_attr = sc.ps("p_attr", [P, 512])
        p_sums = [sc.ps(f"p_sums{s}", [P, 512]) for s in two]
        p_msg = [sc.ps(f"p_msg{s}", [P, 512]) for s in two]
        p_deg = sc.ps("p_deg", [P, 2, 512])
        arrived = [sc.sem(f"arrived{s}") for s in two]
        attr_in, cols_ready, attr_zero, added = (sc.sem(n) for n in ("attr_in", "cols_ready", "attr_zero", "added"))
        gi_ready, oi_ready, keyb_ready, rows_ready, eq_ready = (
            sc.sem(n) for n in ("gi_ready", "oi_ready", "keyb_ready", "rows_ready", "eq_ready"))
        attr_now_ready, attrT_psum, attrT_ready, msg_psum, attrT_used, msg_ready = (
            sc.sem(n) for n in ("attr_now_ready", "attrT_psum", "attrT_ready", "msg_psum", "attrT_used", "msg_ready"))
        summed, sums_ready, hot_ready, hot_used, ones_ready, deg_ready, sq_ready = (
            sc.sem(n) for n in ("summed", "sums_ready", "hot_ready", "hot_used", "ones_ready", "deg_ready", "sq_ready"))
        block = sc.block()
        HI2 = NCOLS - 512 if NCOLS > 512 else 0

        def last_pair(i):
            return isinstance(i, int) and i == EPAIRS - 1

        @block.sync
        def _(sp):
            sp.wait_ge(attr_zero, 1)
            ea = g["edge_attr"]
            sp.dma_start(attr[0:FULL_P, :, :],
                         ea[0:FULL_P * EC, :].rearrange("(p k) f -> p k f", k=EC)).then_inc(attr_in, 16)
            sp.dma_start(attr[FULL_P:FULL_P + 1, 0:REM, :], ea[FULL_P * EC:E, :][None, :, :]).then_inc(attr_in, 16)

        @block.gpsimd
        def _(pool):
            nc.gpsimd.memset(attr[96:P, :, :], 0.0).then_inc(attr_zero, 1)
            pool.wait_ge(attr_zero, 1)
            nc.gpsimd.iota(columns[:, :], pattern=[[1, max(NCOLS, P)]], base=0, channel_multiplier=0,
                           allow_small_or_imprecise_dtypes=True).then_inc(cols_ready, 1)
            gathers, scatters = Turns(pool, sc.tag + "_gathers"), Turns(pool, sc.tag + "_scatters")

            def gather(i, s):
                t = 2 * i + s
                wait(pool, msg_psum, t - 1)
                gathers.wait(gi_ready, t)
                for c in two:
                    pool.indirect_dma_start(rows[s][:, c, :], None, x,
                                            bass.IndirectOffsetOnAxis(ap=gi[s][:, c:c + 1], axis=0)
                                            ).then_inc(arrived[s], 16)

            def step(i):
                for s in two:
                    t = 2 * i + s
                    if not (last_pair(i) and s == 1):
                        gather(*slot_step(i, s, 1))
                    pool.wait_ge(oi_ready, t + 1)
                    wait(pool, added, 32 * t)
                    scatters.wait(sums_ready, t)
                    for c in two:
                        pool.indirect_dma_start(h_t, bass.IndirectOffsetOnAxis(ap=oi[s][:, c:c + 1], axis=0),
                                                sums[s][:, c, :], None, compute_op=ALU.add).then_inc(added, 16)
            gather(0, 0)
            loop_pairs(pool, EPAIRS, step)
            pool.wait_ge(added, 32 * GROUPS)

        @block.tensor
        def _(pe):
            def front(i, s):
                t = 2 * i + s
                pe.wait_ge(keyb_ready, t + 1)
                wait(pe, eq_ready, t)
                for c in two:
                    last = nc.tensor.matmul(p_keys[:, c * P:(c + 1) * P], keyb[s][:, c, :], ident[:, :],
                                            start=True, stop=True)
                last.then_inc(rows_ready, 1)
                pe.wait_ge(attr_now_ready, t + 1)
                wait(pe, attrT_ready, t)
                for c in two:
                    last = nc.tensor.transpose(p_attr[:, c * P:(c + 1) * P], attr_now[s][:, c * DE:c * DE + P],
                                               ident[:, :])
                last.then_inc(attrT_psum, 1)
                pe.wait_ge(attrT_ready, t + 1)
                wait(pe, msg_ready, t - 1)
                for c in two:
                    last = nc.tensor.matmul(p_msg[s][:, c * D:(c + 1) * D], attrT[s][:, c, :], g["WeT"][:, :],
                                            start=(c == 0), stop=False, skip_group_check=True)
                last.then_inc(attrT_used, 1)

            def step(i):
                for s in two:
                    t = 2 * i + s
                    if not (last_pair(i) and s == 1):
                        front(*slot_step(i, s, 1))
                    pe.wait_ge(arrived[s], gathered(i, s))
                    last = nc.tensor.matmul(p_msg[s][:, 0:2 * D], ident[:, :], flat(rows[s]), start=False, stop=True,
                                            skip_group_check=True)
                    last.then_inc(msg_psum, 1)
                    pe.wait_ge(hot_ready, t + 1)
                    for c in two:
                        first, final = isinstance(i, int) and t == 0 and c == 0, last_pair(i) and s == 1 and c == 1
                        last = nc.tensor.matmul(p_deg[:, 0, 0:min(NCOLS, 512)], hot_lo[s][:, c, :],
                                                hot_hi[s][:, c, 0:min(NCOLS, 512)], start=first, stop=final)
                        if HI2:
                            last = nc.tensor.matmul(p_deg[:, 1, 0:HI2], hot_lo[s][:, c, :],
                                                    hot_hi[s][:, c, 512:NCOLS], start=first, stop=final)
                    last.then_inc(hot_used, 1)
                    pe.wait_ge(eq_ready, t + 1)
                    pe.wait_ge(msg_ready, t + 1)
                    wait(pe, sums_ready, t - 1)
                    for c in two:
                        for k in two:
                            last = nc.tensor.matmul(p_sums[s][:, c * D:(c + 1) * D], eq[s][:, k, c * P:(c + 1) * P],
                                                    msg[s][:, k, :], start=(k == 0), stop=(k == 1))
                    last.then_inc(summed, 1)
            pe.wait_ge(ones_ready, 1)
            front(0, 0)
            loop_pairs(pe, EPAIRS, step)

        @block.scalar
        def _(act):
            def front(i, s):
                t = 2 * i + s
                wait(act, attrT_psum, t - 1)
                nc.scalar.copy(attr_now[s][:, 0:2 * DE].rearrange("p (c f) -> p c f", c=2), attr[:, bass.ds(2 * t, 2), :]).then_inc(attr_now_ready, 1)
                act.wait_ge(attrT_psum, t + 1)
                wait(act, attrT_used, t - 1)
                nc.scalar.copy(attrT[s][0:DE, :, :].rearrange("p c e -> p (c e)"), p_attr[0:DE, 0:GROUP]
                               ).then_inc(attrT_ready, 1)

            def step(i):
                for s in two:
                    t = 2 * i + s
                    if not (last_pair(i) and s == 1):
                        front(*slot_step(i, s, 1))
                    act.wait_ge(msg_psum, t + 1)
                    wait(act, summed, t - 1)
                    nc.scalar.activation(flat(msg[s]), p_msg[s][:, 0:2 * D], ACT.Relu).then_inc(msg_ready, 1)
                    act.wait_ge(summed, t + 1)
                    wait(act, added, 32 * (t - 1))
                    nc.scalar.copy(sums[s][:, :, :].rearrange("p c f -> p (c f)"), p_sums[s][:, 0:2 * D]
                                   ).then_inc(sums_ready, 1)
            act.wait_ge(attr_in, 32)
            front(0, 0)
            loop_pairs(act, EPAIRS, step)
            act.wait_ge(deg_ready, 1)
            nc.scalar.activation(g["norm"][:, :], g["deg1"][:, :], ACT.Sqrt).then_inc(sq_ready, 1)

        @block.vector
        def _(dve):
            for s in two:
                nc.vector.memset(attr_now[s][:, 2 * DE:DE + P], 0.0)
                last = nc.vector.memset(attrT[s][DE:DE + 1, :, :], 1.0)
            last.then_inc(ones_ready, 1)
            dve.wait_ge(cols_ready, 1)

            def front(i, s):
                t = 2 * i + s
                wait(dve, arrived[s], gathered(i, s, 1))
                nc.vector.tensor_scalar(gi[s][:, :], index[:, bass.ds(t, 1), 2, :].rearrange("p a c -> p (a c)"), 1.0, None, ALU.mult
                                      ).then_inc(gi_ready, 1)
                wait(dve, eq_ready, t - 1)
                nc.vector.tensor_copy(keyb[s][:, :, :],
                                      keys[:, bass.ds(2 * t, 2)].unsqueeze(2).to_broadcast([P, 2, P])
                                      ).then_inc(keyb_ready, 1)

            def step(i):
                for s in two:
                    t = 2 * i + s
                    if not (last_pair(i) and s == 1):
                        front(*slot_step(i, s, 1))
                    wait(dve, hot_used, t - 1)
                    for c in two:
                        nc.vector.tensor_scalar(hot_lo[s][:, c, :], columns[:, 0:P],
                                                g["lo_digit"][:, bass.ds(2 * t + c, 1)], None, ALU.is_equal)
                        last = nc.vector.tensor_scalar(hot_hi[s][:, c, :], columns[:, 0:NCOLS],
                                                       g["hi_digit"][:, bass.ds(2 * t + c, 1)], None, ALU.is_equal)
                    last.then_inc(hot_ready, 1)
                    dve.wait_ge(rows_ready, t + 1)
                    wait(dve, summed, t - 1)
                    for c in two:
                        last = nc.vector.tensor_scalar(eq[s][:, c, :], p_keys[:, 0:GROUP], keyb[s][:, c, 0:1], None,
                                                       ALU.is_equal)
                    last.then_inc(eq_ready, 1)
                    wait(dve, added, 32 * (t - 1))
                    nc.vector.tensor_scalar(oi[s][:, :], index[:, bass.ds(t, 1), 3, :].rearrange("p a c -> p (a c)"), 1.0, None, ALU.mult
                                          ).then_inc(oi_ready, 1)
            front(0, 0)
            loop_pairs(dve, EPAIRS, step)
            dve.wait_ge(hot_used, GROUPS)
            last = nc.vector.tensor_scalar(g["deg1"][:, 0:min(NCOLS, 512)], p_deg[:, 0, 0:min(NCOLS, 512)], 1.0, None,
                                           ALU.add)
            if HI2:
                last = nc.vector.tensor_scalar(g["deg1"][:, 512:NCOLS], p_deg[:, 1, 0:HI2], 1.0, None, ALU.add)
            last.then_inc(deg_ready, 1)
            dve.wait_ge(sq_ready, 1)
            nc.vector.reciprocal(g["norm"][:, :], g["norm"][:, :])
            nc.vector.reciprocal(g["norm2"][:, :], g["deg1"][:, :])


def first_norm(nc, g):
    N, CHUNKS, PAIRS = g["N"], g["CHUNKS"], g["PAIRS"]
    moments, W1T = g["moments"], g["W1T"]
    with Scope(nc, "bn1") as sc:
        two = range(2)
        hb = [sc.sb(f"hb{s}", [P, J, D]) for s in two]
        hsum = [sc.sb(f"hsum{s}", [P, D]) for s in two]
        mrow = sc.sb("mrow", [1, D])
        cov = sc.sb("cov", [P, D])
        prod = sc.sb("prod", [P, 2 * D])
        mean_z, var_z, std_z = (sc.sb(n, [P, 2]) for n in ("mean_z", "var_z", "std_z"))
        p_mom = sc.ps("p_mom", [P, 512])
        p_mean = sc.ps("p_mean", [P, 512])
        p_small = sc.ps("p_small", [P, 512])
        p_prod = sc.ps("p_prod", [P, 512])
        p_row = sc.ps("p_row", [1, 512])
        p_out = sc.ps("p_out", [P, 512])
        p_var = sc.ps("p_var", [P, 512])
        h_in = [sc.sem(f"h_in{s}") for s in two]
        hsum_ready, h_used, dve_step, pe_step, std_ready = (
            sc.sem(n) for n in ("hsum_ready", "h_used", "dve_step", "pe_step", "std_ready"))
        block = sc.block()
        aggv = g["chunked"](g["h_t"])

        @block.sync
        def _(sp):
            def load(i):
                for s in two:
                    m = 2 * i + s
                    wait(sp, hsum_ready, m - 1)
                    wait(sp, h_used, m - 1)
                    sp.dma_start(flat(hb[s]), g["at"](aggv, m)).then_inc(h_in[s], 16)
            loop_pairs(sp, PAIRS, load)

        @block.vector
        def _(dve):
            def add(i):
                for s in two:
                    m = 2 * i + s
                    dve.wait_ge(h_in[s], 16 * (i + 1))
                    wait(dve, h_used, m - 1)
                    nc.vector.tensor_reduce(hsum[s][:, :], hb[s][:, :, :].rearrange("p j f -> p f j"), AXX, ALU.add
                                            ).then_inc(hsum_ready, 1)
            loop_pairs(dve, PAIRS, add)
            ch = Chain(dve, dve_step)
            dve.wait_ge(h_used, CHUNKS)
            nc.vector.tensor_scalar(moments[:, 0:D], p_mom[:, 0:D], 1.0 / N, None, ALU.mult)
            ch.mark(nc.vector.tensor_scalar(moments[:, D:D + 1], p_mean[:, 0:1], 1.0 / N, None, ALU.mult))
            dve.wait_ge(pe_step, 1)
            ch.mark(nc.vector.tensor_copy(mrow[:, :], p_row[0:1, 0:D]))
            dve.wait_ge(pe_step, 2)
            ch.sync()
            ch.mark(nc.vector.tensor_tensor(cov[:, :], moments[:, 0:D], p_out[:, 0:D], ALU.subtract))
            dve.wait_ge(pe_step, 3)
            ch.mark(nc.vector.tensor_tensor(prod[:, :], W1T[:, :], p_prod[:, 0:2 * D], ALU.mult))
            ch.mark(nc.vector.tensor_tensor(mean_z[:, :], p_small[:, 0:2], g["b1c"][:, :], ALU.add))
            dve.wait_ge(pe_step, 4)
            ch.mark(nc.vector.tensor_copy(var_z[:, :], p_var[:, 0:2]))
            dve.wait_ge(std_ready, 1)
            ch.mark(nc.vector.reciprocal(std_z[:, :], std_z[:, :]))
            ch.mark(nc.vector.tensor_tensor(mean_z[:, :], g["b1c"][:, :], mean_z[:, :], ALU.subtract))
            ch.sync()
            ch.mark(nc.vector.tensor_tensor(g["a1"][:, :], std_z[:, :], g["g1c"][:, :], ALU.mult))
            ch.sync()
            ch.mark(nc.vector.tensor_tensor(mean_z[:, :], mean_z[:, :], g["a1"][:, :], ALU.mult))
            ch.sync()
            ch.mark(nc.vector.tensor_tensor(g["t1"][:, :], mean_z[:, :], g["beta1c"][:, :], ALU.add))

        @block.tensor
        def _(pe):
            def products(i):
                for s in two:
                    m = 2 * i + s
                    r = g["rows_of"](m)
                    pe.wait_ge(h_in[s], 16 * (i + 1))
                    first, final = isinstance(i, int) and m == 0, isinstance(i, int) and m == CHUNKS - 1
                    for j in range(J):
                        nc.tensor.matmul(p_mom[:, 0:D], hb[s][0:r, j, :], hb[s][0:r, j, :],
                                         start=first and j == 0, stop=final and j == J - 1)
                    pe.wait_ge(hsum_ready, m + 1)
                    nc.tensor.matmul(p_mean[:, 0:1], hsum[s][0:r, :], g["ones_col"][0:r, :], start=first, stop=final
                                     ).then_inc(h_used, 1)
            loop_pairs(pe, PAIRS, products)
            pe.wait_ge(dve_step, 1)
            nc.tensor.transpose(p_row[0:1, 0:P], moments[:, D:D + 1], g["ident"][:, :]).then_inc(pe_step, 1)
            pe.wait_ge(dve_step, 2)
            nc.tensor.matmul(p_out[:, 0:D], mrow[:, :], mrow[:, :], start=True, stop=True).then_inc(pe_step, 1)
            for b in two:
                nc.tensor.matmul(p_small[:, b:b + 1], W1T[:, b * D:(b + 1) * D], moments[:, D:D + 1],
                                 start=True, stop=True)
            pe.wait_ge(dve_step, 3)
            nc.tensor.matmul(p_prod[:, 0:2 * D], cov[:, :], W1T[:, :], start=True, stop=True).then_inc(pe_step, 1)
            pe.wait_ge(dve_step, 4)
            for b in two:
                last = nc.tensor.matmul(p_var[:, b:b + 1], prod[:, b * D:(b + 1) * D], g["ones_col"][:, :],
                                        start=True, stop=True)
            last.then_inc(pe_step, 1)

        @block.scalar
        def _(act):
            act.wait_ge(dve_step, 6)
            nc.scalar.activation(std_z[:, :], var_z[:, :], ACT.Sqrt, bias=g["eps_col"][:, 0:1]).then_inc(std_ready, 1)


def mlp(nc, g):
    CHUNKS, PAIRS, NPAD = g["CHUNKS"], g["PAIRS"], g["NPAD"]
    W1T, W2T, ident = g["W1T"], g["W2T"], g["ident"]
    with Scope(nc, "mlp") as sc:
        two = range(2)
        hb = [sc.sb(f"hb{s}", [P, W]) for s in two]
        hT = [sc.sb(f"hT{q}", [P, HALF]) for q in two]
        act1 = [sc.sb(f"act1{q}", [P, 2, HALF]) for q in two]
        z2 = [sc.sb(f"z2{s}", [P, W]) for s in two]
        stats = sc.sb("stats", [P, 2 * CHUNKS, 6])
        mv = sc.sb("mv", [P, 2])
        std = sc.sb("std", [P, 1])
        zero = sc.sb("zero", [P, W])
        fresh = sc.sb("fresh", [P, J, STATE])
        p_hT = [sc.ps(f"p_hT{q}", [P, HALF]) for q in two]
        p_z1 = [sc.ps(f"p_z1{q}", [P, 2, HALF]) for q in two]
        p_z2 = [sc.ps(f"p_z2{q}", [P, HALF]) for q in two]
        h_in = [sc.sem(f"h_in{s}") for s in two]
        stored = [sc.sem(f"stored{s}") for s in two]
        cleared, zero_ready, pool_step = (sc.sem(n) for n in ("cleared", "zero_ready", "pool_step"))
        h_used, hT_ready, z1_ready, act1_ready, z2_psum, z2_ready, z2_counted = (
            sc.sem(n) for n in ("h_used", "hT_ready", "z1_ready", "act1_ready", "z2_psum", "z2_ready",
                                "z2_counted"))
        dve_step, std_ready = sc.sem("dve_step"), sc.sem("std_ready")
        block = sc.block()
        aggv = g["chunked"](g["h_t"])
        cleared_tables = [(g["chunked"](g["agg1"]), zero[:, :]), (g["chunked"](g["agg2"]), zero[:, :]),
                          (g["chunked"](g["state_t"]), fresh[:, :, :].rearrange("p j f -> p (j f)"))]

        @block.sync
        def _(sp):
            sp.wait_ge(zero_ready, 1)

            def load(i):
                for s in two:
                    m = 2 * i + s
                    wait(sp, h_used, 2 * (m - 1))
                    sp.dma_start(hb[s][:, :], g["at"](aggv, m)).then_inc(h_in[s], 16)
                    for table, value in cleared_tables:
                        sp.dma_start(g["at"](table, m), value).then_inc(cleared, 16)
            loop_pairs(sp, PAIRS, load)
            sp.wait_ge(cleared, 16 * 3 * CHUNKS)

        @block.gpsimd
        def _(pool):
            nc.gpsimd.memset(zero[:, :], 0.0)
            nc.gpsimd.memset(fresh[:, :, 0:SUMS], 0.0)
            nc.gpsimd.memset(fresh[:, :, SUMS:STATE], LOWEST).then_inc(zero_ready, 1)

            def store(i):
                for s in two:
                    m = 2 * i + s
                    pool.wait_ge(z2_ready, 2 * (m + 1))
                    pool.dma_start(g["at"](g["z2_t"], m), z2[s][:, :]).then_inc(stored[s], 16)
            loop_pairs(pool, PAIRS, store)
            for s in two:
                pool.wait_ge(stored[s], 16 * PAIRS)

        @block.vector
        def _(dve):
            def evacuate(i, s, q):
                u = 4 * i + 2 * s + q
                dve.wait_ge(h_used, u + 1)
                wait(dve, z1_ready, u - 1)
                nc.vector.tensor_copy(hT[q][:, :], p_hT[q][:, :]).then_inc(hT_ready, 1)

            def count(i, s, q):
                u = 4 * i + 2 * s + q
                r = g["rows_of"](2 * i + s)
                dve.wait_ge(z2_ready, u + 1)
                z = z2[s][:, q * HALF:(q + 1) * HALF]
                z = z if r == P else z.rearrange("p (j n) -> p j n", n=P)[:, :, 0:r]
                if isinstance(u, int):
                    o = stats[:, u, :]
                else:
                    o = stats[:, bass.ds(u, 1), :].rearrange("p a k -> p (a k)")
                nc.vector.bn_stats(o, z).then_inc(z2_counted, 1)

            def step(i):
                last_pair = isinstance(i, int) and i == PAIRS - 1
                first_pair = isinstance(i, int) and i == 0
                for s in two:
                    for q in two:
                        u4 = 2 * s + q
                        if u4 == 0 and not first_pair:
                            count(i - 1, 1, 1)
                        if u4 == 3 and last_pair:
                            count(i, 1, 0)
                            continue
                        if q == 1 and not (last_pair and s == 1):
                            evacuate(*slot_step(i, s, 1), 0)
                        elif q == 0:
                            evacuate(i, s, 1)
                        if u4:
                            count(i, (u4 - 1) // 2, (u4 - 1) % 2)
            evacuate(0, 0, 0)
            loop_pairs(dve, PAIRS, step)
            count(PAIRS - 1, 1, 1)
            dve.wait_ge(z2_counted, 2 * CHUNKS)
            ch = Chain(dve, dve_step)
            ch.mark(nc.vector.bn_aggr(mv[:, :], stats[:, :, :].rearrange("p u k -> p (u k)")))
            dve.wait_ge(std_ready, 1)
            ch.sync()
            ch.mark(nc.vector.reciprocal(std[:, :], std[:, :]))
            ch.mark(nc.vector.tensor_tensor(mv[:, 0:1], mv[:, 0:1], g["b2c"][:, :], ALU.add))
            ch.sync()
            ch.mark(nc.vector.tensor_tensor(g["a2"][:, :], std[:, :], g["g2c"][:, :], ALU.mult))
            ch.mark(nc.vector.tensor_tensor(mv[:, 0:1], g["b2c"][:, :], mv[:, 0:1], ALU.subtract))
            ch.sync()
            ch.mark(nc.vector.tensor_tensor(mv[:, 0:1], mv[:, 0:1], g["a2"][:, :], ALU.mult))
            ch.sync()
            ch.mark(nc.vector.tensor_tensor(g["t2"][:, :], mv[:, 0:1], g["beta2c"][:, :], ALU.add))

        @block.scalar
        def _(act):
            def relu(i, s, q):
                u = 4 * i + 2 * s + q
                act.wait_ge(z1_ready, u + 1)
                wait(act, z2_psum, u - 1)
                for b in two:
                    last = nc.scalar.activation(act1[q][:, b, :], p_z1[q][:, b, :], ACT.Relu,
                                                bias=g["t1"][:, b:b + 1], scale=g["a1"][:, b:b + 1])
                last.then_inc(act1_ready, 1)

            def evacuate(i, s, q):
                u = 4 * i + 2 * s + q
                act.wait_ge(z2_psum, u + 1)
                if q == 0:
                    wait(act, stored[s], 16 * i)
                    wait(act, z2_counted, 4 * i + 2 * s - 2)
                nc.scalar.copy(z2[s][:, q * HALF:(q + 1) * HALF], p_z2[q][:, :]).then_inc(z2_ready, 1)

            def step(i):
                first_pair = isinstance(i, int) and i == 0
                for s in two:
                    for q in two:
                        relu(i, s, q)
                        u4 = 2 * s + q
                        if u4:
                            evacuate(i, (u4 - 1) // 2, (u4 - 1) % 2)
                        elif not first_pair:
                            evacuate(i - 1, 1, 1)
            loop_pairs(act, PAIRS, step)
            evacuate(PAIRS - 1, 1, 1)
            act.wait_ge(dve_step, 1)
            nc.scalar.activation(std[:, :], mv[:, 1:2], ACT.Sqrt, bias=g["eps_col"][:, 0:1]).then_inc(std_ready, 1)

        @block.tensor
        def _(pe):
            def turn(i, s, q):
                u = 4 * i + 2 * s + q
                pe.wait_ge(h_in[s], 16 * (i + 1))
                wait(pe, hT_ready, u - 1)
                for k in range(J // 2):
                    j = q * (J // 2) + k
                    last = nc.tensor.transpose(p_hT[q][:, k * P:(k + 1) * P], hb[s][:, j * D:(j + 1) * D], ident[:, :])
                last.then_inc(h_used, 1)

            def first(i, s, q):
                u = 4 * i + 2 * s + q
                pe.wait_ge(hT_ready, u + 1)
                wait(pe, act1_ready, u - 1)
                for b in two:
                    last = nc.tensor.matmul(p_z1[q][:, b, :], W1T[:, b * D:(b + 1) * D], hT[q][:, :],
                                            start=True, stop=True)
                last.then_inc(z1_ready, 1)

            def second(i, s, q):
                u = 4 * i + 2 * s + q
                pe.wait_ge(act1_ready, u + 1)
                wait(pe, z2_ready, u - 1)
                for b in two:
                    last = nc.tensor.matmul(p_z2[q][:, :], W2T[:, b, :], act1[q][:, b, :],
                                            start=(b == 0), stop=(b == 1))
                last.then_inc(z2_psum, 1)

            def step(i):
                first_pair = isinstance(i, int) and i == 0
                last_pair = isinstance(i, int) and i == PAIRS - 1
                for s in two:
                    for q in two:
                        first(i, s, q)
                        if q == 0:
                            turn(i, s, 1)
                        elif not (last_pair and s == 1):
                            turn(*slot_step(i, s, 1), 0)
                        u4 = 2 * s + q
                        if u4:
                            second(i, (u4 - 1) // 2, (u4 - 1) % 2)
                        elif not first_pair:
                            second(i - 1, 1, 1)
            turn(0, 0, 0)
            loop_pairs(pe, PAIRS, step)
            second(PAIRS - 1, 1, 1)


class NodeNorm:

    def __init__(self, nc, sc, g):
        self.nc, self.g = nc, g
        self.u = [sc.sb(f"u{s}", [P, J, D]) for s in range(2)]
        self.y = [sc.sb(f"y{s}", [P, J, D]) for s in range(2)]
        self.stats = sc.sb("stats", [P, J, 6])
        self.tmp = sc.sb("tmp", [P, 3, J])
        self.mean = [sc.sb(f"mean{s}", [P, J]) for s in range(2)]
        self.var = [sc.sb(f"var{s}", [P, J]) for s in range(2)]
        self.std = [sc.sb(f"std{s}", [P, J]) for s in range(2)]
        self.rstd = [sc.sb(f"rstd{s}", [P, J]) for s in range(2)]
        self.shift = [sc.sb(f"shift{s}", [P, J]) for s in range(2)]
        self.step = sc.sem("dve_step")
        self.u_ready, self.var_ready, self.std_ready, self.scale_ready, self.y_ready, self.y_ready_act = (
            sc.sem(n) for n in ("u_ready", "var_ready", "std_ready", "scale_ready", "y_ready", "y_ready_act"))
        self.stored = [sc.sem(f"stored{s}") for s in range(2)]

    def round(self, dve, ch, cur, prev, add_u=None, scale2=None, scale=None):
        nc, st = self.nc, self.stats
        rows = iter(range(J - ACT_ROWS))

        def row():
            if prev:
                j = next(rows)
                ins = nc.vector.tensor_scalar(self.y[ps][:, j, :], self.u[ps][:, j, :], self.mean[ps][:, j:j + 1],
                                              self.rstd[ps][:, j:j + 1], ALU.subtract, ALU.mult)
                if j == J - ACT_ROWS - 1:
                    ins.then_inc(self.y_ready, 1)
        if prev:
            pi, ps = prev
            pm = 2 * pi + ps
            dve.wait_ge(self.std_ready, pm + 1)
            wait(dve, self.y_ready_act, pm - 1)
            factor = ch.mark(nc.vector.reciprocal(self.rstd[ps][:, :], self.std[ps][:, :]))
        if cur:
            i, s = cur
            m = 2 * i + s
            add_u()
        if prev:
            if scale is not None:
                ch.after(factor)
                factor = ch.mark(nc.vector.tensor_tensor(self.rstd[ps][:, :], self.rstd[ps][:, :], scale, ALU.mult))
            ch.after(factor)
            nc.vector.scalar_tensor_tensor(out=self.shift[ps][:, :], in0=self.mean[ps][:, :], scalar=-1.0,
                                           in1=self.rstd[ps][:, :], op0=ALU.mult, op1=ALU.mult
                                           ).then_inc(self.scale_ready, 1)
        if cur:
            dve.wait_ge(self.u_ready, m + 1)
            for j in range(J):
                last = nc.vector.bn_stats(st[:, j, :], self.u[s][:, j, :])
            counted = ch.mark(last)
        if prev:
            wait(dve, self.stored[ps], 16 * pi)
        row()
        tot, dif, m2 = (self.tmp[:, k, :] for k in range(3))
        if cur:
            ch.after(counted)
            wait(dve, self.y_ready, m - 1)
            ch.mark(nc.vector.tensor_tensor(tot, st[:, :, 1], st[:, :, 4], ALU.add))
            ch.mark(nc.vector.tensor_tensor(dif, st[:, :, 1], st[:, :, 4], ALU.subtract))
            parts = ch.mark(nc.vector.tensor_tensor(m2, st[:, :, 2], st[:, :, 5], ALU.add))
        row()
        if cur:
            ch.after(parts)
            ch.mark(nc.vector.tensor_scalar(self.mean[s][:, :], tot, 0.5, None, ALU.mult))
            square = ch.mark(nc.vector.scalar_tensor_tensor(out=dif, in0=dif, scalar=0.25, in1=dif, op0=ALU.mult,
                                                            op1=ALU.mult))
        row()
        if cur:
            ch.after(square)
            wait(dve, self.std_ready, m - 1)
            var = nc.vector.scalar_tensor_tensor(out=self.var[s][:, :], in0=m2, scalar=1.0 / D, in1=dif,
                                                 op0=ALU.mult, op1=ALU.add)
            if scale2 is None:
                var.then_inc(self.var_ready, 1)
            else:
                plain = ch.mark(var)
        row()
        if cur and scale2 is not None:
            ch.after(plain)
            nc.vector.tensor_tensor(self.var[s][:, :], self.var[s][:, :], scale2, ALU.mult
                                    ).then_inc(self.var_ready, 1)

    def root(self, act, i, s):
        m = 2 * i + s
        act.wait_ge(self.var_ready, m + 1)
        wait(act, self.scale_ready, m - 1)
        self.nc.scalar.activation(self.std[s][:, :], self.var[s][:, :], ACT.Sqrt,
                                  bias=self.g["eps_col"][:, 0:1]).then_inc(self.std_ready, 1)

    def free_u(self, dve, m):
        wait(dve, self.y_ready, m - 1)
        wait(dve, self.y_ready_act, m - 1)

    def apply_act(self, act, i, s):
        m = 2 * i + s
        act.wait_ge(self.scale_ready, m + 1)
        wait(act, self.stored[s], 16 * i)
        for j in range(J - ACT_ROWS, J):
            last = self.nc.scalar.activation(self.y[s][:, j, :], self.u[s][:, j, :], ACT.Identity,
                                             bias=self.shift[s][:, j:j + 1], scale=self.rstd[s][:, j:j + 1])
        last.then_inc(self.y_ready_act, 1)

    def store(self, act, i, s, where):
        m = 2 * i + s
        act.wait_ge(self.y_ready, m + 1)
        act.wait_ge(self.y_ready_act, m + 1)
        rows = where.shape[0]
        act.dma_start(where, self.y[s][0:rows, :, :].rearrange("p j f -> p (j f)")).then_inc(self.stored[s], 16)

    def out(self, act, i, s, where):
        self.apply_act(act, i, s)
        self.store(act, i, s, where)

    def finish(self, sp, pairs):
        for s in range(2):
            sp.wait_ge(self.stored[s], 16 * pairs)


def flat(b):
    return b[:, :, :].rearrange("p j f -> p (j f)")


def ahead(pairs, i, s):
    return None if isinstance(i, int) and i == pairs - 1 and s == 1 else slot_step(i, s, 1)


def behind(i, s):
    if s == 1:
        return i, 0
    return None if isinstance(i, int) and i == 0 else (i - 1, 1)


def per_node(table, i, s):
    return table[:, bass.ds((2 * i + s) * J, J)]


def first_layer_out(nc, g):
    PAIRS = g["PAIRS"]
    with Scope(nc, "out1") as sc:
        two = range(2)
        xb = [sc.sb(f"xb{s}", [P, W]) for s in two]
        zb = [sc.sb(f"zb{s}", [P, W]) for s in two]
        rb = [sc.sb(f"rb{s}", [P, W]) for s in two]
        p_r = [sc.ps(f"p_r{s}", [P, W]) for s in two]
        nn = NodeNorm(nc, sc, g)
        x_in = [sc.sem(f"x_in{s}") for s in two]
        z_in = [sc.sem(f"z_in{s}") for s in two]
        r_ready, turned = sc.sem("r_ready"), sc.sem("turned")
        block = sc.block()
        outv = g["chunked"](g["x1n_t"])

        @block.sync
        def _(sp):
            def load(i, s):
                m = 2 * i + s
                r = g["rows_of"](m)
                wait(sp, r_ready, m - 1)
                sp.dma_start(zb[s][:, :], g["at"](g["z2_t"], m)).then_inc(z_in[s], 16)
                wait(sp, nn.u_ready, m - 1)
                sp.dma_start(xb[s][0:r, :], g["node_rows"](g["x"], m, r)).then_inc(x_in[s], 16)

            def step(i):
                for s in two:
                    if ahead(PAIRS, i, s):
                        load(*ahead(PAIRS, i, s))
            load(0, 0)
            loop_pairs(sp, PAIRS, step)

        @block.scalar
        def _(act):
            def relu(i, s):
                m = 2 * i + s
                act.wait_ge(z_in[s], 16 * (i + 1))
                wait(act, turned, m - 1)
                nc.scalar.activation(rb[s][:, :], zb[s][:, :], ACT.Relu, bias=g["t2"][:, 0:1],
                                     scale=g["a2"][:, 0:1]).then_inc(r_ready, 1)

            def step(i):
                for s in two:
                    if ahead(PAIRS, i, s):
                        relu(*ahead(PAIRS, i, s))
                    nn.root(act, i, s)
                    if behind(i, s):
                        b = behind(i, s)
                        nn.out(act, *b, g["at"](outv, 2 * b[0] + b[1]))
            relu(0, 0)
            loop_pairs(act, PAIRS, step)
            nn.out(act, PAIRS - 1, 1, g["at"](outv, 2 * PAIRS - 1))
            nn.finish(act, PAIRS)

        @block.tensor
        def _(pe):
            def step(i):
                for s in two:
                    m = 2 * i + s
                    pe.wait_ge(r_ready, m + 1)
                    wait(pe, nn.u_ready, m - 1)
                    for j in range(J):
                        last = nc.tensor.transpose(p_r[s][:, j * D:(j + 1) * D], rb[s][:, j * P:(j + 1) * P],
                                                   g["ident"][:, :])
                    last.then_inc(turned, 1)
            loop_pairs(pe, PAIRS, step)

        @block.vector
        def _(dve):
            ch = Chain(dve, nn.step)

            def add(i, s):
                m = 2 * i + s
                dve.wait_ge(x_in[s], 16 * (i + 1))
                dve.wait_ge(turned, m + 1)
                nn.free_u(dve, m)
                nc.vector.tensor_tensor(flat(nn.u[s]), p_r[s][:, :], xb[s][:, :], ALU.add).then_inc(nn.u_ready, 1)

            def step(i):
                for s in two:
                    prev = behind(i, s)
                    nn.round(dve, ch, (i, s), prev, add_u=lambda: add(i, s),
                             scale=per_node(g["norm"], *prev) if prev else None)
            loop_pairs(dve, PAIRS, step, ch, 16)
            nn.round(dve, ch, None, (PAIRS - 1, 1), scale=per_node(g["norm"], PAIRS - 1, 1))


def aggregate(nc, g, tag, table, acc, key_at, gather_kind, owner_kind):
    EC, GROUPS, EPAIRS = g["EDGE_COLS"], g["GROUPS"], g["EPAIRS"]
    keys, index, ident = g["keys"], g["index"], g["ident"]
    with Scope(nc, "sum_" + tag) as sc:
        two = range(2)
        gi = [sc.sb(f"gi{s}", [P, 2], I32) for s in two]
        oi = [sc.sb(f"oi{s}", [P, 2], I32) for s in two]
        keyb = [sc.sb(f"keyb{s}", [P, 2, P]) for s in two]
        eq = [sc.sb(f"eq{s}", [P, 2, GROUP]) for s in two]
        rows = [sc.sb(f"rows{s}", [P, 2, D]) for s in two]
        sums = [sc.sb(f"sums{s}", [P, 2, D]) for s in two]
        p_keys = [sc.ps(f"p_keys{s}", [P, 512]) for s in two]
        p_sums = [sc.ps(f"p_sums{s}", [P, 512]) for s in two]
        arrived = [sc.sem(f"arrived{s}") for s in two]
        added, gi_ready, oi_ready, keyb_ready, rows_ready, eq_ready, summed, sums_ready = (
            sc.sem(n) for n in ("added", "gi_ready", "oi_ready", "keyb_ready", "rows_ready", "eq_ready", "summed",
                                "sums_ready"))
        block = sc.block()

        @block.gpsimd
        def _(pool):
            gathers, scatters = Turns(pool, sc.tag + "_gathers"), Turns(pool, sc.tag + "_scatters")

            def gather(i, s):
                t = 2 * i + s
                wait(pool, summed, t - 1)
                gathers.wait(gi_ready, t)
                for c in two:
                    pool.indirect_dma_start(rows[s][:, c, :], None, table,
                                            bass.IndirectOffsetOnAxis(ap=gi[s][:, c:c + 1], axis=0)
                                            ).then_inc(arrived[s], 16)

            def step(i):
                for s in two:
                    t = 2 * i + s
                    if ahead(EPAIRS, i, s):
                        gather(*ahead(EPAIRS, i, s))
                    pool.wait_ge(oi_ready, t + 1)
                    wait(pool, added, 32 * t)
                    scatters.wait(sums_ready, t)
                    for c in two:
                        pool.indirect_dma_start(acc, bass.IndirectOffsetOnAxis(ap=oi[s][:, c:c + 1], axis=0),
                                                sums[s][:, c, :], None, compute_op=ALU.add).then_inc(added, 16)
            gather(0, 0)
            loop_pairs(pool, EPAIRS, step)
            pool.wait_ge(added, 32 * GROUPS)

        @block.tensor
        def _(pe):
            def spread(i, s):
                t = 2 * i + s
                pe.wait_ge(keyb_ready, t + 1)
                wait(pe, eq_ready, t - 1)
                for c in two:
                    last = nc.tensor.matmul(p_keys[s][:, c * P:(c + 1) * P], keyb[s][:, c, :], ident[:, :],
                                            start=True, stop=True)
                last.then_inc(rows_ready, 1)

            def step(i):
                for s in two:
                    t = 2 * i + s
                    if ahead(EPAIRS, i, s):
                        spread(*ahead(EPAIRS, i, s))
                    pe.wait_ge(eq_ready, t + 1)
                    pe.wait_ge(arrived[s], gathered(i, s))
                    wait(pe, sums_ready, t - 1)
                    for c in two:
                        for k in two:
                            last = nc.tensor.matmul(p_sums[s][:, c * D:(c + 1) * D], eq[s][:, k, c * P:(c + 1) * P],
                                                    rows[s][:, k, :], start=(k == 0), stop=(k == 1))
                    last.then_inc(summed, 1)
            spread(0, 0)
            loop_pairs(pe, EPAIRS, step)

        @block.scalar
        def _(act):
            def step(i):
                for s in two:
                    t = 2 * i + s
                    act.wait_ge(summed, t + 1)
                    wait(act, added, 32 * (t - 1))
                    nc.scalar.copy(sums[s][:, :, :].rearrange("p c f -> p (c f)"), p_sums[s][:, 0:2 * D]
                                   ).then_inc(sums_ready, 1)
            loop_pairs(act, EPAIRS, step)

        @block.vector
        def _(dve):
            def front(i, s):
                t = 2 * i + s
                wait(dve, arrived[s], gathered(i, s, 1))
                nc.vector.tensor_scalar(gi[s][:, :],
                                      index[:, bass.ds(t, 1), gather_kind, :].rearrange("p a c -> p (a c)"), 1.0, None, ALU.mult
                                      ).then_inc(gi_ready, 1)
                wait(dve, eq_ready, t - 1)
                nc.vector.tensor_copy(keyb[s][:, :, :],
                                      keys[:, bass.ds(2 * t + key_at, 2)].unsqueeze(2).to_broadcast([P, 2, P])
                                      ).then_inc(keyb_ready, 1)

            def step(i):
                for s in two:
                    t = 2 * i + s
                    if ahead(EPAIRS, i, s):
                        front(*ahead(EPAIRS, i, s))
                    dve.wait_ge(rows_ready, t + 1)
                    wait(dve, summed, t - 1)
                    for c in two:
                        last = nc.vector.tensor_scalar(eq[s][:, c, :], p_keys[s][:, 0:GROUP], keyb[s][:, c, 0:1], None,
                                                       ALU.is_equal)
                    last.then_inc(eq_ready, 1)
                    wait(dve, added, 32 * (t - 1))
                    nc.vector.tensor_scalar(oi[s][:, :],
                                          index[:, bass.ds(t, 1), owner_kind, :].rearrange("p a c -> p (a c)"), 1.0, None, ALU.mult
                                          ).then_inc(oi_ready, 1)
            front(0, 0)
            loop_pairs(dve, EPAIRS, step)


def convolve(nc, g, tag, table, acc, result, WT):
    PAIRS = g["PAIRS"]
    first = tag == "l1"
    with Scope(nc, "conv_" + tag) as sc:
        two = range(2)
        xb = [sc.sb(f"xb{s}", [P, J, D]) for s in two]
        ab = [sc.sb(f"ab{s}", [P, J, D]) for s in two]
        gb = [sc.sb(f"gb{s}", [P, J, D]) for s in two] if first else ab
        vb = [sc.sb(f"vb{s}", [P, J, D]) for s in two]
        gT = [sc.sb(f"gT{s}", [P, W]) for s in two]
        p_g = [sc.ps(f"p_g{s}", [P, W]) for s in two]
        p_o = [sc.ps(f"p_o{s}", [P, W]) for s in two]
        nn = NodeNorm(nc, sc, g)
        x_in = [sc.sem(f"x_in{s}") for s in two]
        a_in = [sc.sem(f"a_in{s}") for s in two]
        g_ready, v_ready, turned, gT_ready, o_ready = (
            sc.sem(n) for n in ("g_ready", "v_ready", "turned", "gT_ready", "o_ready"))
        block = sc.block()
        xv, av, outv = (g["chunked"](t) for t in (table, acc, result))

        @block.sync
        def _(sp):
            def load(i, s):
                m = 2 * i + s
                wait(sp, v_ready, m - 1)
                sp.dma_start(flat(xb[s]), g["at"](xv, m)).then_inc(x_in[s], 16)
                if not first:
                    wait(sp, turned, m - 1)
                sp.dma_start(flat(ab[s]), g["at"](av, m)).then_inc(a_in[s], 16)

            def step(i):
                for s in two:
                    if ahead(PAIRS, i, s):
                        load(*ahead(PAIRS, i, s))
            load(0, 0)
            loop_pairs(sp, PAIRS, step)

        @block.gpsimd
        def _(pool):
            def step(i):
                for s in two:
                    m = 2 * i + s
                    pool.wait_ge(x_in[s], 16 * (i + 1))
                    if first:
                        pool.wait_ge(a_in[s], 16 * (i + 1))
                        wait(pool, turned, m - 1)
                        nc.gpsimd.tensor_tensor(flat(gb[s]), flat(xb[s]), flat(ab[s]), ALU.add
                                                ).then_inc(g_ready, 1)
                        wait(pool, nn.u_ready, m - 1)
                        nc.gpsimd.tensor_tensor(
                            vb[s][:, :, :], xb[s][:, :, :],
                            per_node(g["deg1"], i, s).unsqueeze(2).to_broadcast([P, J, D]), ALU.mult
                            ).then_inc(v_ready, 1)
                    else:
                        wait(pool, nn.u_ready, m - 1)
                        nc.gpsimd.tensor_tensor(vb[s][:, :, :], xb[s][:, :, :],
                                                g["bL2_all"][:, :].unsqueeze(1).to_broadcast([P, J, D]), ALU.add
                                                ).then_inc(v_ready, 1)
            loop_pairs(pool, PAIRS, step)

        @block.tensor
        def _(pe):
            def turn(i, s):
                m = 2 * i + s
                if first:
                    pe.wait_ge(g_ready, m + 1)
                else:
                    pe.wait_ge(a_in[s], 16 * (i + 1))
                wait(pe, gT_ready, m - 1)
                for j in range(J):
                    last = nc.tensor.transpose(p_g[s][:, j * P:(j + 1) * P], gb[s][:, j, :], g["ident"][:, :])
                last.then_inc(turned, 1)

            def step(i):
                for s in two:
                    m = 2 * i + s
                    if ahead(PAIRS, i, s):
                        turn(*ahead(PAIRS, i, s))
                    pe.wait_ge(gT_ready, m + 1)
                    wait(pe, nn.u_ready, m - 1)
                    for j in range(J):
                        last = nc.tensor.matmul(p_o[s][:, j * D:(j + 1) * D], gT[s][:, j * P:(j + 1) * P], WT[:, :],
                                                start=True, stop=True)
                    last.then_inc(o_ready, 1)
            turn(0, 0)
            loop_pairs(pe, PAIRS, step)

        @block.scalar
        def _(act):
            def evacuate(i, s):
                m = 2 * i + s
                act.wait_ge(turned, m + 1)
                wait(act, o_ready, m - 1)
                nc.scalar.copy(gT[s][:, :], p_g[s][:, :]).then_inc(gT_ready, 1)

            def step(i):
                for s in two:
                    if ahead(PAIRS, i, s):
                        evacuate(*ahead(PAIRS, i, s))
                    nn.root(act, i, s)
                    if behind(i, s):
                        b = behind(i, s)
                        nn.out(act, *b, g["at"](outv, 2 * b[0] + b[1]))
            evacuate(0, 0)
            loop_pairs(act, PAIRS, step)
            nn.out(act, PAIRS - 1, 1, g["at"](outv, 2 * PAIRS - 1))
            nn.finish(act, PAIRS)

        @block.vector
        def _(dve):
            ch = Chain(dve, nn.step)

            def add(i, s):
                m = 2 * i + s
                dve.wait_ge(v_ready, m + 1)
                dve.wait_ge(o_ready, m + 1)
                nn.free_u(dve, m)
                nc.vector.tensor_tensor(flat(nn.u[s]), p_o[s][:, :], flat(vb[s]), ALU.add).then_inc(nn.u_ready, 1)

            def step(i):
                for s in two:
                    prev = behind(i, s)
                    nn.round(dve, ch, (i, s), prev, add_u=lambda: add(i, s),
                             scale2=per_node(g["norm2"], i, s) if first else None,
                             scale=per_node(g["norm"], *prev) if first and prev else None)
            loop_pairs(dve, PAIRS, step, ch, 18 if first else 14)
            nn.round(dve, ch, None, (PAIRS - 1, 1), scale=per_node(g["norm"], PAIRS - 1, 1) if first else None)


def attention(nc, g):
    GROUPS, EPAIRS = g["GROUPS"], g["EPAIRS"]
    keys, index, ident, x3_t, state_t, WT = (g[n] for n in ("keys", "index", "ident", "x3_t", "state_t", "WLT"))
    WT = WT[2]
    SCALE = HD ** -0.5
    with Scope(nc, "attn") as sc:
        two = range(2)
        gi = [sc.sb(f"gi{s}", [P, 4], I32) for s in two]
        oi = [sc.sb(f"oi{s}", [P, 4], I32) for s in two]
        keyb = [sc.sb(f"keyb{s}", [P, 2, P]) for s in two]
        eq = [sc.sb(f"eq{s}", [P, 2, GROUP]) for s in two]
        below = sc.sb("below", [P, 2, GROUP])
        ends = [sc.sb(f"ends{s}", [P, 4, D]) for s in two]
        endsT = [sc.sb(f"endsT{s}", [P, 4 * P]) for s in two]
        ft = [sc.sb(f"ft{s}", [P, 4, D]) for s in two]
        prod = sc.sb("prod", [P, 2, D])
        logit = [sc.sb(f"logit{s}", [P, 2, HEADS]) for s in two]
        shifted = sc.sb("shifted", [P, 2, HEADS, GROUP])
        peak = [sc.sb(f"peak{s}", [P, 2, HEADS]) for s in two]
        gap = [sc.sb(f"gap{s}", [P, 2, HEADS]) for s in two]
        terms = [sc.sb(f"terms{s}", [P, 2, HEADS, HS]) for s in two]
        old = [sc.sb(f"old{s}", [P, 2, STATE]) for s in two]
        new = [sc.sb(f"new{s}", [P, 2, STATE]) for s in two]
        drop = [sc.sb(f"drop{s}", [P, 2, 2, HEADS]) for s in two]
        keep = [sc.sb(f"keep{s}", [P, 2, 2, HEADS]) for s in two]
        part = sc.sb("part", [P, 2, SUMS])
        p_keys = sc.ps("p_keys", [P, 512])
        p_endsT = sc.ps("p_endsT", [P, 512])
        p_ft = sc.ps("p_ft", [P, 512])
        p_logit = sc.ps("p_logit", [P, HEADS, GROUP])
        p_sums = [sc.ps(f"p_sums{s}", [P, 512]) for s in two]
        arrived = [sc.sem(f"arrived{s}") for s in two]
        state_in = [sc.sem(f"state_in{s}") for s in two]
        state_out = sc.sem("state_out")
        names = ("gi_ready", "oi_ready", "keyb_ready", "rows_ready", "eq_ready", "turned", "endsT_ready", "ft_psum",
                 "ft_ready", "logit_ready", "logit_rows", "peak_ready", "weight_ready", "terms_ready", "summed",
                 "drop_ready", "keep_ready", "new_ready", "shift_used", "dve_step", "gap_ready")
        S = {n: sc.sem(n) for n in names}
        block = sc.block()

        def heads(ap):
            return ap.rearrange("p c (h f) -> p c h f", h=HEADS)

        def second_next(i, s):
            return None if isinstance(i, int) and i == EPAIRS - 1 else (i + 1, s)

        @block.gpsimd
        def _(pool):
            gathers, scatters = Turns(pool, sc.tag + "_gathers"), Turns(pool, sc.tag + "_scatters")
            states = Turns(pool, sc.tag + "_states")

            def gather(i, s):
                t = 2 * i + s
                wait(pool, S["turned"], t - 1)
                gathers.wait(S["gi_ready"], t)
                for c in range(4):
                    pool.indirect_dma_start(ends[s][:, c, :], None, x3_t,
                                            bass.IndirectOffsetOnAxis(ap=gi[s][:, c:c + 1], axis=0)
                                            ).then_inc(arrived[s], 16)

            def step(i):
                for s in two:
                    t = 2 * i + s
                    wait(pool, state_out, 32 * t)
                    wait(pool, S["new_ready"], t - 1)
                    states.wait(S["oi_ready"], t)
                    for c in two:
                        pool.indirect_dma_start(old[s][:, c, :], None, state_t,
                                                bass.IndirectOffsetOnAxis(ap=oi[s][:, c:c + 1], axis=0)
                                                ).then_inc(state_in[s], 16)
                    if second_next(i, s):
                        gather(*second_next(i, s))
                    scatters.wait(S["new_ready"], t)
                    for c in two:
                        pool.indirect_dma_start(state_t, bass.IndirectOffsetOnAxis(ap=oi[s][:, 2 + c:3 + c], axis=0),
                                                new[s][:, c, :], None).then_inc(state_out, 16)
            gather(0, 0)
            gather(0, 1)
            loop_pairs(pool, EPAIRS, step)
            pool.wait_ge(state_out, 32 * GROUPS)

        @block.tensor
        def _(pe):
            def front(i, s):
                t = 2 * i + s
                pe.wait_ge(S["keyb_ready"], t + 1)
                wait(pe, S["eq_ready"], t)
                for c in two:
                    last = nc.tensor.matmul(p_keys[:, c * P:(c + 1) * P], keyb[s][:, c, :], ident[:, :],
                                            start=True, stop=True)
                last.then_inc(S["rows_ready"], 1)
                pe.wait_ge(arrived[s], 64 * (i + 1))
                wait(pe, S["endsT_ready"], t)
                for c in range(4):
                    last = nc.tensor.transpose(p_endsT[:, c * P:(c + 1) * P], ends[s][:, c, :], ident[:, :])
                last.then_inc(S["turned"], 1)
                pe.wait_ge(S["endsT_ready"], t + 1)
                wait(pe, S["ft_ready"], t)
                for c in range(4):
                    last = nc.tensor.matmul(p_ft[:, c * D:(c + 1) * D], endsT[s][:, c * P:(c + 1) * P], WT[:, :],
                                            start=True, stop=True)
                last.then_inc(S["ft_psum"], 1)

            def middle(i, s):
                t = 2 * i + s
                pe.wait_ge(S["logit_ready"], t + 1)
                wait(pe, S["peak_ready"], t)
                for h in range(HEADS):
                    for c in two:
                        last = nc.tensor.matmul(p_logit[:, h, c * P:(c + 1) * P],
                                                logit[s][:, c, h:h + 1].to_broadcast([P, P]), ident[:, :],
                                                start=True, stop=True)
                last.then_inc(S["logit_rows"], 1)

            def back(i, s):
                t = 2 * i + s
                pe.wait_ge(S["terms_ready"], t + 1)
                wait(pe, S["new_ready"], t - 1)
                for c in two:
                    for k in two:
                        last = nc.tensor.matmul(p_sums[s][:, c * SUMS:(c + 1) * SUMS],
                                                eq[s][:, k, c * P:(c + 1) * P],
                                                terms[s][:, k, :, :].rearrange("p h f -> p (h f)"),
                                                start=(k == 0), stop=(k == 1))
                last.then_inc(S["summed"], 1)

            def step(i):
                for s in two:
                    if ahead(EPAIRS, i, s):
                        middle(*ahead(EPAIRS, i, s))
                        back(*ahead(EPAIRS, i, s))
                    if second_next(i, s):
                        front(*second_next(i, s))
            front(0, 0)
            middle(0, 0)
            back(0, 0)
            front(0, 1)
            loop_pairs(pe, EPAIRS, step)

        @block.scalar
        def _(act):
            def front(i, s):
                t = 2 * i + s
                act.wait_ge(S["turned"], t + 1)
                wait(act, S["ft_psum"], t - 1)
                nc.scalar.copy(endsT[s][:, :], p_endsT[:, :]).then_inc(S["endsT_ready"], 1)
                act.wait_ge(S["ft_psum"], t + 1)
                wait(act, S["terms_ready"], t - 1)
                nc.scalar.copy(flat(ft[s]), p_ft[:, :]).then_inc(S["ft_ready"], 1)

            def weigh(i, s):
                t = 2 * i + s
                act.wait_ge(S["gap_ready"], t + 1)
                wait(act, S["summed"], t - 1)
                nc.scalar.activation(terms[s][:, :, :, HD], gap[s][:, :, :], ACT.Exp).then_inc(S["weight_ready"], 1)

            def step(i):
                for s in two:
                    t = 2 * i + s
                    act.wait_ge(S["drop_ready"], t + 1)
                    wait(act, S["new_ready"], t - 1)
                    nc.scalar.activation(keep[s][:, :, :, :], drop[s][:, :, :, :], ACT.Exp
                                         ).then_inc(S["keep_ready"], 1)
                    if ahead(EPAIRS, i, s):
                        weigh(*ahead(EPAIRS, i, s))
                    if second_next(i, s):
                        front(*second_next(i, s))
            front(0, 0)
            weigh(0, 0)
            front(0, 1)
            loop_pairs(act, EPAIRS, step)

        @block.vector
        def _(dve):
            ch = Chain(dve, S["dve_step"])
            peaks = Turns(dve, sc.tag + "_peaks")

            def indices(i, s):
                t = 2 * i + s
                wait(dve, arrived[s], 64 * i)
                nc.vector.tensor_scalar(gi[s][:, :].rearrange("p (k c) -> p k c", c=2),
                                      index[:, bass.ds(t, 1), 1:3, :].rearrange("p a k c -> p (a k) c"), 1.0, None, ALU.mult
                                      ).then_inc(S["gi_ready"], 1)
                wait(dve, S["eq_ready"], t - 1)
                nc.vector.tensor_copy(keyb[s][:, :, :],
                                      keys[:, bass.ds(2 * t, 2)].unsqueeze(2).to_broadcast([P, 2, P])
                                      ).then_inc(S["keyb_ready"], 1)

            def state_indices(i, s):
                t = 2 * i + s
                wait(dve, state_out, 32 * (t - 1))
                nc.vector.tensor_scalar(oi[s][:, :].rearrange("p (k c) -> p k c", c=2),
                                      index[:, bass.ds(t, 1), 1:4:2, :].rearrange("p a k c -> p (a k) c"), 1.0, None, ALU.mult
                                      ).then_inc(S["oi_ready"], 1)

            def front(i, s):
                t = 2 * i + s
                dve.wait_ge(S["rows_ready"], t + 1)
                wait(dve, S["summed"], t - 1)
                for c in two:
                    last = nc.vector.tensor_scalar(eq[s][:, c, :], p_keys[:, 0:GROUP], keyb[s][:, c, 0:1], None,
                                                   ALU.is_equal)
                last.then_inc(S["eq_ready"], 1)
                dve.wait_ge(S["ft_ready"], t + 1)
                ch.mark(nc.vector.tensor_tensor(prod[:, :, :], ft[s][:, 0:2, :], ft[s][:, 2:4, :], ALU.mult))
                ch.sync()
                dve.wait_ge(S["eq_ready"], t + 1)
                ch.mark(nc.vector.tensor_reduce(logit[s][:, :, :], heads(prod[:, :, :]), AXX, ALU.add))
                ch.mark(nc.vector.tensor_scalar(below[:, :, :], eq[s][:, :, :], 1.0, -LOWEST, ALU.subtract, ALU.mult))
                ch.sync()
                nc.vector.tensor_scalar(logit[s][:, :, :], logit[s][:, :, :], SCALE, None, ALU.mult
                                        ).then_inc(S["logit_ready"], 1)
                dve.wait_ge(S["logit_ready"], t + 1)
                peaks.wait(S["logit_rows"], t)
                for c in two:
                    for h in range(HEADS):
                        last = nc.vector.tensor_tensor_reduce(
                            out=shifted[:, c, h, :], in0=p_logit[:, h, :], in1=below[:, c, :], scale=1.0,
                            scalar=LOWEST, op0=ALU.add, op1=ALU.max, accum_out=peak[s][:, c, h:h + 1])
                last.then_inc(S["peak_ready"], 1)
                dve.wait_ge(S["peak_ready"], t + 1)
                wait(dve, S["weight_ready"], t - 1)
                nc.vector.tensor_tensor(gap[s][:, :, :], logit[s][:, :, :], peak[s][:, :, :], ALU.subtract
                                        ).then_inc(S["gap_ready"], 1)
                dve.wait_ge(S["weight_ready"], t + 1)
                nc.vector.tensor_tensor(terms[s][:, :, :, 0:HD], heads(ft[s][:, 2:4, :]),
                                        terms[s][:, :, :, HD].unsqueeze(3).to_broadcast([P, 2, HEADS, HD]),
                                        ALU.mult).then_inc(S["terms_ready"], 1)

            def join(i, s):
                t = 2 * i + s
                dve.wait_ge(state_in[s], 32 * (i + 1))
                new_max = new[s][:, :, SUMS:STATE]
                ch.mark(nc.vector.tensor_tensor(new_max, old[s][:, :, SUMS:STATE], peak[s][:, :, :], ALU.max))
                ch.sync()
                ch.mark(nc.vector.tensor_tensor(drop[s][:, 0, :, :], old[s][:, :, SUMS:STATE], new_max, ALU.subtract))
                nc.vector.tensor_tensor(drop[s][:, 1, :, :], peak[s][:, :, :], new_max, ALU.subtract
                                        ).then_inc(S["drop_ready"], 1)
                dve.wait_ge(S["keep_ready"], t + 1)
                dve.wait_ge(S["summed"], t + 1)
                p_s = p_sums[s][:, 0:2 * SUMS].rearrange("p (c f) -> p c f", c=2)

                def kept(k):
                    return keep[s][:, k, :, :]
                ch.mark(nc.vector.tensor_tensor(heads(new[s][:, :, 0:SUMS]), heads(old[s][:, :, 0:SUMS]),
                                                kept(0).unsqueeze(3).to_broadcast([P, 2, HEADS, HS]), ALU.mult))
                ch.mark(nc.vector.tensor_tensor(heads(part[:, :, :]), heads(p_s), kept(1).unsqueeze(3).to_broadcast(
                    [P, 2, HEADS, HS]), ALU.mult))
                ch.sync()
                nc.vector.tensor_tensor(new[s][:, :, 0:SUMS], new[s][:, :, 0:SUMS], part[:, :, :], ALU.add
                                        ).then_inc(S["new_ready"], 1)
                dve.wait_ge(S["new_ready"], t + 1)

            def step(i):
                for s in two:
                    join(i, s)
                    if second_next(i, s):
                        indices(*second_next(i, s))
                    if ahead(EPAIRS, i, s):
                        state_indices(*ahead(EPAIRS, i, s))
                        front(*ahead(EPAIRS, i, s))
            indices(0, 0)
            indices(0, 1)
            state_indices(0, 0)
            front(0, 0)
            loop_pairs(dve, EPAIRS, step, ch, 14)


def last_layer_out(nc, g):
    PAIRS = g["PAIRS"]
    with Scope(nc, "out4") as sc:
        two = range(2)
        xb = [sc.sb(f"xb{s}", [P, J, D]) for s in two]
        sb_ = [sc.sb(f"state{s}", [P, J, STATE]) for s in two]
        mean_ft = [sc.sb(f"mean_ft{s}", [P, J, D]) for s in two]
        den = sc.sb("den", [P, J, HEADS])
        inv = [sc.sb(f"inv{s}", [P, J, HEADS]) for s in two]
        nn = NodeNorm(nc, sc, g)
        x_in = [sc.sem(f"x_in{s}") for s in two]
        s_in = [sc.sem(f"s_in{s}") for s in two]
        inv_ready, mean_ready = sc.sem("inv_ready"), sc.sem("mean_ready")
        block = sc.block()
        xv, sv = g["chunked"](g["x3_t"]), g["chunked"](g["state_t"])

        @block.sync
        def _(sp):
            def load(i, s):
                m = 2 * i + s
                wait(sp, mean_ready, m - 1)
                sp.dma_start(flat(sb_[s]), g["at"](sv, m)).then_inc(s_in[s], 16)
                wait(sp, nn.u_ready, m - 1)
                sp.dma_start(flat(xb[s]), g["at"](xv, m)).then_inc(x_in[s], 16)

            def step(i):
                for s in two:
                    if ahead(PAIRS, i, s):
                        load(*ahead(PAIRS, i, s))
            load(0, 0)
            loop_pairs(sp, PAIRS, step)

        @block.gpsimd
        def _(pool):
            def step(i):
                for s in two:
                    m = 2 * i + s
                    pool.wait_ge(inv_ready, m + 1)
                    wait(pool, nn.u_ready, m - 1)
                    nc.gpsimd.tensor_tensor(
                        mean_ft[s][:, :, :].rearrange("p j (h f) -> p j h f", h=HEADS),
                        sb_[s][:, :, 0:SUMS].rearrange("p j (h f) -> p j h f", h=HEADS)[:, :, :, 0:HD],
                        inv[s][:, :, :].unsqueeze(3).to_broadcast([P, J, HEADS, HD]), ALU.mult
                        ).then_inc(mean_ready, 1)
            loop_pairs(pool, PAIRS, step)

        @block.scalar
        def _(act):
            def step(i):
                for s in two:
                    nn.root(act, i, s)
                    if behind(i, s):
                        b = behind(i, s)
                        nn.out(act, *b, g["node_rows"](g["out"], 2 * b[0] + b[1], P))
            loop_pairs(act, PAIRS, step)
            nn.out(act, PAIRS - 1, 1, g["node_rows"](g["out"], 2 * PAIRS - 1, g["TAIL_P"]))
            nn.finish(act, PAIRS)

        @block.vector
        def _(dve):
            ch = Chain(dve, nn.step)

            def invert(i, s):
                m = 2 * i + s
                dve.wait_ge(s_in[s], 16 * (i + 1))
                d = sb_[s][:, :, 0:SUMS].rearrange("p j (h f) -> p j h f", h=HEADS)[:, :, :, HD]
                ch.mark(nc.vector.scalar_tensor_tensor(out=den[:, :, :], in0=d, scalar=0.0, in1=d,
                                                       op0=ALU.is_equal, op1=ALU.add))
                ch.sync()
                wait(dve, mean_ready, m - 1)
                nc.vector.reciprocal(inv[s][:, :, :], den[:, :, :]).then_inc(inv_ready, 1)
                dve.wait_ge(inv_ready, m + 1)

            def add(i, s):
                m = 2 * i + s
                dve.wait_ge(mean_ready, m + 1)
                dve.wait_ge(x_in[s], 16 * (i + 1))
                nn.free_u(dve, m)
                nc.vector.scalar_tensor_tensor(out=flat(nn.u[s]), in0=flat(xb[s]), scalar=2.0, in1=flat(mean_ft[s]),
                                               op0=ALU.mult, op1=ALU.add).then_inc(nn.u_ready, 1)

            def step(i):
                for s in two:
                    if ahead(PAIRS, i, s):
                        invert(*ahead(PAIRS, i, s))
                    nn.round(dve, ch, (i, s), behind(i, s), add_u=lambda: add(i, s))
            invert(0, 0)
            loop_pairs(dve, PAIRS, step, ch, 16)
            nn.round(dve, ch, None, (PAIRS - 1, 1))


_INS = ['x', 'src', 'dst', 'edge_attr_64', 'L0_gnn_We', 'L0_gnn_be', 'L0_gnn_W1', 'L0_gnn_b1', 'L0_gnn_g1',
        'L0_gnn_beta1', 'L0_gnn_W2', 'L0_gnn_b2', 'L0_gnn_g2', 'L0_gnn_beta2', 'L0_gnn_eps', 'L1_gnn_W',
        'L2_gnn_W', 'L2_gnn_b', 'L3_gnn_W']


def kernel(**inputs):
    import numpy as _np
    import concourse.bacc as _bacc
    from concourse import mybir as _mybir
    from concourse.bass_utils import run_bass_kernel_spmd as _run

    nc = _bacc.Bacc("TRN2", target_bir_lowering=False, num_devices=1)
    arrays, args = {}, []
    for name in _INS:
        a = _np.ascontiguousarray(inputs[name])
        if name == 'L0_gnn_eps':
            a = a.reshape(1)
        arrays[f"in_{name}_dram"] = a
        args.append(nc.dram_tensor(f"in_{name}_dram", a.shape, _mybir.dt.from_np(a.dtype), kind="ExternalInput").ap())
    args.append(nc.dram_tensor("out_0_dram", tuple(inputs['x'].shape), _mybir.dt.float32, kind="ExternalOutput").ap())
    gnn_kernel(nc, *args)
    r = _run(nc, [arrays], core_ids=[0])
    return r.results[0]["out_0_dram"]
```

```python
import concourse.bass as bass
from concourse import mybir
from contextlib import ExitStack

FP32 = mybir.dt.float32
BF16 = mybir.dt.bfloat16
I32 = mybir.dt.int32
ALU = mybir.AluOpType
ACT = mybir.ActivationFunctionType
AXX = mybir.AxisListType.X

P = 128
D = 128
J = 8
CHUNK = P * J
W = J * D
HALF = W // 2
GROUP = 2 * P
HEADS = 4
HD = D // HEADS
HS = HD + 1
SUMS = HEADS * HS
STATE = SUMS + HEADS
EPS = 1e-5
LOWEST = -3.0e38
STEP = 14
LOADS = 7
STORE_LAG = 5
LEAD = 4
ACT_ROWS = 7


def wait(eng, sem, value):
    if isinstance(value, int) and value <= 0:
        return
    eng.wait_ge(sem, value)


class Chain:

    def __init__(self, eng, sem):
        self.eng, self.sem, self.base, self.k = eng, sem, 0, 0

    def mark(self, ins):
        self.k += 1
        ins.then_inc(self.sem, 1)
        return self.base + self.k

    def after(self, ticket):
        self.eng.wait_ge(self.sem, ticket)

    def sync(self):
        self.eng.wait_ge(self.sem, self.base + self.k)

    def enter(self, i, start, per):
        self.fixed = self.base + self.k
        self.base, self.k, self.start, self.per = i * per + (self.fixed - start * per), 0, start, per

    def leave(self, count):
        assert self.k == self.per, f"this loop's body marks {self.k}"
        self.base, self.k = self.fixed + count * self.per, 0


def loop(eng, turns, body, chain=None, per=0):
    body(0)
    with eng.Fori(1, turns - 1) as i:
        if chain:
            chain.enter(i, 1, per)
        body(i)
    if chain:
        chain.leave(turns - 2)
    body(turns - 1)



def slot_turn(i, k, slots=LOADS):
    return STEP // slots * i + k // slots


def loop_chunks(eng, chunks, body, chain=None, per=0):
    def step(i):
        for k in range(STEP):
            body(i, k)
    loop(eng, chunks // STEP, step, chain, per * STEP)


def later(chunks, i, k, n):
    if k + n < STEP:
        return i, k + n
    return None if isinstance(i, int) and i == chunks // STEP - 1 else (i + 1, k + n - STEP)


def next_chunk(chunks, i, k):
    return later(chunks, i, k, 1)


def earlier(i, k, n):
    if k >= n:
        return i, k - n
    return None if isinstance(i, int) and i == 0 else (i - 1, STEP + k - n)


def chunk_before(i, k):
    return earlier(i, k, 1)


def gnn_kernel(nc, x, src, dst, edge_attr, We, be, W1, b1, g1, beta1, W2, b2, g2, beta2, eps,
               WL1, WL2, bL2, WL3, out):
    N = x.shape[0]
    E = src.shape[0]
    DE = edge_attr.shape[1]
    CHUNKS = -(-N // CHUNK)
    TAIL_P = (N - (CHUNKS - 1) * CHUNK) // J
    PAIRS = CHUNKS // 2
    LAST = (CHUNKS // STEP - 1, STEP - 1)
    NPAD = CHUNKS * CHUNK
    EDGE_COLS = -(-E // (4 * P)) * 4
    FULL_P = E // EDGE_COLS
    REM = E - FULL_P * EDGE_COLS
    GROUPS = EDGE_COLS // 2
    EPAIRS = GROUPS // 2
    NCOLS = CHUNKS * J
    assert CHUNKS % 2 == 0 and (N - (CHUNKS - 1) * CHUNK) % J == 0 and N + GROUP < NPAD
    assert CHUNKS % STEP == 0 and CHUNKS // STEP > 2 and GROUPS % STEP == 0 and EPAIRS > 2 and GROUPS >= CHUNKS

    ctx = ExitStack()

    def sb(name, shape, dt=FP32):
        return ctx.enter_context(nc.sbuf_tensor(name, shape, dt))

    def dram(name, cols):
        return nc.dram_tensor(name, (NPAD, cols), FP32, kind="Internal").ap()

    h_t, agg1, agg2 = dram("h", D), dram("agg1", D), dram("agg2", D)
    z2_t = nc.dram_tensor("z2_t", (CHUNKS, P, W), FP32, kind="Internal").ap()
    x1n_t, x2_t, x3_t = dram("x1n", D), dram("x2", D), dram("x3", D)
    state_t = dram("state", STATE)

    def chunked(table, rows=P):
        return table.rearrange("(m p j) f -> m p (j f)", p=P, j=J)

    def at(view, m, rows=P):
        if isinstance(m, int):
            return view[m, 0:rows, :]
        return view[bass.ds(m, 1), 0:rows, :].rearrange("a p f -> (a p) f")

    def node_rows(table, m, rows=P):
        if isinstance(m, int):
            v = table[m * CHUNK:m * CHUNK + rows * J, :]
            return v.rearrange("(p j) f -> p (j f)", j=J)
        body = table[0:(CHUNKS - 1) * CHUNK, :].rearrange("(m p j) f -> m p (j f)", p=P, j=J)
        return body[bass.ds(m, 1), :, :].rearrange("a p f -> (a p) f")

    def rows_of(m):
        return TAIL_P if isinstance(m, int) and m == CHUNKS - 1 else P

    with ctx:
        ident = sb("ident", [P, P])
        ones_col = sb("ones_col", [P, 1])
        eps_col = sb("eps_col", [P, 1])
        gin_scale = sb("gin_scale", [P, 1])
        WeT = sb("WeT", [DE + 1, D])
        W1T = sb("W1T", [P, 2 * D])
        W2T = sb("W2T", [P, 2, D])
        WLT = [sb(f"WLT{n}", [P, D]) for n in range(3)]
        b1c, g1c, beta1c = (sb(n, [P, 2]) for n in ("b1c", "g1c", "beta1c"))
        b2c, g2c, beta2c = (sb(n, [P, 1]) for n in ("b2c", "g2c", "beta2c"))
        bL2_all = sb("bL2_all", [P, D])
        keys = sb("keys", [P, 2 * EDGE_COLS])
        index = sb("index", [P, GROUPS, 4, 2], I32)
        lo_digit = sb("lo_digit", [P, EDGE_COLS])
        hi_digit = sb("hi_digit", [P, EDGE_COLS])
        deg1 = sb("deg1", [P, NCOLS])
        norm = sb("norm", [P, NCOLS])
        norm2 = sb("norm2", [P, NCOLS])
        a1, t1 = sb("a1", [P, 2]), sb("t1", [P, 2])
        a2, t2 = sb("a2", [P, 1]), sb("t2", [P, 1])
        moments = sb("moments", [P, D + 1])

        prepare(nc, locals())
        degrees_and_first_sum(nc, locals())
        first_norm(nc, locals())
        mlp(nc, locals())
        first_layer_out(nc, locals())
        aggregate(nc, locals(), "l1", x1n_t, agg1, EDGE_COLS, 1, 0, clear_state=True)
        convolve(nc, locals(), "l1", x1n_t, agg1, x2_t, WLT[0])
        aggregate(nc, locals(), "l2", x2_t, agg2, 0, 2, 3)
        convolve(nc, locals(), "l2", x2_t, agg2, x3_t, WLT[1])
        attention(nc, locals())
        last_layer_out(nc, locals())


class Turns:

    def __init__(self, eng, name):
        self.eng = eng
        self.count = eng.alloc_register(name)
        eng.reg_mov(self.count, 1)

    def wait(self, sem, t):
        self.eng.wait_ge(sem, t + 1 if isinstance(t, int) else self.count)
        self.eng.reg_add(self.count, self.count, 1)


class Scope:

    def __init__(self, nc, tag):
        self.nc, self.tag, self.ctx, self.sems = nc, tag, ExitStack(), []

    def __enter__(self):
        self.ctx.__enter__()
        return self

    def __exit__(self, *e):
        self.ctx.__exit__(*e)
        self.nc.clear_and_free_semaphores(self.sems)
        self.nc.all_engine_barrier()

    def sb(self, name, shape, dt=FP32):
        return self.ctx.enter_context(self.nc.sbuf_tensor(f"{self.tag}_{name}", shape, dt))

    def ps(self, name, shape, dt=FP32):
        return self.ctx.enter_context(self.nc.psum_tensor(f"{self.tag}_{name}", shape, dt))

    def sem(self, name):
        self.sems.append(self.nc.alloc_semaphore(f"{self.tag}_{name}"))
        return self.sems[-1]

    def block(self):
        return self.ctx.enter_context(self.nc.Block())


def prepare(nc, g):
    N, E, DE = g["N"], g["E"], g["DE"]
    EC, GROUPS, FULL_P, REM, CHUNKS = g["EDGE_COLS"], g["GROUPS"], g["FULL_P"], g["REM"], g["CHUNKS"]
    keys, index, ident = g["keys"], g["index"], g["ident"]
    with Scope(nc, "prep") as sc:
        w1 = sc.sb("w1", [P, 2, D])
        w2 = sc.sb("w2", [P, 2, D])
        we = sc.sb("we", [P, DE])
        wl = [sc.sb(f"wl{n}", [P, D]) for n in range(3)]
        xb = [sc.sb(f"xb{l}", [P, W]) for l in range(LOADS)]
        hb = [sc.sb(f"hb{s}", [P, W]) for s in range(2)]
        raw = sc.sb("raw", [P, 2, EC], I32)
        no_edge = sc.sb("no_edge", [P, EC])
        later_mask = sc.sb("later_mask", [P, 2, GROUP])
        spare = sc.sb("spare", [P, 2 * GROUPS, 2])
        later = sc.sb("later", [P, 2 * EC])
        own = sc.sb("own", [P, 2 * EC])
        key_int = sc.sb("key_int", [P, 2, EC], I32)
        digit = sc.sb("digit", [P, 4, EC], I32)
        keyb = [sc.sb(f"keyb{s}", [P, 2, P]) for s in range(2)]
        mark = [sc.sb(f"mark{s}", [P, 2, GROUP]) for s in range(2)]
        wps = sc.ps("wps", [P, 8, 512])
        pwt = [wps[:, b, 0:P] for b in range(6)]
        key_rows = [wps[:, 6 + s, 0:GROUP] for s in range(2)]
        params_in, edges_in, h_ready, scale_ready = (
            sc.sem(n) for n in ("params_in", "edges_in", "h_ready", "scale_ready"))
        x_in = [sc.sem(f"x_in{l}") for l in range(LOADS)]
        stored = [sc.sem(f"stored{s}") for s in range(2)]
        raw_ready, consts_ready, pool_step = (sc.sem(n) for n in ("raw_ready", "consts_ready", "pool_step"))
        dve_step, wt_ready, keyb_ready, rows_ready, marked = (
            sc.sem(n) for n in ("dve_step", "wt_ready", "keyb_ready", "rows_ready", "marked"))
        block = sc.block()
        NPARAM = 16

        @block.sync
        def _(sp):
            with nc.allow_non_contiguous_dma(reason="parameter vectors as columns"):
                sp.dma_start(w1[:, :, :], g["W1"].rearrange("(b p) f -> p b f", p=P)).then_inc(params_in, 16)
                sp.dma_start(w2[:, :, :], g["W2"].rearrange("p (b f) -> p b f", b=2)).then_inc(params_in, 16)
                sp.dma_start(we[:, :], g["We"]).then_inc(params_in, 16)
                for n, name in enumerate(("WL1", "WL2", "WL3")):
                    sp.dma_start(wl[n][:, :], g[name]).then_inc(params_in, 16)
                sp.dma_start(g["WeT"][DE:DE + 1, :], g["be"][None, :]).then_inc(params_in, 16)
                for col, vec in (("b1c", "b1"), ("g1c", "g1"), ("beta1c", "beta1")):
                    sp.dma_start(g[col][:, :], g[vec].rearrange("(b p) -> p b", p=P)).then_inc(params_in, 16)
                for col, vec in (("b2c", "b2"), ("g2c", "g2"), ("beta2c", "beta2")):
                    sp.dma_start(g[col][:, :], g[vec].rearrange("(p b) -> p b", b=1)).then_inc(params_in, 16)
                sp.dma_start(g["bL2_all"][:, :], g["bL2"][None, :].to_broadcast([P, D])).then_inc(params_in, 16)
                sp.dma_start(g["gin_scale"][:, :], g["eps"][None, :].to_broadcast([P, 1])).then_inc(params_in, 16)
                sp.wait_ge(raw_ready, 1)
                for n, name in enumerate(("dst", "src")):
                    v = g[name]
                    sp.dma_start(raw[0:FULL_P, n, :],
                                 v[0:FULL_P * EC].rearrange("(p k) -> p k", k=EC)).then_inc(edges_in, 16)
                    sp.dma_start(raw[FULL_P:FULL_P + 1, n, 0:REM],
                                 v[FULL_P * EC:E][None, :]).then_inc(edges_in, 16)

            def load(i, k):
                m, l = STEP * i + k, k % LOADS
                r = g["rows_of"](m)
                wait(sp, h_ready, m - LOADS + 1)
                sp.dma_start(xb[l][0:r, :], g["node_rows"](g["x"], m, r)).then_inc(x_in[l], 16)
            loop_chunks(sp, CHUNKS, load)

        @block.scalar
        def _(act):
            h_v = g["chunked"](g["h_t"])
            act.wait_ge(scale_ready, 1)

            def scale(i, k):
                m, s, l = STEP * i + k, k % 2, k % LOADS
                act.wait_ge(x_in[l], 16 * (slot_turn(i, k) + 1))
                wait(act, stored[s], 16 * slot_turn(i, k, 2))
                nc.scalar.mul(hb[s][:, :], xb[l][:, :], g["gin_scale"][:, 0:1]).then_inc(h_ready, 1)
                act.wait_ge(h_ready, m + 1)
                act.dma_start(g["at"](h_v, m), hb[s][:, :]).then_inc(stored[s], 16)
            loop_chunks(act, CHUNKS, scale)
            for s in range(2):
                act.wait_ge(stored[s], 8 * CHUNKS)

        @block.gpsimd
        def _(pool):
            nc.gpsimd.memset(raw[:, :, :], 0).then_inc(raw_ready, 1)
            nc.gpsimd.memset(g["ones_col"][:, :], 1.0)
            nc.gpsimd.memset(g["eps_col"][:, :], EPS)
            nc.gpsimd.memset(ident[:, :], 1.0)
            nc.gpsimd.memset(later_mask[:, :, :], 1.0)
            nc.gpsimd.memset(no_edge[:, :], float(N)).then_inc(pool_step, 1)
            pool.wait_ge(pool_step, 1)
            nc.gpsimd.affine_select(out=ident[:, :], in_=ident[:, :], compare_op=ALU.is_equal, fill=0.0,
                                    base=0, pattern=[[-1, P]], channel_multiplier=1)
            nc.gpsimd.affine_select(out=later_mask[:, :, :], in_=later_mask[:, :, :], compare_op=ALU.is_gt,
                                    fill=0.0, base=0, pattern=[[-P, 2], [1, GROUP]], channel_multiplier=-1)
            nc.gpsimd.affine_select(out=no_edge[:, :], in_=no_edge[:, :], compare_op=ALU.is_ge, fill=0.0,
                                    base=-E, pattern=[[1, EC]], channel_multiplier=EC)
            nc.gpsimd.iota(spare[:, :, :], pattern=[[0, 2 * GROUPS], [P, 2]], base=N + 1, channel_multiplier=1,
                           allow_small_or_imprecise_dtypes=True).then_inc(consts_ready, 1)

        @block.tensor
        def _(pe):
            pe.wait_ge(consts_ready, 1)
            pe.wait_ge(params_in, 16 * (NPARAM - 1))
            wide = [w1[:, 0, :], w1[:, 1, :], w2[:, 0, :], w2[:, 1, :]]
            for b, w in enumerate(wide):
                last = nc.tensor.transpose(pwt[b], w, ident[:, :])
            for n in range(2):
                last = nc.tensor.transpose(pwt[4 + n], wl[n][:, :], ident[:, :])
            last = nc.tensor.transpose(wps[:, 4, P:2 * P], wl[2][:, :], ident[:, :])
            last = nc.tensor.transpose(wps[0:DE, 5, P:2 * P], we[:, :], ident[:, :])
            last.then_inc(wt_ready, 1)
            def rows(i):
                for s in range(2):
                    q = 2 * i + s
                    pe.wait_ge(keyb_ready, q + 1)
                    wait(pe, marked, q - 1)
                    for c in range(2):
                        last = nc.tensor.matmul(key_rows[s][:, c * P:(c + 1) * P], keyb[s][:, c, :],
                                                ident[:, :], start=True, stop=True)
                    last.then_inc(rows_ready, 1)
            loop(pe, GROUPS, rows)

        @block.vector
        def _(dve):
            ch = Chain(dve, dve_step)
            dve.wait_ge(params_in, 16 * (NPARAM - 1))
            nc.vector.tensor_scalar(g["gin_scale"][:, :], g["gin_scale"][:, :], 1.0, None, ALU.add
                                    ).then_inc(scale_ready, 1)
            dve.wait_ge(wt_ready, 1)
            nc.vector.tensor_copy(g["W1T"][:, 0:D], pwt[0])
            nc.vector.tensor_copy(g["W1T"][:, D:2 * D], pwt[1])
            nc.vector.tensor_copy(g["W2T"][:, 0, :], pwt[2])
            nc.vector.tensor_copy(g["W2T"][:, 1, :], pwt[3])
            nc.vector.tensor_copy(g["WLT"][0][:, :], pwt[4])
            nc.vector.tensor_copy(g["WLT"][1][:, :], pwt[5])
            nc.vector.tensor_copy(g["WLT"][2][:, :], wps[:, 4, P:2 * P])
            nc.vector.tensor_copy(g["WeT"][0:DE, :], wps[0:DE, 5, P:2 * P])
            dve.wait_ge(edges_in, 64)
            dve.wait_ge(consts_ready, 1)
            for n in range(2):
                ch.mark(nc.vector.tensor_copy(keys[:, n * EC:(n + 1) * EC], raw[:, n, :]))
            ch.sync()
            for n in range(2):
                ch.mark(nc.vector.tensor_tensor(keys[:, n * EC:(n + 1) * EC], keys[:, n * EC:(n + 1) * EC],
                                                no_edge[:, :], ALU.add))
            ch.sync()
            ch.mark(nc.vector.tensor_copy(key_int[:, 1, :], keys[:, EC:2 * EC]))
            ch.sync()
            src_int = key_int[:, 1, :]
            ch.mark(nc.vector.tensor_scalar(digit[:, 0, :], src_int, 3, P - 1, ALU.logical_shift_right,
                                            ALU.bitwise_and))
            ch.mark(nc.vector.tensor_scalar(digit[:, 1, :], src_int, 10, 3, ALU.logical_shift_right,
                                            ALU.logical_shift_left))
            ch.mark(nc.vector.tensor_scalar(digit[:, 2, :], src_int, J - 1, None, ALU.bitwise_and))
            ch.sync()
            ch.mark(nc.vector.tensor_copy(g["lo_digit"][:, :], digit[:, 0, :]))
            ch.mark(nc.vector.tensor_tensor(g["hi_digit"][:, :], digit[:, 1, :], digit[:, 2, :], ALU.add))

            def spread(q, s):
                wait(dve, marked, q - 1)
                nc.vector.tensor_scalar(keyb[s][:, :, :],
                                        keys[:, bass.ds(2 * q, 2)].unsqueeze(2).to_broadcast([P, 2, P]), 1.0, None,
                                        ALU.mult).then_inc(keyb_ready, 1)

            def count(i):
                for s in range(2):
                    q = 2 * i + s
                    if s == 0 or not (isinstance(i, int) and i == GROUPS - 1):
                        spread(q + 1, 1 - s)
                    dve.wait_ge(rows_ready, q + 1)
                    for c in range(2):
                        last = nc.vector.scalar_tensor_tensor(
                            out=mark[s][:, c, :], in0=key_rows[s], scalar=keyb[s][:, c, 0:1],
                            in1=later_mask[:, c, :], op0=ALU.is_equal, op1=ALU.mult,
                            accum_out=later[:, bass.ds(2 * q + c, 1)])
                    last.then_inc(marked, 1)
            spread(0, 0)
            loop(dve, GROUPS, count)
            dve.wait_ge(marked, 2 * GROUPS)
            spare_flat = spare[:, :, :].rearrange("p q c -> p (q c)")
            ch.mark(nc.vector.tensor_scalar(later[:, :], later[:, :], 1.0, None, ALU.min))
            ch.mark(nc.vector.tensor_tensor(own[:, :], spare_flat, keys[:, :], ALU.subtract))
            ch.sync()
            ch.mark(nc.vector.tensor_tensor(own[:, :], own[:, :], later[:, :], ALU.mult))
            ch.sync()
            ch.mark(nc.vector.tensor_tensor(own[:, :], own[:, :], keys[:, :], ALU.add))
            ch.sync()
            own_v = own[:, :].rearrange("p (n q c) -> p n q c", n=2, c=2)
            raw_v = raw[:, :, :].rearrange("p n (q c) -> p n q c", c=2)
            nc.vector.tensor_copy(index[:, :, 0, :], own_v[:, 1, :, :])
            nc.vector.tensor_copy(index[:, :, 1, :], raw_v[:, 0, :, :])
            nc.vector.tensor_copy(index[:, :, 2, :], raw_v[:, 1, :, :])
            nc.vector.tensor_copy(index[:, :, 3, :], own_v[:, 0, :, :])


def clear_tables(sp, g, tables, cleared, pace, pairs):
    def clear(i):
        for s in range(2):
            m = 2 * i + s
            wait(sp, pace, m - 1)
            for table, value in tables:
                sp.dma_start(g["at"](g["chunked"](table), m), value).then_inc(cleared, 16)
    loop(sp, pairs, clear)
    sp.wait_ge(cleared, 16 * len(tables) * 2 * pairs)


def slot_step(i, s, ahead):
    return i + (s + ahead) // 2, (s + ahead) % 2


def degrees_and_first_sum(nc, g):
    DE, EC, GROUPS, EPAIRS = g["DE"], g["EDGE_COLS"], g["GROUPS"], g["EPAIRS"]
    FULL_P, REM, E, NCOLS = g["FULL_P"], g["REM"], g["E"], g["NCOLS"]
    keys, index, ident, x, h_t = g["keys"], g["index"], g["ident"], g["x"], g["h_t"]
    with Scope(nc, "l0") as sc:
        two = range(2)
        zero = sc.sb("zero", [P, W])
        attr = sc.sb("attr", [P, EC, DE])
        columns = sc.sb("columns", [P, max(NCOLS, P)])
        gi = [sc.sb(f"gi{r}", [P, 2], I32) for r in range(LOADS)]
        oi = [sc.sb(f"oi{s}", [P, 2], I32) for s in two]
        keyb = [sc.sb(f"keyb{s}", [P, 2, P]) for s in two]
        eq = [sc.sb(f"eq{s}", [P, 2, GROUP]) for s in two]
        rows = [sc.sb(f"rows{r}", [P, 2, D]) for r in range(LOADS)]
        sums = [sc.sb(f"sums{s}", [P, 2, D]) for s in two]
        attr_now = [sc.sb(f"attr_now{s}", [P, 2 * DE + P - DE]) for s in two]
        attrT = [sc.sb(f"attrT{s}", [DE + 1, 2, P]) for s in two]
        msg = [sc.sb(f"msg{s}", [P, 2, D]) for s in two]
        hot_lo = [sc.sb(f"hot_lo{s}", [P, 2, P], BF16) for s in two]
        hot_hi = [sc.sb(f"hot_hi{s}", [P, 2, NCOLS], BF16) for s in two]
        p_keys = sc.ps("p_keys", [P, 512])
        p_attr = sc.ps("p_attr", [P, 512])
        p_sums = [sc.ps(f"p_sums{s}", [P, 512]) for s in two]
        p_msg = [sc.ps(f"p_msg{s}", [P, 512]) for s in two]
        p_deg = sc.ps("p_deg", [P, 2, 512])
        arrived = [sc.sem(f"arrived{r}") for r in range(LOADS)]
        attr_in, cols_ready, attr_zero, zero_ready, added, cleared = (
            sc.sem(n) for n in ("attr_in", "cols_ready", "attr_zero", "zero_ready", "added", "cleared"))
        gi_ready, oi_ready, keyb_ready, rows_ready, eq_ready = (
            sc.sem(n) for n in ("gi_ready", "oi_ready", "keyb_ready", "rows_ready", "eq_ready"))
        attr_now_ready, attrT_psum, attrT_ready, msg_psum, attrT_used, msg_ready = (
            sc.sem(n) for n in ("attr_now_ready", "attrT_psum", "attrT_ready", "msg_psum", "attrT_used", "msg_ready"))
        summed, sums_ready, hot_ready, hot_used, ones_ready, deg_ready, sq_ready = (
            sc.sem(n) for n in ("summed", "sums_ready", "hot_ready", "hot_used", "ones_ready", "deg_ready", "sq_ready"))
        block = sc.block()
        HI2 = NCOLS - 512 if NCOLS > 512 else 0

        @block.sync
        def _(sp):
            sp.wait_ge(attr_zero, 1)
            ea = g["edge_attr"]
            sp.dma_start(attr[0:FULL_P, :, :],
                         ea[0:FULL_P * EC, :].rearrange("(p k) f -> p k f", k=EC)).then_inc(attr_in, 16)
            sp.dma_start(attr[FULL_P:FULL_P + 1, 0:REM, :], ea[FULL_P * EC:E, :][None, :, :]).then_inc(attr_in, 16)
            clear_tables(sp, g, [(g["agg1"], zero[:, :])], cleared, summed, g["PAIRS"])

        @block.gpsimd
        def _(pool):
            nc.gpsimd.memset(zero[:, :], 0.0).then_inc(zero_ready, 1)
            pool.wait_ge(zero_ready, 1)
            nc.gpsimd.memset(attr[96:P, :, :], 0.0).then_inc(attr_zero, 1)
            pool.wait_ge(attr_zero, 1)
            nc.gpsimd.iota(columns[:, :], pattern=[[1, max(NCOLS, P)]], base=0, channel_multiplier=0,
                           allow_small_or_imprecise_dtypes=True).then_inc(cols_ready, 1)
            gathers, scatters = Turns(pool, sc.tag + "_gathers"), Turns(pool, sc.tag + "_scatters")

            def gather(i, k):
                t, r = STEP * i + k, k % LOADS
                wait(pool, msg_psum, t - LOADS + 1)
                gathers.wait(gi_ready, t)
                for c in two:
                    pool.indirect_dma_start(rows[r][:, c, :], None, x,
                                            bass.IndirectOffsetOnAxis(ap=gi[r][:, c:c + 1], axis=0)
                                            ).then_inc(arrived[r], 16)

            def step(i, k):
                t, s = STEP * i + k, k % 2
                if later(GROUPS, i, k, LEAD):
                    gather(*later(GROUPS, i, k, LEAD))
                pool.wait_ge(oi_ready, t + 1)
                wait(pool, added, 32 * t)
                scatters.wait(sums_ready, t)
                for c in two:
                    pool.indirect_dma_start(h_t, bass.IndirectOffsetOnAxis(ap=oi[s][:, c:c + 1], axis=0),
                                            sums[s][:, c, :], None, compute_op=ALU.add).then_inc(added, 16)
            for k in range(LEAD):
                gather(0, k)
            loop_chunks(pool, GROUPS, step)
            pool.wait_ge(added, 32 * GROUPS)

        @block.tensor
        def _(pe):
            def front(i, k):
                t, s = STEP * i + k, k % 2
                pe.wait_ge(keyb_ready, t + 1)
                wait(pe, eq_ready, t)
                for c in two:
                    last = nc.tensor.matmul(p_keys[:, c * P:(c + 1) * P], keyb[s][:, c, :], ident[:, :],
                                            start=True, stop=True)
                last.then_inc(rows_ready, 1)
                pe.wait_ge(attr_now_ready, t + 1)
                wait(pe, attrT_ready, t)
                for c in two:
                    last = nc.tensor.transpose(p_attr[:, c * P:(c + 1) * P], attr_now[s][:, c * DE:c * DE + P],
                                               ident[:, :])
                last.then_inc(attrT_psum, 1)

            def project(i, k):
                t, s = STEP * i + k, k % 2
                pe.wait_ge(attrT_ready, t + 1)
                wait(pe, msg_ready, t - 1)
                for c in two:
                    last = nc.tensor.matmul(p_msg[s][:, c * D:(c + 1) * D], attrT[s][:, c, :], g["WeT"][:, :],
                                            start=(c == 0), stop=False, skip_group_check=True)
                last.then_inc(attrT_used, 1)

            def step(i, k):
                t, s, r = STEP * i + k, k % 2, k % LOADS
                if next_chunk(GROUPS, i, k):
                    front(*next_chunk(GROUPS, i, k))
                pe.wait_ge(arrived[r], 32 * (slot_turn(i, k) + 1))
                last = nc.tensor.matmul(p_msg[s][:, 0:2 * D], ident[:, :], flat(rows[r]), start=False, stop=True,
                                        skip_group_check=True)
                last.then_inc(msg_psum, 1)
                pe.wait_ge(hot_ready, t + 1)
                for c in two:
                    first = isinstance(i, int) and t == 0 and c == 0
                    final = isinstance(i, int) and t == GROUPS - 1 and c == 1
                    last = nc.tensor.matmul(p_deg[:, 0, 0:min(NCOLS, 512)], hot_lo[s][:, c, :],
                                            hot_hi[s][:, c, 0:min(NCOLS, 512)], start=first, stop=final)
                    if HI2:
                        last = nc.tensor.matmul(p_deg[:, 1, 0:HI2], hot_lo[s][:, c, :],
                                                hot_hi[s][:, c, 512:NCOLS], start=first, stop=final)
                last.then_inc(hot_used, 1)
                pe.wait_ge(eq_ready, t + 1)
                pe.wait_ge(msg_ready, t + 1)
                wait(pe, sums_ready, t - 1)
                for c in two:
                    for n in two:
                        last = nc.tensor.matmul(p_sums[s][:, c * D:(c + 1) * D], eq[s][:, n, c * P:(c + 1) * P],
                                                msg[s][:, n, :], start=(n == 0), stop=(n == 1))
                last.then_inc(summed, 1)
                if next_chunk(GROUPS, i, k):
                    project(*next_chunk(GROUPS, i, k))
            pe.wait_ge(ones_ready, 1)
            front(0, 0)
            project(0, 0)
            loop_chunks(pe, GROUPS, step)

        @block.scalar
        def _(act):
            def pick(i, k):
                t, s = STEP * i + k, k % 2
                wait(act, attrT_psum, t - 1)
                nc.scalar.copy(attr_now[s][:, 0:2 * DE].rearrange("p (c f) -> p c f", c=2),
                               attr[:, bass.ds(2 * t, 2), :]).then_inc(attr_now_ready, 1)

            def evacuate(i, k):
                t, s = STEP * i + k, k % 2
                act.wait_ge(attrT_psum, t + 1)
                wait(act, attrT_used, t - 1)
                nc.scalar.copy(attrT[s][0:DE, :, :].rearrange("p c e -> p (c e)"), p_attr[0:DE, 0:GROUP]
                               ).then_inc(attrT_ready, 1)

            def step(i, k):
                t, s = STEP * i + k, k % 2
                if next_chunk(GROUPS, i, k):
                    pick(*next_chunk(GROUPS, i, k))
                    evacuate(*next_chunk(GROUPS, i, k))
                act.wait_ge(msg_psum, t + 1)
                wait(act, summed, t - 1)
                nc.scalar.activation(flat(msg[s]), p_msg[s][:, 0:2 * D], ACT.Relu).then_inc(msg_ready, 1)
                act.wait_ge(summed, t + 1)
                wait(act, added, 32 * (t - 1))
                nc.scalar.copy(sums[s][:, :, :].rearrange("p c f -> p (c f)"), p_sums[s][:, 0:2 * D]
                               ).then_inc(sums_ready, 1)
            act.wait_ge(attr_in, 32)
            pick(0, 0)
            evacuate(0, 0)
            loop_chunks(act, GROUPS, step)
            act.wait_ge(deg_ready, 1)
            nc.scalar.activation(g["norm"][:, :], g["deg1"][:, :], ACT.Sqrt).then_inc(sq_ready, 1)

        @block.vector
        def _(dve):
            for s in two:
                nc.vector.memset(attr_now[s][:, 2 * DE:DE + P], 0.0)
                last = nc.vector.memset(attrT[s][DE:DE + 1, :, :], 1.0)
            last.then_inc(ones_ready, 1)
            dve.wait_ge(cols_ready, 1)

            def gather_index(i, k):
                t, r = STEP * i + k, k % LOADS
                wait(dve, arrived[r], 32 * slot_turn(i, k))
                nc.vector.tensor_scalar(gi[r][:, :], index[:, bass.ds(t, 1), 2, :].rearrange("p a c -> p (a c)"),
                                        1.0, None, ALU.mult
                                      ).then_inc(gi_ready, 1)

            def spread_keys(i, k):
                t, s = STEP * i + k, k % 2
                wait(dve, eq_ready, t - 1)
                nc.vector.tensor_copy(keyb[s][:, :, :],
                                      keys[:, bass.ds(2 * t, 2)].unsqueeze(2).to_broadcast([P, 2, P])
                                      ).then_inc(keyb_ready, 1)

            def step(i, k):
                t, s = STEP * i + k, k % 2
                if later(GROUPS, i, k, LEAD):
                    gather_index(*later(GROUPS, i, k, LEAD))
                if next_chunk(GROUPS, i, k):
                    spread_keys(*next_chunk(GROUPS, i, k))
                dve.wait_ge(rows_ready, t + 1)
                wait(dve, summed, t - 1)
                for c in two:
                    last = nc.vector.tensor_scalar(eq[s][:, c, :], p_keys[:, 0:GROUP], keyb[s][:, c, 0:1], None,
                                                   ALU.is_equal)
                last.then_inc(eq_ready, 1)
                wait(dve, added, 32 * (t - 1))
                nc.vector.tensor_scalar(oi[s][:, :], index[:, bass.ds(t, 1), 3, :].rearrange("p a c -> p (a c)"),
                                        1.0, None, ALU.mult
                                      ).then_inc(oi_ready, 1)
                wait(dve, hot_used, t - 1)
                for c in two:
                    nc.vector.tensor_scalar(hot_lo[s][:, c, :], columns[:, 0:P],
                                            g["lo_digit"][:, bass.ds(2 * t + c, 1)], None, ALU.is_equal)
                    last = nc.vector.tensor_scalar(hot_hi[s][:, c, :], columns[:, 0:NCOLS],
                                                   g["hi_digit"][:, bass.ds(2 * t + c, 1)], None, ALU.is_equal)
                last.then_inc(hot_ready, 1)
            for k in range(LEAD):
                gather_index(0, k)
            spread_keys(0, 0)
            loop_chunks(dve, GROUPS, step)
            dve.wait_ge(hot_used, GROUPS)
            last = nc.vector.tensor_scalar(g["deg1"][:, 0:min(NCOLS, 512)], p_deg[:, 0, 0:min(NCOLS, 512)], 1.0, None,
                                           ALU.add)
            if HI2:
                last = nc.vector.tensor_scalar(g["deg1"][:, 512:NCOLS], p_deg[:, 1, 0:HI2], 1.0, None, ALU.add)
            last.then_inc(deg_ready, 1)
            dve.wait_ge(sq_ready, 1)
            nc.vector.reciprocal(g["norm"][:, :], g["norm"][:, :])
            nc.vector.reciprocal(g["norm2"][:, :], g["deg1"][:, :])


def first_norm(nc, g):
    N, CHUNKS = g["N"], g["CHUNKS"]
    moments, W1T = g["moments"], g["W1T"]
    with Scope(nc, "bn1") as sc:
        two, slots = range(2), range(LOADS)
        hb = [sc.sb(f"hb{s}", [P, J, D]) for s in slots]
        hsum = [sc.sb(f"hsum{s}", [P, D]) for s in slots]
        mrow = sc.sb("mrow", [1, D])
        cov = sc.sb("cov", [P, D])
        prod = sc.sb("prod", [P, 2 * D])
        mean_z, var_z, std_z = (sc.sb(n, [P, 2]) for n in ("mean_z", "var_z", "std_z"))
        p_mom = sc.ps("p_mom", [P, 512])
        p_mean = sc.ps("p_mean", [P, 512])
        p_small = sc.ps("p_small", [P, 512])
        p_prod = sc.ps("p_prod", [P, 512])
        p_row = sc.ps("p_row", [1, 512])
        p_out = sc.ps("p_out", [P, 512])
        p_var = sc.ps("p_var", [P, 512])
        h_in = [sc.sem(f"h_in{s}") for s in slots]
        hsum_ready, h_used, dve_step, pe_step, std_ready = (
            sc.sem(n) for n in ("hsum_ready", "h_used", "dve_step", "pe_step", "std_ready"))
        block = sc.block()
        aggv = g["chunked"](g["h_t"])

        @block.sync
        def _(sp):
            def load(i, k):
                m, s = STEP * i + k, k % LOADS
                wait(sp, hsum_ready, m - LOADS + 1)
                wait(sp, h_used, m - LOADS + 1)
                sp.dma_start(flat(hb[s]), g["at"](aggv, m)).then_inc(h_in[s], 16)
            loop_chunks(sp, CHUNKS, load)

        @block.vector
        def _(dve):
            def add(i, k):
                m, s = STEP * i + k, k % LOADS
                dve.wait_ge(h_in[s], 16 * (slot_turn(i, k) + 1))
                wait(dve, h_used, m - LOADS + 1)
                nc.vector.tensor_reduce(hsum[s][:, :], hb[s][:, :, :].rearrange("p j f -> p f j"), AXX, ALU.add
                                        ).then_inc(hsum_ready, 1)
            loop_chunks(dve, CHUNKS, add)
            ch = Chain(dve, dve_step)
            dve.wait_ge(h_used, CHUNKS)
            nc.vector.tensor_scalar(moments[:, 0:D], p_mom[:, 0:D], 1.0 / N, None, ALU.mult)
            ch.mark(nc.vector.tensor_scalar(moments[:, D:D + 1], p_mean[:, 0:1], 1.0 / N, None, ALU.mult))
            dve.wait_ge(pe_step, 1)
            ch.mark(nc.vector.tensor_copy(mrow[:, :], p_row[0:1, 0:D]))
            dve.wait_ge(pe_step, 2)
            ch.sync()
            ch.mark(nc.vector.tensor_tensor(cov[:, :], moments[:, 0:D], p_out[:, 0:D], ALU.subtract))
            dve.wait_ge(pe_step, 3)
            ch.mark(nc.vector.tensor_tensor(prod[:, :], W1T[:, :], p_prod[:, 0:2 * D], ALU.mult))
            ch.mark(nc.vector.tensor_tensor(mean_z[:, :], p_small[:, 0:2], g["b1c"][:, :], ALU.add))
            dve.wait_ge(pe_step, 4)
            ch.mark(nc.vector.tensor_copy(var_z[:, :], p_var[:, 0:2]))
            dve.wait_ge(std_ready, 1)
            ch.mark(nc.vector.reciprocal(std_z[:, :], std_z[:, :]))
            ch.mark(nc.vector.tensor_tensor(mean_z[:, :], g["b1c"][:, :], mean_z[:, :], ALU.subtract))
            ch.sync()
            ch.mark(nc.vector.tensor_tensor(g["a1"][:, :], std_z[:, :], g["g1c"][:, :], ALU.mult))
            ch.sync()
            ch.mark(nc.vector.tensor_tensor(mean_z[:, :], mean_z[:, :], g["a1"][:, :], ALU.mult))
            ch.sync()
            ch.mark(nc.vector.tensor_tensor(g["t1"][:, :], mean_z[:, :], g["beta1c"][:, :], ALU.add))

        @block.tensor
        def _(pe):
            def products(i, k):
                m, s = STEP * i + k, k % LOADS
                r = g["rows_of"](m)
                pe.wait_ge(h_in[s], 16 * (slot_turn(i, k) + 1))
                first, final = isinstance(i, int) and m == 0, isinstance(i, int) and m == CHUNKS - 1
                for j in range(J):
                    nc.tensor.matmul(p_mom[:, 0:D], hb[s][0:r, j, :], hb[s][0:r, j, :],
                                     start=first and j == 0, stop=final and j == J - 1)
                pe.wait_ge(hsum_ready, m + 1)
                nc.tensor.matmul(p_mean[:, 0:1], hsum[s][0:r, :], g["ones_col"][0:r, :], start=first, stop=final
                                 ).then_inc(h_used, 1)
            loop_chunks(pe, CHUNKS, products)
            pe.wait_ge(dve_step, 1)
            nc.tensor.transpose(p_row[0:1, 0:P], moments[:, D:D + 1], g["ident"][:, :]).then_inc(pe_step, 1)
            pe.wait_ge(dve_step, 2)
            nc.tensor.matmul(p_out[:, 0:D], mrow[:, :], mrow[:, :], start=True, stop=True).then_inc(pe_step, 1)
            for b in two:
                nc.tensor.matmul(p_small[:, b:b + 1], W1T[:, b * D:(b + 1) * D], moments[:, D:D + 1],
                                 start=True, stop=True)
            pe.wait_ge(dve_step, 3)
            nc.tensor.matmul(p_prod[:, 0:2 * D], cov[:, :], W1T[:, :], start=True, stop=True).then_inc(pe_step, 1)
            pe.wait_ge(dve_step, 4)
            for b in two:
                last = nc.tensor.matmul(p_var[:, b:b + 1], prod[:, b * D:(b + 1) * D], g["ones_col"][:, :],
                                        start=True, stop=True)
            last.then_inc(pe_step, 1)

        @block.scalar
        def _(act):
            act.wait_ge(dve_step, 6)
            nc.scalar.activation(std_z[:, :], var_z[:, :], ACT.Sqrt, bias=g["eps_col"][:, 0:1]).then_inc(std_ready, 1)


def mlp(nc, g):
    CHUNKS, LAST = g["CHUNKS"], g["LAST"]
    W1T, W2T, ident = g["W1T"], g["W2T"], g["ident"]
    with Scope(nc, "mlp") as sc:
        two = range(2)
        hb = [sc.sb(f"hb{l}", [P, W]) for l in range(LOADS)]
        zero = sc.sb("zero", [P, W])
        hT = [sc.sb(f"hT{q}", [P, HALF]) for q in two]
        act1 = [sc.sb(f"act1{q}", [P, 2, HALF]) for q in two]
        z2 = [sc.sb(f"z2{s}", [P, W]) for s in two]
        stats = sc.sb("stats", [P, 2 * CHUNKS, 6])
        mv = sc.sb("mv", [P, 2])
        std = sc.sb("std", [P, 1])
        p_hT = [sc.ps(f"p_hT{q}", [P, HALF]) for q in two]
        p_z1 = [sc.ps(f"p_z1{q}", [P, 2, HALF]) for q in two]
        p_z2 = [sc.ps(f"p_z2{q}", [P, HALF]) for q in two]
        h_in = [sc.sem(f"h_in{l}") for l in range(LOADS)]
        stored = [sc.sem(f"stored{s}") for s in two]
        h_used, hT_ready, z1_ready, act1_ready, z2_psum, z2_ready, z2_counted = (
            sc.sem(n) for n in ("h_used", "hT_ready", "z1_ready", "act1_ready", "z2_psum", "z2_ready",
                                "z2_counted"))
        dve_step, std_ready, zero_ready, cleared = (
            sc.sem(n) for n in ("dve_step", "std_ready", "zero_ready", "cleared"))
        block = sc.block()
        aggv = g["chunked"](g["h_t"])

        def half_before(i, k, q):
            return (i, k, 0) if q else (*chunk_before(i, k), 1) if chunk_before(i, k) else None

        def next_half(i, k, q):
            return (i, k, 1) if q == 0 else (*next_chunk(CHUNKS, i, k), 0) if next_chunk(CHUNKS, i, k) else None

        @block.sync
        def _(sp):
            def load(i, k):
                m, l = STEP * i + k, k % LOADS
                wait(sp, h_used, 2 * (m - LOADS + 1))
                sp.dma_start(hb[l][:, :], g["at"](aggv, m)).then_inc(h_in[l], 16)
                sp.dma_start(g["at"](g["chunked"](g["agg2"]), m), zero[:, :]).then_inc(cleared, 16)
            sp.wait_ge(zero_ready, 1)
            loop_chunks(sp, CHUNKS, load)
            sp.wait_ge(cleared, 16 * CHUNKS)

        @block.gpsimd
        def _(pool):
            nc.gpsimd.memset(zero[:, :], 0.0).then_inc(zero_ready, 1)

            def store(i, k):
                m, s = STEP * i + k, k % 2
                pool.wait_ge(z2_ready, 2 * (m + 1))
                pool.dma_start(g["at"](g["z2_t"], m), z2[s][:, :]).then_inc(stored[s], 16)
            loop_chunks(pool, CHUNKS, store)
            for s in two:
                pool.wait_ge(stored[s], 8 * CHUNKS)

        @block.vector
        def _(dve):
            def evacuate(i, k, q):
                u = 2 * (STEP * i + k) + q
                dve.wait_ge(h_used, u + 1)
                wait(dve, z1_ready, u - 1)
                nc.vector.tensor_copy(hT[q][:, :], p_hT[q][:, :]).then_inc(hT_ready, 1)

            def count(i, k, q):
                u, s = 2 * (STEP * i + k) + q, k % 2
                r = g["rows_of"](STEP * i + k)
                dve.wait_ge(z2_ready, u + 1)
                z = z2[s][:, q * HALF:(q + 1) * HALF]
                z = z if r == P else z.rearrange("p (j n) -> p j n", n=P)[:, :, 0:r]
                if isinstance(u, int):
                    o = stats[:, u, :]
                else:
                    o = stats[:, bass.ds(u, 1), :].rearrange("p a k -> p (a k)")
                nc.vector.bn_stats(o, z).then_inc(z2_counted, 1)

            def step(i, k):
                for q in two:
                    if next_half(i, k, q):
                        evacuate(*next_half(i, k, q))
                    if half_before(i, k, q):
                        count(*half_before(i, k, q))
            evacuate(0, 0, 0)
            loop_chunks(dve, CHUNKS, step)
            count(*LAST, 1)
            dve.wait_ge(z2_counted, 2 * CHUNKS)
            ch = Chain(dve, dve_step)
            ch.mark(nc.vector.bn_aggr(mv[:, :], stats[:, :, :].rearrange("p u k -> p (u k)")))
            dve.wait_ge(std_ready, 1)
            ch.sync()
            ch.mark(nc.vector.reciprocal(std[:, :], std[:, :]))
            ch.mark(nc.vector.tensor_tensor(mv[:, 0:1], mv[:, 0:1], g["b2c"][:, :], ALU.add))
            ch.sync()
            ch.mark(nc.vector.tensor_tensor(g["a2"][:, :], std[:, :], g["g2c"][:, :], ALU.mult))
            ch.mark(nc.vector.tensor_tensor(mv[:, 0:1], g["b2c"][:, :], mv[:, 0:1], ALU.subtract))
            ch.sync()
            ch.mark(nc.vector.tensor_tensor(mv[:, 0:1], mv[:, 0:1], g["a2"][:, :], ALU.mult))
            ch.sync()
            ch.mark(nc.vector.tensor_tensor(g["t2"][:, :], mv[:, 0:1], g["beta2c"][:, :], ALU.add))

        @block.scalar
        def _(act):
            def relu(i, k, q):
                u = 2 * (STEP * i + k) + q
                act.wait_ge(z1_ready, u + 1)
                wait(act, z2_psum, u - 1)
                for b in two:
                    last = nc.scalar.activation(act1[q][:, b, :], p_z1[q][:, b, :], ACT.Relu,
                                                bias=g["t1"][:, b:b + 1], scale=g["a1"][:, b:b + 1])
                last.then_inc(act1_ready, 1)

            def evacuate(i, k, q):
                u = 2 * (STEP * i + k) + q
                s = k % 2
                act.wait_ge(z2_psum, u + 1)
                if q == 0:
                    wait(act, stored[s], 16 * slot_turn(i, k, 2))
                    wait(act, z2_counted, u - 2)
                nc.scalar.copy(z2[s][:, q * HALF:(q + 1) * HALF], p_z2[q][:, :]).then_inc(z2_ready, 1)

            def step(i, k):
                for q in two:
                    relu(i, k, q)
                    if half_before(i, k, q):
                        evacuate(*half_before(i, k, q))
            loop_chunks(act, CHUNKS, step)
            evacuate(*LAST, 1)
            act.wait_ge(dve_step, 1)
            nc.scalar.activation(std[:, :], mv[:, 1:2], ACT.Sqrt, bias=g["eps_col"][:, 0:1]).then_inc(std_ready, 1)

        @block.tensor
        def _(pe):
            def turn(i, k, q):
                u = 2 * (STEP * i + k) + q
                l = k % LOADS
                pe.wait_ge(h_in[l], 16 * (slot_turn(i, k) + 1))
                wait(pe, hT_ready, u - 1)
                for n in range(J // 2):
                    j = q * (J // 2) + n
                    last = nc.tensor.transpose(p_hT[q][:, n * P:(n + 1) * P], hb[l][:, j * D:(j + 1) * D], ident[:, :])
                last.then_inc(h_used, 1)

            def first(i, k, q):
                u = 2 * (STEP * i + k) + q
                pe.wait_ge(hT_ready, u + 1)
                wait(pe, act1_ready, u - 1)
                for b in two:
                    last = nc.tensor.matmul(p_z1[q][:, b, :], W1T[:, b * D:(b + 1) * D], hT[q][:, :],
                                            start=True, stop=True)
                last.then_inc(z1_ready, 1)

            def second(i, k, q):
                u = 2 * (STEP * i + k) + q
                pe.wait_ge(act1_ready, u + 1)
                wait(pe, z2_ready, u - 1)
                for b in two:
                    last = nc.tensor.matmul(p_z2[q][:, :], W2T[:, b, :], act1[q][:, b, :],
                                            start=(b == 0), stop=(b == 1))
                last.then_inc(z2_psum, 1)

            def step(i, k):
                for q in two:
                    first(i, k, q)
                    if next_half(i, k, q):
                        turn(*next_half(i, k, q))
                    if half_before(i, k, q):
                        second(*half_before(i, k, q))
            turn(0, 0, 0)
            loop_chunks(pe, CHUNKS, step)
            second(*LAST, 1)


class NodeNorm:

    def __init__(self, nc, sc, g):
        self.nc, self.g = nc, g
        self.u = [sc.sb(f"u{s}", [P, J, D]) for s in range(LOADS)]
        self.y = [sc.sb(f"y{s}", [P, J, D]) for s in range(LOADS)]
        self.stats = sc.sb("stats", [P, J, 6])
        self.tmp = sc.sb("tmp", [P, 3, J])
        self.mean = [sc.sb(f"mean{s}", [P, J]) for s in range(LOADS)]
        self.var = [sc.sb(f"var{s}", [P, J]) for s in range(LOADS)]
        self.std = [sc.sb(f"std{s}", [P, J]) for s in range(LOADS)]
        self.rstd = [sc.sb(f"rstd{s}", [P, J]) for s in range(LOADS)]
        self.shift = [sc.sb(f"shift{s}", [P, J]) for s in range(LOADS)]
        self.step = sc.sem("dve_step")
        self.u_ready, self.var_ready, self.std_ready, self.scale_ready, self.y_ready, self.y_ready_act = (
            sc.sem(n) for n in ("u_ready", "var_ready", "std_ready", "scale_ready", "y_ready", "y_ready_act"))
        self.stored = [sc.sem(f"stored{s}") for s in range(LOADS)]

    def round(self, dve, ch, cur, prev, add_u=None, scale2=None, scale=None):
        nc, st = self.nc, self.stats
        rows = iter(range(J - ACT_ROWS))

        def row():
            j = next(rows, None)
            if prev and j is not None:
                ins = nc.vector.tensor_scalar(self.y[ps][:, j, :], self.u[ps][:, j, :], self.mean[ps][:, j:j + 1],
                                              self.rstd[ps][:, j:j + 1], ALU.subtract, ALU.mult)
                if j == J - ACT_ROWS - 1:
                    ins.then_inc(self.y_ready, 1)
        if cur:
            m, s = STEP * cur[0] + cur[1], cur[1] % LOADS
            add_u()
        if prev:
            pm, ps = STEP * prev[0] + prev[1], prev[1] % LOADS
            dve.wait_ge(self.std_ready, pm + 1)
            wait(dve, self.y_ready_act, pm - LOADS + 1)
            factor = ch.mark(nc.vector.reciprocal(self.rstd[ps][:, :], self.std[ps][:, :]))
        if cur:
            dve.wait_ge(self.u_ready, m + 1)

        def count(j0, j1):
            if cur:
                for j in range(j0, j1):
                    self.counted = nc.vector.bn_stats(st[:, j, :], self.u[s][:, j, :])
        count(0, 2)
        if prev:
            if scale is not None:
                ch.after(factor)
                factor = ch.mark(nc.vector.tensor_tensor(self.rstd[ps][:, :], self.rstd[ps][:, :], scale, ALU.mult))
        count(2, 4)
        if prev:
            ch.after(factor)
            nc.vector.scalar_tensor_tensor(out=self.shift[ps][:, :], in0=self.mean[ps][:, :], scalar=-1.0,
                                           in1=self.rstd[ps][:, :], op0=ALU.mult, op1=ALU.mult
                                           ).then_inc(self.scale_ready, 1)
        count(4, J)
        if cur:
            counted = ch.mark(self.counted)
        if prev:
            wait(dve, self.stored[ps], 16 * slot_turn(*prev))
        row()
        tot, dif, m2 = (self.tmp[:, k, :] for k in range(3))
        if cur:
            ch.after(counted)
            wait(dve, self.y_ready, m - LOADS + 1)
            ch.mark(nc.vector.tensor_tensor(tot, st[:, :, 1], st[:, :, 4], ALU.add))
            ch.mark(nc.vector.tensor_tensor(dif, st[:, :, 1], st[:, :, 4], ALU.subtract))
            parts = ch.mark(nc.vector.tensor_tensor(m2, st[:, :, 2], st[:, :, 5], ALU.add))
        row()
        if cur:
            ch.after(parts)
            ch.mark(nc.vector.tensor_scalar(self.mean[s][:, :], tot, 0.5, None, ALU.mult))
            square = ch.mark(nc.vector.scalar_tensor_tensor(out=dif, in0=dif, scalar=0.25, in1=dif, op0=ALU.mult,
                                                            op1=ALU.mult))
        row()
        if cur:
            ch.after(square)
            wait(dve, self.std_ready, m - LOADS + 1)
            var = nc.vector.scalar_tensor_tensor(out=self.var[s][:, :], in0=m2, scalar=1.0 / D, in1=dif,
                                                 op0=ALU.mult, op1=ALU.add)
            if scale2 is None:
                var.then_inc(self.var_ready, 1)
            else:
                plain = ch.mark(var)
        row()
        if cur and scale2 is not None:
            ch.after(plain)
            nc.vector.tensor_tensor(self.var[s][:, :], self.var[s][:, :], scale2, ALU.mult
                                    ).then_inc(self.var_ready, 1)

    def root(self, act, i, k):
        m, s = STEP * i + k, k % LOADS
        act.wait_ge(self.var_ready, m + 1)
        wait(act, self.scale_ready, m - LOADS + 1)
        self.nc.scalar.activation(self.std[s][:, :], self.var[s][:, :], ACT.Sqrt,
                                  bias=self.g["eps_col"][:, 0:1]).then_inc(self.std_ready, 1)

    def free_u(self, dve, m):
        wait(dve, self.y_ready, m - LOADS + 1)
        wait(dve, self.y_ready_act, m - LOADS + 1)

    def apply_act(self, act, i, k):
        m, s = STEP * i + k, k % LOADS
        act.wait_ge(self.scale_ready, m + 1)
        wait(act, self.stored[s], 16 * slot_turn(i, k))
        for j in range(J - ACT_ROWS, J):
            last = self.nc.scalar.activation(self.y[s][:, j, :], self.u[s][:, j, :], ACT.Identity,
                                             bias=self.shift[s][:, j:j + 1], scale=self.rstd[s][:, j:j + 1])
        last.then_inc(self.y_ready_act, 1)

    def load_and_store(self, sp, chunks, load, store):
        def put(i, k):
            m, s = STEP * i + k, k % LOADS
            sp.wait_ge(self.y_ready, m + 1)
            sp.wait_ge(self.y_ready_act, m + 1)
            where = store(m)
            rows = where.shape[0]
            sp.dma_start(where, self.y[s][0:rows, :, :].rearrange("p j f -> p (j f)")).then_inc(self.stored[s], 16)

        def step(i, k):
            load(i, k)
            if earlier(i, k, STORE_LAG):
                put(*earlier(i, k, STORE_LAG))
        loop_chunks(sp, chunks, step)
        for k in range(STEP - STORE_LAG, STEP):
            put(chunks // STEP - 1, k)
        for s in range(LOADS):
            sp.wait_ge(self.stored[s], 16 * chunks // LOADS)


def flat(b):
    return b[:, :, :].rearrange("p j f -> p (j f)")


def ahead(pairs, i, s):
    return None if isinstance(i, int) and i == pairs - 1 and s == 1 else slot_step(i, s, 1)


def per_node(table, i, k):
    return table[:, bass.ds((STEP * i + k) * J, J)]


def first_layer_out(nc, g):
    CHUNKS, LAST = g["CHUNKS"], g["LAST"]
    with Scope(nc, "out1") as sc:
        two = range(2)
        xb = [sc.sb(f"xb{l}", [P, W]) for l in range(LOADS)]
        zb = [sc.sb(f"zb{l}", [P, W]) for l in range(LOADS)]
        rb = [sc.sb(f"rb{s}", [P, W]) for s in two]
        p_r = [sc.ps(f"p_r{s}", [P, W]) for s in two]
        nn = NodeNorm(nc, sc, g)
        x_in = [sc.sem(f"x_in{l}") for l in range(LOADS)]
        z_in = [sc.sem(f"z_in{l}") for l in range(LOADS)]
        r_ready, turned = sc.sem("r_ready"), sc.sem("turned")
        block = sc.block()
        outv = g["chunked"](g["x1n_t"])

        @block.sync
        def _(sp):
            def load(i, k):
                m, l = STEP * i + k, k % LOADS
                r = g["rows_of"](m)
                wait(sp, r_ready, m - LOADS + 1)
                sp.dma_start(zb[l][:, :], g["at"](g["z2_t"], m)).then_inc(z_in[l], 16)
                wait(sp, nn.u_ready, m - LOADS + 1)
                sp.dma_start(xb[l][0:r, :], g["node_rows"](g["x"], m, r)).then_inc(x_in[l], 16)
            nn.load_and_store(sp, CHUNKS, load, lambda m: g["at"](outv, m))

        @block.scalar
        def _(act):
            def relu(i, k):
                m, s, l = STEP * i + k, k % 2, k % LOADS
                act.wait_ge(z_in[l], 16 * (slot_turn(i, k) + 1))
                wait(act, turned, m - 1)
                nc.scalar.activation(rb[s][:, :], zb[l][:, :], ACT.Relu, bias=g["t2"][:, 0:1],
                                     scale=g["a2"][:, 0:1]).then_inc(r_ready, 1)

            def step(i, k):
                b = chunk_before(i, k)
                if next_chunk(CHUNKS, i, k):
                    relu(*next_chunk(CHUNKS, i, k))
                if b:
                    nn.apply_act(act, *b)
                nn.root(act, i, k)
            relu(0, 0)
            loop_chunks(act, CHUNKS, step)
            nn.apply_act(act, *LAST)

        @block.tensor
        def _(pe):
            def step(i, k):
                m, s = STEP * i + k, k % 2
                pe.wait_ge(r_ready, m + 1)
                wait(pe, nn.u_ready, m - 1)
                for j in range(J):
                    last = nc.tensor.transpose(p_r[s][:, j * D:(j + 1) * D], rb[s][:, j * P:(j + 1) * P],
                                               g["ident"][:, :])
                last.then_inc(turned, 1)
            loop_chunks(pe, CHUNKS, step)

        @block.vector
        def _(dve):
            ch = Chain(dve, nn.step)

            def add(i, k):
                m, s, l = STEP * i + k, k % 2, k % LOADS
                dve.wait_ge(x_in[l], 16 * (slot_turn(i, k) + 1))
                dve.wait_ge(turned, m + 1)
                nn.free_u(dve, m)
                nc.vector.tensor_tensor(flat(nn.u[k % LOADS]), p_r[s][:, :], xb[l][:, :], ALU.add
                                        ).then_inc(nn.u_ready, 1)

            def step(i, k):
                prev = chunk_before(i, k)
                nn.round(dve, ch, (i, k), prev, add_u=lambda: add(i, k),
                         scale=per_node(g["norm"], *prev) if prev else None)
            loop_chunks(dve, CHUNKS, step, ch, 8)
            nn.round(dve, ch, None, LAST, scale=per_node(g["norm"], *LAST))


def aggregate(nc, g, tag, table, acc, key_at, gather_kind, owner_kind, clear_state=False):
    EC, GROUPS, EPAIRS = g["EDGE_COLS"], g["GROUPS"], g["EPAIRS"]
    keys, index, ident = g["keys"], g["index"], g["ident"]
    with Scope(nc, "sum_" + tag) as sc:
        two = range(2)
        gi = [sc.sb(f"gi{r}", [P, 2], I32) for r in range(LOADS)]
        oi = [sc.sb(f"oi{s}", [P, 2], I32) for s in two]
        keyb = [sc.sb(f"keyb{s}", [P, 2, P]) for s in two]
        eq = [sc.sb(f"eq{s}", [P, 2, GROUP]) for s in two]
        rows = [sc.sb(f"rows{r}", [P, 2, D]) for r in range(LOADS)]
        sums = [sc.sb(f"sums{s}", [P, 2, D]) for s in two]
        p_keys = [sc.ps(f"p_keys{s}", [P, 512]) for s in two]
        p_sums = [sc.ps(f"p_sums{s}", [P, 512]) for s in two]
        arrived = [sc.sem(f"arrived{r}") for r in range(LOADS)]
        added, gi_ready, oi_ready, keyb_ready, rows_ready, eq_ready, summed, sums_ready = (
            sc.sem(n) for n in ("added", "gi_ready", "oi_ready", "keyb_ready", "rows_ready", "eq_ready", "summed",
                                "sums_ready"))
        if clear_state:
            fresh = sc.sb("fresh", [P, J, STATE])
            fresh_ready, cleared = sc.sem("fresh_ready"), sc.sem("cleared")
        block = sc.block()

        if clear_state:
            @block.sync
            def _(sp):
                sp.wait_ge(fresh_ready, 1)
                clear_tables(sp, g, [(g["state_t"], flat(fresh))], cleared, summed, g["PAIRS"])

        @block.gpsimd
        def _(pool):
            if clear_state:
                nc.gpsimd.memset(fresh[:, :, 0:SUMS], 0.0)
                nc.gpsimd.memset(fresh[:, :, SUMS:STATE], LOWEST).then_inc(fresh_ready, 1)
            gathers, scatters = Turns(pool, sc.tag + "_gathers"), Turns(pool, sc.tag + "_scatters")

            def gather(i, k):
                t, r = STEP * i + k, k % LOADS
                wait(pool, summed, t - LOADS + 1)
                gathers.wait(gi_ready, t)
                for c in two:
                    pool.indirect_dma_start(rows[r][:, c, :], None, table,
                                            bass.IndirectOffsetOnAxis(ap=gi[r][:, c:c + 1], axis=0)
                                            ).then_inc(arrived[r], 16)

            def step(i, k):
                t, s = STEP * i + k, k % 2
                if later(GROUPS, i, k, LEAD):
                    gather(*later(GROUPS, i, k, LEAD))
                pool.wait_ge(oi_ready, t + 1)
                wait(pool, added, 32 * t)
                scatters.wait(sums_ready, t)
                for c in two:
                    pool.indirect_dma_start(acc, bass.IndirectOffsetOnAxis(ap=oi[s][:, c:c + 1], axis=0),
                                            sums[s][:, c, :], None, compute_op=ALU.add).then_inc(added, 16)
            for k in range(LEAD):
                gather(0, k)
            loop_chunks(pool, GROUPS, step)
            pool.wait_ge(added, 32 * GROUPS)

        @block.tensor
        def _(pe):
            def spread(i, k):
                t, s = STEP * i + k, k % 2
                pe.wait_ge(keyb_ready, t + 1)
                wait(pe, eq_ready, t - 1)
                for c in two:
                    last = nc.tensor.matmul(p_keys[s][:, c * P:(c + 1) * P], keyb[s][:, c, :], ident[:, :],
                                            start=True, stop=True)
                last.then_inc(rows_ready, 1)

            def step(i, k):
                t, s, r = STEP * i + k, k % 2, k % LOADS
                if next_chunk(GROUPS, i, k):
                    spread(*next_chunk(GROUPS, i, k))
                pe.wait_ge(eq_ready, t + 1)
                pe.wait_ge(arrived[r], 32 * (slot_turn(i, k) + 1))
                wait(pe, sums_ready, t - 1)
                for c in two:
                    for n in two:
                        last = nc.tensor.matmul(p_sums[s][:, c * D:(c + 1) * D], eq[s][:, n, c * P:(c + 1) * P],
                                                rows[r][:, n, :], start=(n == 0), stop=(n == 1))
                last.then_inc(summed, 1)
            spread(0, 0)
            loop_chunks(pe, GROUPS, step)

        @block.scalar
        def _(act):
            def step(i, k):
                t, s = STEP * i + k, k % 2
                act.wait_ge(summed, t + 1)
                wait(act, added, 32 * (t - 1))
                nc.scalar.copy(sums[s][:, :, :].rearrange("p c f -> p (c f)"), p_sums[s][:, 0:2 * D]
                               ).then_inc(sums_ready, 1)
            loop_chunks(act, GROUPS, step)

        @block.vector
        def _(dve):
            def gather_index(i, k):
                t, r = STEP * i + k, k % LOADS
                wait(dve, arrived[r], 32 * slot_turn(i, k))
                nc.vector.tensor_scalar(gi[r][:, :],
                                      index[:, bass.ds(t, 1), gather_kind, :].rearrange("p a c -> p (a c)"),
                                      1.0, None, ALU.mult
                                      ).then_inc(gi_ready, 1)

            def spread_keys(i, k):
                t, s = STEP * i + k, k % 2
                wait(dve, eq_ready, t - 1)
                nc.vector.tensor_copy(keyb[s][:, :, :],
                                      keys[:, bass.ds(2 * t + key_at, 2)].unsqueeze(2).to_broadcast([P, 2, P])
                                      ).then_inc(keyb_ready, 1)

            def step(i, k):
                t, s = STEP * i + k, k % 2
                if later(GROUPS, i, k, LEAD):
                    gather_index(*later(GROUPS, i, k, LEAD))
                if next_chunk(GROUPS, i, k):
                    spread_keys(*next_chunk(GROUPS, i, k))
                dve.wait_ge(rows_ready, t + 1)
                wait(dve, summed, t - 1)
                for c in two:
                    last = nc.vector.tensor_scalar(eq[s][:, c, :], p_keys[s][:, 0:GROUP], keyb[s][:, c, 0:1], None,
                                                   ALU.is_equal)
                last.then_inc(eq_ready, 1)
                wait(dve, added, 32 * (t - 1))
                nc.vector.tensor_scalar(oi[s][:, :],
                                      index[:, bass.ds(t, 1), owner_kind, :].rearrange("p a c -> p (a c)"),
                                      1.0, None, ALU.mult
                                      ).then_inc(oi_ready, 1)
            for k in range(LEAD):
                gather_index(0, k)
            spread_keys(0, 0)
            loop_chunks(dve, GROUPS, step)


def convolve(nc, g, tag, table, acc, result, WT):
    CHUNKS, LAST = g["CHUNKS"], g["LAST"]
    first = tag == "l1"
    with Scope(nc, "conv_" + tag) as sc:
        two = range(2)
        xb = [sc.sb(f"xb{l}", [P, J, D]) for l in range(LOADS)]
        ab = [sc.sb(f"ab{l}", [P, J, D]) for l in range(LOADS)]
        gb = [sc.sb(f"gb{s}", [P, J, D]) for s in two] if first else None
        vb = [sc.sb(f"vb{s}", [P, J, D]) for s in two]
        gT = [sc.sb(f"gT{s}", [P, W]) for s in two]
        p_g = [sc.ps(f"p_g{s}", [P, W]) for s in two]
        p_o = [sc.ps(f"p_o{s}", [P, W]) for s in two]
        nn = NodeNorm(nc, sc, g)
        x_in = [sc.sem(f"x_in{l}") for l in range(LOADS)]
        a_in = [sc.sem(f"a_in{l}") for l in range(LOADS)]
        g_ready, v_ready, turned, gT_ready, o_ready = (
            sc.sem(n) for n in ("g_ready", "v_ready", "turned", "gT_ready", "o_ready"))
        block = sc.block()
        xv, av, outv = (g["chunked"](t) for t in (table, acc, result))

        @block.sync
        def _(sp):
            def load(i, k):
                m, l = STEP * i + k, k % LOADS
                wait(sp, v_ready, m - LOADS + 1)
                sp.dma_start(flat(xb[l]), g["at"](xv, m)).then_inc(x_in[l], 16)
                if not first:
                    wait(sp, turned, m - LOADS + 1)
                sp.dma_start(flat(ab[l]), g["at"](av, m)).then_inc(a_in[l], 16)
            nn.load_and_store(sp, CHUNKS, load, lambda m: g["at"](outv, m))

        @block.gpsimd
        def _(pool):
            def sum_rows(i, k):
                m, s, l = STEP * i + k, k % 2, k % LOADS
                pool.wait_ge(x_in[l], 16 * (slot_turn(i, k) + 1))
                pool.wait_ge(a_in[l], 16 * (slot_turn(i, k) + 1))
                wait(pool, turned, m - 1)
                nc.gpsimd.tensor_tensor(flat(gb[s]), flat(xb[l]), flat(ab[l]), ALU.add).then_inc(g_ready, 1)

            def step(i, k):
                m, s, l = STEP * i + k, k % 2, k % LOADS
                if first:
                    if next_chunk(CHUNKS, i, k):
                        sum_rows(*next_chunk(CHUNKS, i, k))
                    wait(pool, nn.u_ready, m - 1)
                    nc.gpsimd.tensor_tensor(
                        vb[s][:, :, :], xb[l][:, :, :],
                        per_node(g["deg1"], i, k).unsqueeze(2).to_broadcast([P, J, D]), ALU.mult
                        ).then_inc(v_ready, 1)
                else:
                    pool.wait_ge(x_in[l], 16 * (slot_turn(i, k) + 1))
                    wait(pool, nn.u_ready, m - 1)
                    nc.gpsimd.tensor_tensor(vb[s][:, :, :], xb[l][:, :, :],
                                            g["bL2_all"][:, :].unsqueeze(1).to_broadcast([P, J, D]), ALU.add
                                            ).then_inc(v_ready, 1)
            if first:
                sum_rows(0, 0)
            loop_chunks(pool, CHUNKS, step)

        @block.tensor
        def _(pe):
            def turn(i, k):
                m, s, l = STEP * i + k, k % 2, k % LOADS
                if first:
                    pe.wait_ge(g_ready, m + 1)
                else:
                    pe.wait_ge(a_in[l], 16 * (slot_turn(i, k) + 1))
                wait(pe, gT_ready, m - 1)
                rows = gb[s] if first else ab[l]
                for j in range(J):
                    last = nc.tensor.transpose(p_g[s][:, j * P:(j + 1) * P], rows[:, j, :], g["ident"][:, :])
                last.then_inc(turned, 1)

            def step(i, k):
                m, s = STEP * i + k, k % 2
                if next_chunk(CHUNKS, i, k):
                    turn(*next_chunk(CHUNKS, i, k))
                pe.wait_ge(gT_ready, m + 1)
                wait(pe, nn.u_ready, m - 1)
                for j in range(J):
                    last = nc.tensor.matmul(p_o[s][:, j * D:(j + 1) * D], gT[s][:, j * P:(j + 1) * P], WT[:, :],
                                            start=True, stop=True)
                last.then_inc(o_ready, 1)
            turn(0, 0)
            loop_chunks(pe, CHUNKS, step)

        @block.scalar
        def _(act):
            def evacuate(i, k):
                m, s = STEP * i + k, k % 2
                act.wait_ge(turned, m + 1)
                wait(act, o_ready, m - 1)
                nc.scalar.copy(gT[s][:, :], p_g[s][:, :]).then_inc(gT_ready, 1)

            def step(i, k):
                b = chunk_before(i, k)
                if next_chunk(CHUNKS, i, k):
                    evacuate(*next_chunk(CHUNKS, i, k))
                if b:
                    nn.apply_act(act, *b)
                nn.root(act, i, k)
            evacuate(0, 0)
            loop_chunks(act, CHUNKS, step)
            nn.apply_act(act, *LAST)

        @block.vector
        def _(dve):
            ch = Chain(dve, nn.step)

            def add(i, k):
                m, s = STEP * i + k, k % 2
                dve.wait_ge(v_ready, m + 1)
                dve.wait_ge(o_ready, m + 1)
                nn.free_u(dve, m)
                nc.vector.tensor_tensor(flat(nn.u[k % LOADS]), p_o[s][:, :], flat(vb[s]), ALU.add
                                        ).then_inc(nn.u_ready, 1)

            def step(i, k):
                prev = chunk_before(i, k)
                nn.round(dve, ch, (i, k), prev, add_u=lambda: add(i, k),
                         scale2=per_node(g["norm2"], i, k) if first else None,
                         scale=per_node(g["norm"], *prev) if first and prev else None)
            loop_chunks(dve, CHUNKS, step, ch, 9 if first else 7)
            nn.round(dve, ch, None, LAST, scale=per_node(g["norm"], *LAST) if first else None)


def attention(nc, g):
    GROUPS, EPAIRS = g["GROUPS"], g["EPAIRS"]
    keys, index, ident, x3_t, state_t, WT = (g[n] for n in ("keys", "index", "ident", "x3_t", "state_t", "WLT"))
    WT = WT[2]
    SCALE = HD ** -0.5
    with Scope(nc, "attn") as sc:
        two = range(2)
        gi = [sc.sb(f"gi{s}", [P, 4], I32) for s in two]
        oi = [sc.sb(f"oi{s}", [P, 4], I32) for s in two]
        keyb = [sc.sb(f"keyb{s}", [P, 2, P]) for s in two]
        eq = [sc.sb(f"eq{s}", [P, 2, GROUP]) for s in two]
        below = sc.sb("below", [P, 2, GROUP])
        ends = [sc.sb(f"ends{s}", [P, 4, D]) for s in two]
        endsT = [sc.sb(f"endsT{s}", [P, 4 * P]) for s in two]
        ft = [sc.sb(f"ft{s}", [P, 4, D]) for s in two]
        prod = sc.sb("prod", [P, 2, D])
        logit = [sc.sb(f"logit{s}", [P, 2, HEADS]) for s in two]
        shifted = sc.sb("shifted", [P, 2, HEADS, GROUP])
        peak = [sc.sb(f"peak{s}", [P, 2, HEADS]) for s in two]
        gap = [sc.sb(f"gap{s}", [P, 2, HEADS]) for s in two]
        terms = [sc.sb(f"terms{s}", [P, 2, HEADS, HS]) for s in two]
        old = [sc.sb(f"old{s}", [P, 2, STATE]) for s in two]
        new = [sc.sb(f"new{s}", [P, 2, STATE]) for s in two]
        drop = [sc.sb(f"drop{s}", [P, 2, 2, HEADS]) for s in two]
        keep = [sc.sb(f"keep{s}", [P, 2, 2, HEADS]) for s in two]
        part = sc.sb("part", [P, 2, SUMS])
        p_keys = sc.ps("p_keys", [P, 512])
        p_endsT = sc.ps("p_endsT", [P, 512])
        p_ft = sc.ps("p_ft", [P, 512])
        p_logit = sc.ps("p_logit", [P, HEADS, GROUP])
        p_sums = [sc.ps(f"p_sums{s}", [P, 512]) for s in two]
        arrived = [sc.sem(f"arrived{s}") for s in two]
        state_in = [sc.sem(f"state_in{s}") for s in two]
        state_out = sc.sem("state_out")
        names = ("gi_ready", "oi_ready", "keyb_ready", "rows_ready", "eq_ready", "turned", "endsT_ready", "ft_psum",
                 "ft_ready", "logit_ready", "logit_rows", "peak_ready", "weight_ready", "terms_ready", "summed",
                 "drop_ready", "keep_ready", "new_ready", "dve_step", "gap_ready")
        S = {n: sc.sem(n) for n in names}
        block = sc.block()

        def heads(ap):
            return ap.rearrange("p c (h f) -> p c h f", h=HEADS)

        def second_next(i, s):
            return None if isinstance(i, int) and i == EPAIRS - 1 else (i + 1, s)

        @block.gpsimd
        def _(pool):
            gathers, scatters = Turns(pool, sc.tag + "_gathers"), Turns(pool, sc.tag + "_scatters")
            states = Turns(pool, sc.tag + "_states")

            def gather(i, s):
                t = 2 * i + s
                wait(pool, S["turned"], t - 1)
                gathers.wait(S["gi_ready"], t)
                for c in range(4):
                    pool.indirect_dma_start(ends[s][:, c, :], None, x3_t,
                                            bass.IndirectOffsetOnAxis(ap=gi[s][:, c:c + 1], axis=0)
                                            ).then_inc(arrived[s], 16)

            def step(i):
                for s in two:
                    t = 2 * i + s
                    wait(pool, state_out, 32 * t)
                    wait(pool, S["new_ready"], t - 1)
                    states.wait(S["oi_ready"], t)
                    for c in two:
                        pool.indirect_dma_start(old[s][:, c, :], None, state_t,
                                                bass.IndirectOffsetOnAxis(ap=oi[s][:, c:c + 1], axis=0)
                                                ).then_inc(state_in[s], 16)
                    if second_next(i, s):
                        gather(*second_next(i, s))
                    scatters.wait(S["new_ready"], t)
                    for c in two:
                        pool.indirect_dma_start(state_t, bass.IndirectOffsetOnAxis(ap=oi[s][:, 2 + c:3 + c], axis=0),
                                                new[s][:, c, :], None).then_inc(state_out, 16)
            gather(0, 0)
            gather(0, 1)
            loop(pool, EPAIRS, step)
            pool.wait_ge(state_out, 32 * GROUPS)

        @block.tensor
        def _(pe):
            def front(i, s):
                t = 2 * i + s
                pe.wait_ge(S["keyb_ready"], t + 1)
                wait(pe, S["eq_ready"], t)
                for c in two:
                    last = nc.tensor.matmul(p_keys[:, c * P:(c + 1) * P], keyb[s][:, c, :], ident[:, :],
                                            start=True, stop=True)
                last.then_inc(S["rows_ready"], 1)
                pe.wait_ge(arrived[s], 64 * (i + 1))
                wait(pe, S["endsT_ready"], t)
                for c in range(4):
                    last = nc.tensor.transpose(p_endsT[:, c * P:(c + 1) * P], ends[s][:, c, :], ident[:, :])
                last.then_inc(S["turned"], 1)
                pe.wait_ge(S["endsT_ready"], t + 1)
                wait(pe, S["ft_ready"], t)
                for c in range(4):
                    last = nc.tensor.matmul(p_ft[:, c * D:(c + 1) * D], endsT[s][:, c * P:(c + 1) * P], WT[:, :],
                                            start=True, stop=True)
                last.then_inc(S["ft_psum"], 1)

            def middle(i, s):
                t = 2 * i + s
                pe.wait_ge(S["logit_ready"], t + 1)
                wait(pe, S["peak_ready"], t)
                for h in range(HEADS):
                    for c in two:
                        last = nc.tensor.matmul(p_logit[:, h, c * P:(c + 1) * P],
                                                logit[s][:, c, h:h + 1].to_broadcast([P, P]), ident[:, :],
                                                start=True, stop=True)
                last.then_inc(S["logit_rows"], 1)

            def back(i, s):
                t = 2 * i + s
                pe.wait_ge(S["terms_ready"], t + 1)
                wait(pe, S["new_ready"], t - 1)
                for c in two:
                    for k in two:
                        last = nc.tensor.matmul(p_sums[s][:, c * SUMS:(c + 1) * SUMS],
                                                eq[s][:, k, c * P:(c + 1) * P],
                                                terms[s][:, k, :, :].rearrange("p h f -> p (h f)"),
                                                start=(k == 0), stop=(k == 1))
                last.then_inc(S["summed"], 1)

            def step(i):
                for s in two:
                    back(i, s)
                    if ahead(EPAIRS, i, s):
                        middle(*ahead(EPAIRS, i, s))
                    if second_next(i, s):
                        front(*second_next(i, s))
            front(0, 0)
            middle(0, 0)
            front(0, 1)
            loop(pe, EPAIRS, step)

        @block.scalar
        def _(act):
            def turned(i, s):
                t = 2 * i + s
                act.wait_ge(S["turned"], t + 1)
                wait(act, S["ft_psum"], t - 1)
                nc.scalar.copy(endsT[s][:, :], p_endsT[:, :]).then_inc(S["endsT_ready"], 1)

            def projected(i, s):
                t = 2 * i + s
                act.wait_ge(S["ft_psum"], t + 1)
                wait(act, S["terms_ready"], t - 1)
                nc.scalar.copy(flat(ft[s]), p_ft[:, :]).then_inc(S["ft_ready"], 1)

            def weigh(i, s):
                t = 2 * i + s
                act.wait_ge(S["gap_ready"], t + 1)
                wait(act, S["summed"], t - 1)
                nc.scalar.activation(terms[s][:, :, :, HD], gap[s][:, :, :], ACT.Exp).then_inc(S["weight_ready"], 1)

            def step(i):
                for s in two:
                    t = 2 * i + s
                    weigh(i, s)
                    if ahead(EPAIRS, i, s):
                        projected(*ahead(EPAIRS, i, s))
                    act.wait_ge(S["drop_ready"], t + 1)
                    wait(act, S["new_ready"], t - 1)
                    nc.scalar.activation(keep[s][:, :, :, :], drop[s][:, :, :, :], ACT.Exp
                                         ).then_inc(S["keep_ready"], 1)
                    if second_next(i, s):
                        turned(*second_next(i, s))
            turned(0, 0)
            projected(0, 0)
            turned(0, 1)
            loop(act, EPAIRS, step)

        @block.vector
        def _(dve):
            ch = Chain(dve, S["dve_step"])
            peaks = Turns(dve, sc.tag + "_peaks")

            def indices(i, s):
                t = 2 * i + s
                wait(dve, arrived[s], 64 * i)
                nc.vector.tensor_scalar(gi[s][:, :].rearrange("p (k c) -> p k c", c=2),
                                      index[:, bass.ds(t, 1), 1:3, :].rearrange("p a k c -> p (a k) c"),
                                      1.0, None, ALU.mult
                                      ).then_inc(S["gi_ready"], 1)

            def spread(i, s):
                t = 2 * i + s
                wait(dve, S["eq_ready"], t - 1)
                nc.vector.tensor_copy(keyb[s][:, :, :],
                                      keys[:, bass.ds(2 * t, 2)].unsqueeze(2).to_broadcast([P, 2, P])
                                      ).then_inc(S["keyb_ready"], 1)

            def state_indices(i, s):
                t = 2 * i + s
                wait(dve, state_out, 32 * (t - 1))
                nc.vector.tensor_scalar(oi[s][:, :].rearrange("p (k c) -> p k c", c=2),
                                      index[:, bass.ds(t, 1), 1:4:2, :].rearrange("p a k c -> p (a k) c"),
                                      1.0, None, ALU.mult
                                      ).then_inc(S["oi_ready"], 1)

            def front(i, s):
                t = 2 * i + s
                dve.wait_ge(S["rows_ready"], t + 1)
                wait(dve, S["summed"], t - 1)
                for c in two:
                    last = nc.vector.tensor_scalar(eq[s][:, c, :], p_keys[:, 0:GROUP], keyb[s][:, c, 0:1], None,
                                                   ALU.is_equal)
                last.then_inc(S["eq_ready"], 1)
                dve.wait_ge(S["ft_ready"], t + 1)
                ch.mark(nc.vector.scalar_tensor_tensor(out=prod[:, :, :], in0=ft[s][:, 0:2, :], scalar=SCALE,
                                                       in1=ft[s][:, 2:4, :], op0=ALU.mult, op1=ALU.mult))
                ch.sync()
                nc.vector.tensor_reduce(logit[s][:, :, :], heads(prod[:, :, :]), AXX, ALU.add
                                        ).then_inc(S["logit_ready"], 1)

            def middle(i, s):
                t = 2 * i + s
                dve.wait_ge(S["eq_ready"], t + 1)
                ch.mark(nc.vector.tensor_scalar(below[:, :, :], eq[s][:, :, :], 1.0, -LOWEST, ALU.subtract, ALU.mult))
                ch.sync()
                dve.wait_ge(S["logit_ready"], t + 1)
                peaks.wait(S["logit_rows"], t)
                for c in two:
                    for h in range(HEADS):
                        last = nc.vector.tensor_tensor_reduce(
                            out=shifted[:, c, h, :], in0=p_logit[:, h, :], in1=below[:, c, :], scale=1.0,
                            scalar=LOWEST, op0=ALU.add, op1=ALU.max, accum_out=peak[s][:, c, h:h + 1])
                last.then_inc(S["peak_ready"], 1)
                dve.wait_ge(S["peak_ready"], t + 1)
                wait(dve, S["weight_ready"], t - 1)
                nc.vector.tensor_tensor(gap[s][:, :, :], logit[s][:, :, :], peak[s][:, :, :], ALU.subtract
                                        ).then_inc(S["gap_ready"], 1)
                dve.wait_ge(S["weight_ready"], t + 1)
                nc.vector.tensor_tensor(terms[s][:, :, :, 0:HD], heads(ft[s][:, 2:4, :]),
                                        terms[s][:, :, :, HD].unsqueeze(3).to_broadcast([P, 2, HEADS, HD]),
                                        ALU.mult).then_inc(S["terms_ready"], 1)

            def join(i, s):
                t = 2 * i + s
                dve.wait_ge(state_in[s], 32 * (i + 1))
                new_max = new[s][:, :, SUMS:STATE]
                ch.mark(nc.vector.tensor_tensor(new_max, old[s][:, :, SUMS:STATE], peak[s][:, :, :], ALU.max))
                ch.sync()
                ch.mark(nc.vector.tensor_tensor(drop[s][:, 0, :, :], old[s][:, :, SUMS:STATE], new_max, ALU.subtract))
                nc.vector.tensor_tensor(drop[s][:, 1, :, :], peak[s][:, :, :], new_max, ALU.subtract
                                        ).then_inc(S["drop_ready"], 1)
                dve.wait_ge(S["keep_ready"], t + 1)
                dve.wait_ge(S["summed"], t + 1)
                p_s = p_sums[s][:, 0:2 * SUMS].rearrange("p (c f) -> p c f", c=2)

                def kept(k):
                    return keep[s][:, k, :, :]
                ch.mark(nc.vector.tensor_tensor(heads(new[s][:, :, 0:SUMS]), heads(old[s][:, :, 0:SUMS]),
                                                kept(0).unsqueeze(3).to_broadcast([P, 2, HEADS, HS]), ALU.mult))
                ch.mark(nc.vector.tensor_tensor(heads(part[:, :, :]), heads(p_s), kept(1).unsqueeze(3).to_broadcast(
                    [P, 2, HEADS, HS]), ALU.mult))
                ch.sync()
                nc.vector.tensor_tensor(new[s][:, :, 0:SUMS], new[s][:, :, 0:SUMS], part[:, :, :], ALU.add
                                        ).then_inc(S["new_ready"], 1)
                dve.wait_ge(S["new_ready"], t + 1)

            def step(i):
                for s in two:
                    if second_next(i, s):
                        indices(*second_next(i, s))
                    if ahead(EPAIRS, i, s):
                        front(*ahead(EPAIRS, i, s))
                        state_indices(*ahead(EPAIRS, i, s))
                    join(i, s)
                    if second_next(i, s):
                        spread(*second_next(i, s))
                    if ahead(EPAIRS, i, s):
                        middle(*ahead(EPAIRS, i, s))
            indices(0, 0)
            indices(0, 1)
            spread(0, 0)
            spread(0, 1)
            state_indices(0, 0)
            front(0, 0)
            middle(0, 0)
            loop(dve, EPAIRS, step, ch, 12)


def last_layer_out(nc, g):
    CHUNKS, LAST = g["CHUNKS"], g["LAST"]
    with Scope(nc, "out4") as sc:
        two = range(2)
        xb = [sc.sb(f"xb{l}", [P, J, D]) for l in range(LOADS)]
        sb_ = [sc.sb(f"state{l}", [P, J, STATE]) for l in range(LOADS)]
        mean_ft = [sc.sb(f"mean_ft{s}", [P, J, D]) for s in two]
        den = sc.sb("den", [P, J, HEADS])
        inv = [sc.sb(f"inv{s}", [P, J, HEADS]) for s in two]
        nn = NodeNorm(nc, sc, g)
        x_in = [sc.sem(f"x_in{l}") for l in range(LOADS)]
        s_in = [sc.sem(f"s_in{l}") for l in range(LOADS)]
        inv_ready, mean_ready = sc.sem("inv_ready"), sc.sem("mean_ready")
        block = sc.block()
        xv, sv = g["chunked"](g["x3_t"]), g["chunked"](g["state_t"])

        @block.sync
        def _(sp):
            def load(i, k):
                m, l = STEP * i + k, k % LOADS
                wait(sp, mean_ready, m - LOADS + 1)
                sp.dma_start(flat(sb_[l]), g["at"](sv, m)).then_inc(s_in[l], 16)
                wait(sp, nn.u_ready, m - LOADS + 1)
                sp.dma_start(flat(xb[l]), g["at"](xv, m)).then_inc(x_in[l], 16)
            nn.load_and_store(sp, CHUNKS, load, lambda m: g["node_rows"](g["out"], m, g["rows_of"](m)))

        @block.gpsimd
        def _(pool):
            def step(i, k):
                m, s, l = STEP * i + k, k % 2, k % LOADS
                pool.wait_ge(inv_ready, m + 1)
                wait(pool, nn.u_ready, m - 1)
                nc.gpsimd.tensor_tensor(
                    mean_ft[s][:, :, :].rearrange("p j (h f) -> p j h f", h=HEADS),
                    sb_[l][:, :, 0:SUMS].rearrange("p j (h f) -> p j h f", h=HEADS)[:, :, :, 0:HD],
                    inv[s][:, :, :].unsqueeze(3).to_broadcast([P, J, HEADS, HD]), ALU.mult
                    ).then_inc(mean_ready, 1)
            loop_chunks(pool, CHUNKS, step)

        @block.scalar
        def _(act):
            def step(i, k):
                b = chunk_before(i, k)
                if b:
                    nn.apply_act(act, *b)
                nn.root(act, i, k)
            loop_chunks(act, CHUNKS, step)
            nn.apply_act(act, *LAST)

        @block.vector
        def _(dve):
            ch = Chain(dve, nn.step)

            def denominators(i, k):
                m, l = STEP * i + k, k % LOADS
                dve.wait_ge(s_in[l], 16 * (slot_turn(i, k) + 1))
                wait(dve, inv_ready, m)
                d = sb_[l][:, :, 0:SUMS].rearrange("p j (h f) -> p j h f", h=HEADS)[:, :, :, HD]
                return ch.mark(nc.vector.scalar_tensor_tensor(out=den[:, :, :], in0=d, scalar=0.0, in1=d,
                                                              op0=ALU.is_equal, op1=ALU.add))

            def invert(i, k, den_ready):
                m, s = STEP * i + k, k % 2
                ch.after(den_ready)
                wait(dve, mean_ready, m - 1)
                nc.vector.reciprocal(inv[s][:, :, :], den[:, :, :]).then_inc(inv_ready, 1)

            def add(i, k):
                m, s, l = STEP * i + k, k % 2, k % LOADS
                dve.wait_ge(mean_ready, m + 1)
                dve.wait_ge(x_in[l], 16 * (slot_turn(i, k) + 1))
                nn.free_u(dve, m)
                nc.vector.scalar_tensor_tensor(out=flat(nn.u[k % LOADS]), in0=flat(xb[l]), scalar=2.0,
                                               in1=flat(mean_ft[s]), op0=ALU.mult, op1=ALU.add).then_inc(nn.u_ready, 1)

            def step(i, k):
                after_next = later(CHUNKS, i, k, 2)
                if after_next:
                    den_ready = denominators(*after_next)
                nn.round(dve, ch, (i, k), chunk_before(i, k), add_u=lambda: add(i, k))
                if after_next:
                    invert(*after_next, den_ready)
            invert(0, 0, denominators(0, 0))
            invert(0, 1, denominators(0, 1))
            loop_chunks(dve, CHUNKS, step, ch, 8)
            nn.round(dve, ch, None, LAST)


_INS = ['x', 'src', 'dst', 'edge_attr_64', 'L0_gnn_We', 'L0_gnn_be', 'L0_gnn_W1', 'L0_gnn_b1', 'L0_gnn_g1',
        'L0_gnn_beta1', 'L0_gnn_W2', 'L0_gnn_b2', 'L0_gnn_g2', 'L0_gnn_beta2', 'L0_gnn_eps', 'L1_gnn_W',
        'L2_gnn_W', 'L2_gnn_b', 'L3_gnn_W']


def kernel(**inputs):
    import numpy as _np
    import concourse.bacc as _bacc
    from concourse import mybir as _mybir
    from concourse.bass_utils import run_bass_kernel_spmd as _run

    nc = _bacc.Bacc("TRN2", target_bir_lowering=False, num_devices=1)
    arrays, args = {}, []
    for name in _INS:
        a = _np.ascontiguousarray(inputs[name])
        if name == 'L0_gnn_eps':
            a = a.reshape(1)
        arrays[f"in_{name}_dram"] = a
        args.append(nc.dram_tensor(f"in_{name}_dram", a.shape, _mybir.dt.from_np(a.dtype), kind="ExternalInput").ap())
    args.append(nc.dram_tensor("out_0_dram", tuple(inputs['x'].shape), _mybir.dt.float32, kind="ExternalOutput").ap())
    gnn_kernel(nc, *args)
    r = _run(nc, [arrays], core_ids=[0])
    return r.results[0]["out_0_dram"]
```
